# Optimizing a Trainium2 kernel written in Bass

```python
import numpy as np
import jax
import jax.numpy as jnp

def _softmax(x, axis=-1):
    return jax.nn.softmax(x, axis=axis)

def _gelu(x):
    return jax.nn.gelu(x, approximate=True)

def _silu(x):
    return jax.nn.silu(x)

def _sigmoid(x):
    return jax.nn.sigmoid(x)

def _layernorm(x, axis=-1, eps=1e-05):
    m = jnp.mean(x, axis=axis, keepdims=True)
    v = jnp.var(x, axis=axis, keepdims=True)
    return (x - m) / jnp.sqrt(v + eps)

def _scatter_add(tgt, idx, src, axis=0):
    return tgt.at[idx].add(src)

def _segment_sum(src, seg, n):
    return jax.ops.segment_sum(src, seg, n)
kernel_name = 'mk_decoder_postln_d2_seqx_r8_b451b5'

def setup_inputs(seed: int=0):
    np.random.seed(seed)
    _w = jnp.asarray

    def _rec_inputs():
        import jax
        import jax.numpy as jnp
        _rk = jax.random.key(seed)
        x = -0.0003929 + 0.9999 * jax.random.normal(jax.random.fold_in(_rk, 1), (16, 128, 256), jnp.float32)
        _lenS = 128 - jax.random.randint(jax.random.fold_in(_rk, 7), (16,), 0, max(1, 128 // 4) + 1, jnp.int32)
        _lenS2 = 128 - jax.random.randint(jax.random.fold_in(_rk, 8), (16,), 0, max(1, 128 // 4) + 1, jnp.int32)
        _ctx_2048P = jax.random.normal(jax.random.fold_in(_rk, 11), (16, 16, 256), jnp.float32)
        _ctx_2048c = jax.random.dirichlet(jax.random.fold_in(_rk, 511), 0.3 * jnp.ones((16,), jnp.float32), (16, 128))
        _ctx_2048t = jnp.einsum('bsk,bkd->bsd', _ctx_2048c, _ctx_2048P)
        _ctx_2048t = _ctx_2048t * jax.lax.rsqrt(jnp.mean(jnp.square(_ctx_2048t)) + 1e-12) * 0.953939
        ctx_2048 = 2.81802e-05 + 1.00001 * (_ctx_2048t + 0.3 * jax.random.normal(jax.random.fold_in(_rk, 611), (16, 128, 256), jnp.float32))
        _validS = jnp.arange(128)[None, :] < _lenS[:, None]
        _validS2 = jnp.arange(128)[None, :] < _lenS2[:, None]
        _causal = jnp.tril(jnp.ones((128, 128), dtype=bool))
        mask_BxS2_ff1 = jnp.where(jnp.ones((16, 128), dtype=bool), 1.0, 0.0).astype(jnp.float32)
        return (x, ctx_2048, mask_BxS2_ff1)
    x, ctx_2048, mask_BxS2_ff1 = _rec_inputs()

    def _L0_attn_setup():
        import jax, jax.numpy as jnp
        import numpy as np
        import math
        D_MODEL = 256
        NUM_HEADS = 16
        HEAD_DIM = D_MODEL // NUM_HEADS
        key = jax.random.key(seed)
        k_x, k_wqkv, k_bqkv, k_wo, k_bo = jax.random.split(key, 5)
        B, S = (2, 256)
        scale = 1.0 / math.sqrt(D_MODEL)
        return {'x': jax.random.normal(k_x, (B, S, D_MODEL), dtype=jnp.float32), 'w_qkv': jax.random.normal(k_wqkv, (3 * D_MODEL, D_MODEL), dtype=jnp.float32) * scale, 'b_qkv': jax.random.normal(k_bqkv, (3 * D_MODEL,), dtype=jnp.float32) * 0.01, 'w_out': jax.random.normal(k_wo, (D_MODEL, D_MODEL), dtype=jnp.float32) * scale, 'b_out': jax.random.normal(k_bo, (D_MODEL,), dtype=jnp.float32) * 0.01}
    _L0_attn_all = _L0_attn_setup()
    _L0_attn_in = {k: v for k, v in _L0_attn_all.items() if k in ('w_qkv', 'b_qkv', 'w_out', 'b_out')}
    del _L0_attn_all

    def _L0_xattn_setup():
        import jax, jax.numpy as jnp
        import numpy as np
        HIDDEN = 256
        NUM_HEADS = 16
        HEAD_DIM = HIDDEN // NUM_HEADS
        CHUNK = 128
        SCALE = HEAD_DIM ** (-0.5)

        def _chunked_causal_attention(q, k, v):
            B, H, S, D = q.shape
            n_chunks = S // CHUNK
            kc = k.reshape(B, H, n_chunks, CHUNK, D).transpose(2, 0, 1, 3, 4)
            vc = v.reshape(B, H, n_chunks, CHUNK, D).transpose(2, 0, 1, 3, 4)
            j0s = jnp.arange(n_chunks) * CHUNK
            q_idx = jnp.arange(S)[:, None]
            k_off = jnp.arange(CHUNK)[None, :]
            out0 = jnp.zeros_like(q)
            m0 = jnp.full((B, H, S, 1), -jnp.inf, dtype=q.dtype)
            s0 = jnp.zeros((B, H, S, 1), dtype=q.dtype)

            def step(carry, inputs):
                out, m, s = carry
                kj, vj, j0 = inputs
                scores = jnp.einsum('bhqd,bhkd->bhqk', q, kj) * SCALE
                causal = j0 + k_off > q_idx
                scores = jnp.where(causal[None, None], -jnp.inf, scores)
                chunk_max = scores.max(axis=-1, keepdims=True)
                new_m = jnp.maximum(m, chunk_max)
                exp_old = jnp.exp(m - new_m)
                exp_c = jnp.exp(scores - new_m)
                new_s = s * exp_old + exp_c.sum(axis=-1, keepdims=True)
                out = out * (s / new_s) * exp_old + jnp.einsum('bhqk,bhkd->bhqd', exp_c / new_s, vj)
                return ((out, new_m, new_s), None)
            (out, _, _), _ = jax.lax.scan(step, (out0, m0, s0), (kc, vc, j0s))
            return out
        key = jax.random.key(seed)
        kq, kk, kv = jax.random.split(key, 3)
        B, S = (2, 512)
        return {'query': jax.random.normal(kq, (B, S, HIDDEN), dtype=jnp.float32), 'key': jax.random.normal(kk, (B, S, HIDDEN), dtype=jnp.float32), 'value': jax.random.normal(kv, (B, S, HIDDEN), dtype=jnp.float32)}
    _L0_xattn_all = _L0_xattn_setup()
    _L0_xattn_in = {k: v for k, v in _L0_xattn_all.items() if k in ()}
    del _L0_xattn_all

    def _L0_ffn_setup():
        import jax, jax.numpy as jnp
        import numpy as np
        MIN_EXPERTS = 2
        NEG_INF = -1000000000.0

        def _l2norm(x, axis):
            return x / jnp.maximum(jnp.linalg.norm(x, axis=axis, keepdims=True), 1e-12)

        def _ste(x):
            return x + jax.lax.stop_gradient((x > 0).astype(x.dtype) - x)

        def _forward(hidden_states, sim_matrix, gates, q_proj, k_proj, v_proj, o_proj):
            B, T, C = hidden_states.shape
            E = gates.shape[0]
            H = q_proj.shape[-1]
            x = hidden_states.reshape(B * T, C)
            logits = _l2norm(x, -1) @ _l2norm(sim_matrix, 0) - jax.nn.sigmoid(gates)
            gated = jax.nn.relu(logits)
            mask = _ste(gated)
            inactive = jnp.sum(mask, axis=1) == 0
            fb_idx = jax.lax.top_k(logits, MIN_EXPERTS)[1]
            fb_mask = jnp.max(jax.nn.one_hot(fb_idx, E, dtype=mask.dtype), axis=1)
            mask = jnp.where(inactive[:, None] & (fb_mask > 0), jnp.ones_like(mask), mask)
            masked_logits = jnp.where(mask > 0, gated, jnp.full_like(gated, NEG_INF))
            probs = jax.nn.softmax(masked_logits, axis=-1)
            w = probs * (mask > 0)

            def mix(proj):
                pe = jnp.einsum('nc,ech->neh', x, proj)
                return jnp.einsum('ne,neh->nh', w, pe).reshape(B, T, H)
            q, k, v = (mix(q_proj), mix(k_proj), mix(v_proj))
            scale = 1.0 / jnp.sqrt(jnp.asarray(H, dtype=q.dtype))
            scores = jnp.einsum('bqh,bkh->bqk', q, k) * scale
            causal = jnp.tril(jnp.ones((T, T), dtype=bool))
            scores = jnp.where(causal[None], scores, jnp.full_like(scores, NEG_INF))
            attn = jax.nn.softmax(scores, axis=-1)
            ao = jnp.einsum('bqk,bkh->bqh', attn, v).reshape(B * T, H)
            wa = jnp.einsum('ne,nh->enh', w, ao)
            out = jnp.einsum('enh,ehc->nc', wa, o_proj)
            return out.reshape(B, T, C)
        key = jax.random.key(seed)
        ks = jax.random.split(key, 6)
        B, T, C, H, E = (4, 256, 256, 128, 16)
        xavier_qkv = float(np.sqrt(2.0 / (C + H)))
        return {'hidden_states': jax.random.normal(ks[0], (B, T, C), dtype=jnp.float32), 'sim_matrix': jax.random.normal(ks[1], (C, E), dtype=jnp.float32), 'gates': jnp.full((E,), -6.0, dtype=jnp.float32), 'q_proj': jax.random.normal(ks[2], (E, C, H), dtype=jnp.float32) * xavier_qkv, 'k_proj': jax.random.normal(ks[3], (E, C, H), dtype=jnp.float32) * xavier_qkv, 'v_proj': jax.random.normal(ks[4], (E, C, H), dtype=jnp.float32) * xavier_qkv, 'o_proj': jax.random.normal(ks[5], (E, H, C), dtype=jnp.float32) * xavier_qkv}
    _L0_ffn_all = _L0_ffn_setup()
    _L0_ffn_in = {k: v for k, v in _L0_ffn_all.items() if k in ('sim_matrix', 'gates', 'q_proj', 'k_proj', 'v_proj', 'o_proj')}
    del _L0_ffn_all

    def _L1_attn_setup():
        import jax, jax.numpy as jnp
        import numpy as np
        B, T, E = (4, 256, 256)
        H, KV = (16, 4)
        G = H // KV
        D = E // H
        key = jax.random.key(seed)
        kx, kq, kk, kv, ko = jax.random.split(key, 5)
        s = 1.0 / np.sqrt(E).astype(np.float32)
        x = jax.random.normal(kx, (B, T, E), jnp.float32)
        Wq = jax.random.normal(kq, (E, H * D), jnp.float32) * s
        Wk = jax.random.normal(kk, (E, KV * D), jnp.float32) * s
        Wv = jax.random.normal(kv, (E, KV * D), jnp.float32) * s
        Wo = jax.random.normal(ko, (H * D, E), jnp.float32) * s
        return {'x': x, 'Wq': Wq, 'Wk': Wk, 'Wv': Wv, 'Wo': Wo}
    _L1_attn_all = _L1_attn_setup()
    _L1_attn_in = {k: v for k, v in _L1_attn_all.items() if k in ('Wq', 'Wk', 'Wv', 'Wo')}
    del _L1_attn_all

    def _L1_xattn_setup():
        import jax, jax.numpy as jnp
        import numpy as np
        H = 256
        NH = 16
        HD = H // NH
        FD = 64
        key = jax.random.key(seed)
        ks = jax.random.split(key, 12)
        B, S = (4, 512)
        s = 1.0 / np.sqrt(H)
        sf = 1.0 / np.sqrt(HD)
        return {'query': jax.random.normal(ks[0], (B, S, H), jnp.float32), 'key': jax.random.normal(ks[1], (B, S, H), jnp.float32), 'value': jax.random.normal(ks[2], (B, S, H), jnp.float32), 'attention_mask': jnp.ones((B, S), jnp.float32), 'Wq': jax.random.normal(ks[3], (H, H), jnp.float32) * s, 'bq': jnp.zeros((H,), jnp.float32), 'Wk': jax.random.normal(ks[4], (H, H), jnp.float32) * s, 'bk': jnp.zeros((H,), jnp.float32), 'Wv': jax.random.normal(ks[5], (H, H), jnp.float32) * s, 'bv': jnp.zeros((H,), jnp.float32), 'Wqf': jax.random.normal(ks[6], (FD, HD), jnp.float32) * sf, 'Wkf': jax.random.normal(ks[7], (FD, HD), jnp.float32) * sf, 'Wo': jax.random.normal(ks[8], (H, H), jnp.float32) * s, 'bo': jnp.zeros((H,), jnp.float32)}
    _L1_xattn_all = _L1_xattn_setup()
    _L1_xattn_in = {k: v for k, v in _L1_xattn_all.items() if k in ('Wq', 'bq', 'Wk', 'bk', 'Wv', 'bv', 'Wqf', 'Wkf', 'Wo', 'bo')}
    del _L1_xattn_all

    def _L1_ffn_setup():
        import jax, jax.numpy as jnp
        import numpy as np
        B, S, D = (4, 256, 256)
        DFF = 704
        E, K, R = (8, 2, 16)
        SCALING = 32.0 / 16.0
        key = jax.random.key(seed)
        ks = jax.random.split(key, 12)
        s = lambda k, shape, scale: jax.random.normal(k, shape, dtype=jnp.float32) * scale
        return {'x': s(ks[0], (B, S, D), 1.0), 'Wg': s(ks[1], (DFF, D), 0.02), 'Wu': s(ks[2], (DFF, D), 0.02), 'Wd': s(ks[3], (D, DFF), 0.02), 'Wr': s(ks[4], (E, D), 0.02), 'Ag': s(ks[5], (E, R, D), 0.02), 'Bg': s(ks[6], (E, DFF, R), 0.02), 'Au': s(ks[7], (E, R, D), 0.02), 'Bu': s(ks[8], (E, DFF, R), 0.02), 'Ad': s(ks[9], (E, R, DFF), 0.02), 'Bd': s(ks[10], (E, D, R), 0.02)}
    _L1_ffn_all = _L1_ffn_setup()
    _L1_ffn_in = {k: v for k, v in _L1_ffn_all.items() if k in ('Wg', 'Wu', 'Wd', 'Wr', 'Ag', 'Bg', 'Au', 'Bu', 'Ad', 'Bd')}
    del _L1_ffn_all
    return {'x': x, 'ctx_2048': ctx_2048, 'mask_BxS2_ff1': mask_BxS2_ff1, 'L0_attn_w_qkv': _L0_attn_in['w_qkv'], 'L0_attn_b_qkv': _L0_attn_in['b_qkv'], 'L0_attn_w_out': _L0_attn_in['w_out'], 'L0_attn_b_out': _L0_attn_in['b_out'], 'L0_ffn_sim_matrix': _L0_ffn_in['sim_matrix'], 'L0_ffn_gates': _L0_ffn_in['gates'], 'L0_ffn_q_proj': _L0_ffn_in['q_proj'], 'L0_ffn_k_proj': _L0_ffn_in['k_proj'], 'L0_ffn_v_proj': _L0_ffn_in['v_proj'], 'L0_ffn_o_proj': _L0_ffn_in['o_proj'], 'L1_attn_Wq': _L1_attn_in['Wq'], 'L1_attn_Wk': _L1_attn_in['Wk'], 'L1_attn_Wv': _L1_attn_in['Wv'], 'L1_attn_Wo': _L1_attn_in['Wo'], 'L1_xattn_Wq': _L1_xattn_in['Wq'], 'L1_xattn_bq': _L1_xattn_in['bq'], 'L1_xattn_Wk': _L1_xattn_in['Wk'], 'L1_xattn_bk': _L1_xattn_in['bk'], 'L1_xattn_Wv': _L1_xattn_in['Wv'], 'L1_xattn_bv': _L1_xattn_in['bv'], 'L1_xattn_Wqf': _L1_xattn_in['Wqf'], 'L1_xattn_Wkf': _L1_xattn_in['Wkf'], 'L1_xattn_Wo': _L1_xattn_in['Wo'], 'L1_xattn_bo': _L1_xattn_in['bo'], 'L1_ffn_Wg': _L1_ffn_in['Wg'], 'L1_ffn_Wu': _L1_ffn_in['Wu'], 'L1_ffn_Wd': _L1_ffn_in['Wd'], 'L1_ffn_Wr': _L1_ffn_in['Wr'], 'L1_ffn_Ag': _L1_ffn_in['Ag'], 'L1_ffn_Bg': _L1_ffn_in['Bg'], 'L1_ffn_Au': _L1_ffn_in['Au'], 'L1_ffn_Bu': _L1_ffn_in['Bu'], 'L1_ffn_Ad': _L1_ffn_in['Ad'], 'L1_ffn_Bd': _L1_ffn_in['Bd']}

def reference(x, ctx_2048, mask_BxS2_ff1, L0_attn_w_qkv, L0_attn_b_qkv, L0_attn_w_out, L0_attn_b_out, L0_ffn_sim_matrix, L0_ffn_gates, L0_ffn_q_proj, L0_ffn_k_proj, L0_ffn_v_proj, L0_ffn_o_proj, L1_attn_Wq, L1_attn_Wk, L1_attn_Wv, L1_attn_Wo, L1_xattn_Wq, L1_xattn_bq, L1_xattn_Wk, L1_xattn_bk, L1_xattn_Wv, L1_xattn_bv, L1_xattn_Wqf, L1_xattn_Wkf, L1_xattn_Wo, L1_xattn_bo, L1_ffn_Wg, L1_ffn_Wu, L1_ffn_Wd, L1_ffn_Wr, L1_ffn_Ag, L1_ffn_Bg, L1_ffn_Au, L1_ffn_Bu, L1_ffn_Ad, L1_ffn_Bd):
    import jax
    import jax.numpy as jnp

    def _L0_attn_ref(x, w_qkv, b_qkv, w_out, b_out):
        import jax, jax.numpy as jnp
        import numpy as np
        import math
        D_MODEL = 256
        NUM_HEADS = 16
        HEAD_DIM = D_MODEL // NUM_HEADS
        B, S, D = x.shape
        H, Hd = (NUM_HEADS, HEAD_DIM)
        qkv = jnp.einsum('bsd,ed->bse', x, w_qkv) + b_qkv
        qkv = qkv.reshape(B, S, 3, H, Hd)
        q = jnp.transpose(qkv[:, :, 0], (0, 2, 1, 3))
        k = jnp.transpose(qkv[:, :, 1], (0, 2, 1, 3))
        v = jnp.transpose(qkv[:, :, 2], (0, 2, 1, 3))
        scores = jnp.einsum('bhqd,bhkd->bhqk', q, k) / math.sqrt(Hd)
        causal = jnp.triu(jnp.full((S, S), -jnp.inf, dtype=scores.dtype), k=1)
        scores = scores + causal[None, None]
        attn = jax.nn.softmax(scores, axis=-1)
        out = jnp.einsum('bhqk,bhkd->bhqd', attn, v)
        out = jnp.transpose(out, (0, 2, 1, 3)).reshape(B, S, D)
        return jnp.einsum('bsd,ed->bse', out, w_out) + b_out

    def _L0_xattn_ref(query, key, value):
        import jax, jax.numpy as jnp
        import numpy as np
        HIDDEN = 256
        NUM_HEADS = 16
        HEAD_DIM = HIDDEN // NUM_HEADS
        CHUNK = 128
        SCALE = HEAD_DIM ** (-0.5)

        def _chunked_causal_attention(q, k, v):
            B, H, S, D = q.shape
            n_chunks = S // CHUNK
            kc = k.reshape(B, H, n_chunks, CHUNK, D).transpose(2, 0, 1, 3, 4)
            vc = v.reshape(B, H, n_chunks, CHUNK, D).transpose(2, 0, 1, 3, 4)
            j0s = jnp.arange(n_chunks) * CHUNK
            q_idx = jnp.arange(S)[:, None]
            k_off = jnp.arange(CHUNK)[None, :]
            out0 = jnp.zeros_like(q)
            m0 = jnp.full((B, H, S, 1), -jnp.inf, dtype=q.dtype)
            s0 = jnp.zeros((B, H, S, 1), dtype=q.dtype)

            def step(carry, inputs):
                out, m, s = carry
                kj, vj, j0 = inputs
                scores = jnp.einsum('bhqd,bhkd->bhqk', q, kj) * SCALE
                causal = j0 + k_off > q_idx
                scores = jnp.where(causal[None, None], -jnp.inf, scores)
                chunk_max = scores.max(axis=-1, keepdims=True)
                new_m = jnp.maximum(m, chunk_max)
                exp_old = jnp.exp(m - new_m)
                exp_c = jnp.exp(scores - new_m)
                new_s = s * exp_old + exp_c.sum(axis=-1, keepdims=True)
                out = out * (s / new_s) * exp_old + jnp.einsum('bhqk,bhkd->bhqd', exp_c / new_s, vj)
                return ((out, new_m, new_s), None)
            (out, _, _), _ = jax.lax.scan(step, (out0, m0, s0), (kc, vc, j0s))
            return out
        B, S, _ = query.shape
        q = query.reshape(B, S, NUM_HEADS, HEAD_DIM).transpose(0, 2, 1, 3)
        k = key.reshape(B, S, NUM_HEADS, HEAD_DIM).transpose(0, 2, 1, 3)
        v = value.reshape(B, S, NUM_HEADS, HEAD_DIM).transpose(0, 2, 1, 3)
        out = _chunked_causal_attention(q, k, v)
        return out.transpose(0, 2, 1, 3).reshape(B, S, HIDDEN)

    def _L0_ffn_ref(hidden_states, sim_matrix, gates, q_proj, k_proj, v_proj, o_proj):
        import jax, jax.numpy as jnp
        import numpy as np
        MIN_EXPERTS = 2
        NEG_INF = -1000000000.0

        def _l2norm(x, axis):
            return x / jnp.maximum(jnp.linalg.norm(x, axis=axis, keepdims=True), 1e-12)

        def _ste(x):
            return x + jax.lax.stop_gradient((x > 0).astype(x.dtype) - x)

        def _forward(hidden_states, sim_matrix, gates, q_proj, k_proj, v_proj, o_proj):
            B, T, C = hidden_states.shape
            E = gates.shape[0]
            H = q_proj.shape[-1]
            x = hidden_states.reshape(B * T, C)
            logits = _l2norm(x, -1) @ _l2norm(sim_matrix, 0) - jax.nn.sigmoid(gates)
            gated = jax.nn.relu(logits)
            mask = _ste(gated)
            inactive = jnp.sum(mask, axis=1) == 0
            fb_idx = jax.lax.top_k(logits, MIN_EXPERTS)[1]
            fb_mask = jnp.max(jax.nn.one_hot(fb_idx, E, dtype=mask.dtype), axis=1)
            mask = jnp.where(inactive[:, None] & (fb_mask > 0), jnp.ones_like(mask), mask)
            masked_logits = jnp.where(mask > 0, gated, jnp.full_like(gated, NEG_INF))
            probs = jax.nn.softmax(masked_logits, axis=-1)
            w = probs * (mask > 0)

            def mix(proj):
                pe = jnp.einsum('nc,ech->neh', x, proj)
                return jnp.einsum('ne,neh->nh', w, pe).reshape(B, T, H)
            q, k, v = (mix(q_proj), mix(k_proj), mix(v_proj))
            scale = 1.0 / jnp.sqrt(jnp.asarray(H, dtype=q.dtype))
            scores = jnp.einsum('bqh,bkh->bqk', q, k) * scale
            causal = jnp.tril(jnp.ones((T, T), dtype=bool))
            scores = jnp.where(causal[None], scores, jnp.full_like(scores, NEG_INF))
            attn = jax.nn.softmax(scores, axis=-1)
            ao = jnp.einsum('bqk,bkh->bqh', attn, v).reshape(B * T, H)
            wa = jnp.einsum('ne,nh->enh', w, ao)
            out = jnp.einsum('enh,ehc->nc', wa, o_proj)
            return out.reshape(B, T, C)
        return _forward(hidden_states, sim_matrix, gates, q_proj, k_proj, v_proj, o_proj)

    def _L1_attn_ref(x, Wq, Wk, Wv, Wo):
        import jax, jax.numpy as jnp
        import numpy as np
        B, T, E = (4, 256, 256)
        H, KV = (16, 4)
        G = H // KV
        D = E // H
        b, t, _ = x.shape
        scale = 1.0 / np.sqrt(D).astype(np.float32)
        q = (x @ Wq).reshape(b, t, KV, G, D)
        k = (x @ Wk).reshape(b, t, KV, D)
        v = (x @ Wv).reshape(b, t, KV, D)
        scores = jnp.einsum('bqhgd,bkhd->bhgqk', q, k) * scale
        causal_mask = jnp.tril(jnp.ones((t, t), dtype=bool))
        scores = jnp.where(causal_mask, scores, -jnp.inf)
        w = jax.nn.softmax(scores, axis=-1)
        y = jnp.einsum('bhgqk,bkhd->bqhgd', w, v)
        y = y.reshape(b, t, H * D)
        return y @ Wo

    def _L1_xattn_ref(query, key, value, attention_mask, Wq, bq, Wk, bk, Wv, bv, Wqf, Wkf, Wo, bo):
        import jax, jax.numpy as jnp
        import numpy as np
        H = 256
        NH = 16
        HD = H // NH
        FD = 64
        B, Sq, _ = query.shape
        Sk = key.shape[1]

        def heads(x, W, b, S):
            return (x @ W.T + b).reshape(B, S, NH, HD).transpose(0, 2, 1, 3)
        q = heads(query, Wq, bq, Sq)
        k = heads(key, Wk, bk, Sk)
        v = heads(value, Wv, bv, Sk)
        q_prime = jax.nn.relu(jnp.einsum('bhnd,fd->bhnf', q, Wqf))
        k_prime = jax.nn.relu(jnp.einsum('bhnd,fd->bhnf', k, Wkf))
        k_prime = k_prime * attention_mask[:, None, :, None]
        kv = jnp.einsum('bhnf,bhne->bhfe', k_prime, v)
        qkv = jnp.einsum('bhmf,bhfe->bhme', q_prime, kv)
        k_sum = jnp.sum(k_prime, axis=2)
        qk_sum = jnp.einsum('bhmf,bhf->bhm', q_prime, k_sum)[..., None]
        out = qkv / (qk_sum + 1e-08)
        out = out.transpose(0, 2, 1, 3).reshape(B, Sq, H)
        return out @ Wo.T + bo

    def _L1_ffn_ref(x, Wg, Wu, Wd, Wr, Ag, Bg, Au, Bu, Ad, Bd):
        import jax, jax.numpy as jnp
        import numpy as np
        B, S, D = (4, 256, 256)
        DFF = 704
        E, K, R = (8, 2, 16)
        SCALING = 32.0 / 16.0
        b, s, d = x.shape
        xf = x.reshape(-1, d)
        gate_base = xf @ Wg.T
        up_base = xf @ Wu.T
        base_out = jax.nn.silu(gate_base) * up_base @ Wd.T
        router_logits = xf @ Wr.T
        probs = jax.nn.softmax(router_logits.astype(jnp.float32), axis=-1)
        topw, topi = jax.lax.top_k(probs, K)
        topw = topw.astype(x.dtype)
        expert_w = jnp.sum(jax.nn.one_hot(topi, E, dtype=x.dtype) * topw[..., None], axis=1)

        def expert_step(acc, params):
            Ag_e, Bg_e, Au_e, Bu_e, Ad_e, Bd_e, we = params
            g_lora = xf @ Ag_e.T @ Bg_e.T * SCALING
            u_lora = xf @ Au_e.T @ Bu_e.T * SCALING
            h = jax.nn.silu(gate_base + g_lora) * (up_base + u_lora)
            d_delta = h @ Ad_e.T @ Bd_e.T * SCALING
            return (acc + d_delta * we[:, None], None)
        acc0 = jnp.zeros_like(base_out)
        acc, _ = jax.lax.scan(expert_step, acc0, (Ag, Bg, Au, Bu, Ad, Bd, expert_w.T))
        return (base_out + acc).reshape(b, s, d)
    x = _layernorm(x + _L0_attn_ref(x, L0_attn_w_qkv, L0_attn_b_qkv, L0_attn_w_out, L0_attn_b_out), axis=-1)
    x = _layernorm(x + _L0_xattn_ref(x, ctx_2048, ctx_2048), axis=-1)
    x = _layernorm(x + _L0_ffn_ref(x, L0_ffn_sim_matrix, L0_ffn_gates, L0_ffn_q_proj, L0_ffn_k_proj, L0_ffn_v_proj, L0_ffn_o_proj), axis=-1)
    x = _layernorm(x + _L1_attn_ref(x, L1_attn_Wq, L1_attn_Wk, L1_attn_Wv, L1_attn_Wo), axis=-1)
    x = _layernorm(x + _L1_xattn_ref(x, ctx_2048, ctx_2048, mask_BxS2_ff1, L1_xattn_Wq, L1_xattn_bq, L1_xattn_Wk, L1_xattn_bk, L1_xattn_Wv, L1_xattn_bv, L1_xattn_Wqf, L1_xattn_Wkf, L1_xattn_Wo, L1_xattn_bo), axis=-1)
    x = _layernorm(x + _L1_ffn_ref(x, L1_ffn_Wg, L1_ffn_Wu, L1_ffn_Wd, L1_ffn_Wr, L1_ffn_Ag, L1_ffn_Bg, L1_ffn_Au, L1_ffn_Bu, L1_ffn_Ad, L1_ffn_Bd), axis=-1)
    return x

_drawn_inputs = setup_inputs


def setup_inputs(seed=0):
    import zlib

    import numpy as np

    out = dict(_drawn_inputs(seed))
    spreads = {'L0_ffn_gates': (-6.0, 0.6),
     'L1_xattn_bq': (0.0, 0.8),
     'L1_xattn_bk': (0.0, 0.8),
     'L1_xattn_bv': (0.0, 0.1),
     'L1_xattn_bo': (0.0, 0.1)}
    factors = {'L0_attn_b_qkv': 4.639,
     'L0_attn_b_out': 5.007,
     'L0_ffn_q_proj': 8.0,
     'L0_ffn_k_proj': 8.0,
     'L1_ffn_Wr': 8.0,
     'L1_ffn_Ag': 8.0,
     'L1_ffn_Bg': 8.0,
     'L1_ffn_Au': 8.0,
     'L1_ffn_Bu': 8.0,
     'L1_ffn_Ad': 8.0,
     'L1_ffn_Bd': 8.0,
     'L1_ffn_Wd': 42.769}
    for name, (base, spread) in spreads.items():
        noise = np.random.default_rng([zlib.crc32(name.encode()), seed]).standard_normal(out[name].shape)
        drawn = base * np.exp(spread * noise) if base else spread * noise
        out[name] = jnp.asarray(drawn.astype(out[name].dtype))
    for name, factor in factors.items():
        out[name] = (out[name] * factor).astype(out[name].dtype)
    return out
```

```python
from contextlib import ExitStack

import concourse.bass as bass
from concourse import mybir

ALU = mybir.AluOpType
ACT = mybir.ActivationFunctionType
AX = mybir.AxisListType
F32 = mybir.dt.float32
BF16 = mybir.dt.bfloat16
U32 = mybir.dt.uint32

P = 128
D = 256
KC = D // P
NH, HD = 16, 16
HA = HD + 1
LANES = 2
E0, H0 = 16, 128
DFF, E1, R1 = 704, 8, 16
FC = -(-DFF // P)
BANKS = 4
BANK = 512
LN_EPS = 1e-5
LORA_SCALE = 2.0
C_ID, C_MASK, C_IOTA, C_BLK, C_PAR = 0, 128, 640, 656, 690
NCONST = 692


def decoder(nc, x, ctx_in, mask_in, const, w_qkv0, b_qk0, b_v0, w_o0, b_o0, sim, gates, moe_qkv, moe_o,
            w_qk1, w_v1, w_o1, x_qk, x_v, x_o, x_bqk, x_bv, x_bo, x_f, f_gu, f_d, f_r, f_a, f_b, f_ad, f_bd, out):
    with ExitStack() as es:
        def sb(name, shape, dt=F32):
            return es.enter_context(nc.sbuf_tensor(name, shape, dt))

        def sem(name):
            return es.enter_context(nc.semaphore(name))

        def lanes(name, shape, dt=F32):
            return [sb(f"{name}{l}", shape, dt) for l in range(LANES)]

        cst = sb("cst", [P, NCONST])
        ident = cst[:, C_ID:C_ID + P]
        iota = cst[:, C_IOTA:C_IOTA + 16]
        block_mask = cst[:, C_BLK:C_BLK + 2 * HA]
        even, odd = cst[:, C_PAR:C_PAR + 1], cst[:, C_PAR + 1:C_PAR + 2]
        ident_b = sb("ident_b", [P, P], BF16)
        mask_b = sb("mask_b", [P, BANK], BF16)
        ones = sb("ones", [P, P])
        neg_half = sb("neg_half", [P, 1])
        eps = sb("eps", [P, 1])
        wqkv0 = sb("wqkv0", [P, KC, 3 * D])
        bqk0 = sb("bqk0", [P, 4])
        bq0_eo = sb("bq0_eo", [P, 2, KC])
        bv0 = sb("bv0", [P, D])
        wo0 = sb("wo0", [P, KC, D])
        bo0 = sb("bo0", [P, D])
        simn = sb("simn", [P, KC, E0])
        simsq = sb("simsq", [P, KC, E0])
        simr = sb("simr", [P, E0])
        neg_half16 = sb("neg_half16", [P, E0])
        sig = sb("sig", [P, E0])
        wmoe = sb("wmoe", [P, KC, E0, 3 * H0])
        wmo = sb("wmo", [P, E0, D])
        wqk1 = sb("wqk1", [P, KC, 2 * D])
        wv1 = sb("wv1", [P, KC, 64])
        wo1 = sb("wo1", [P, KC, D])
        xqk = sb("xqk", [P, KC, 2 * D])
        xv = sb("xv", [P, KC, D])
        xo = sb("xo", [P, KC, D])
        xbqk = sb("xbqk", [P, 4])
        xbv = sb("xbv", [P, D])
        xbo = sb("xbo", [P, D])
        xf = sb("xf", [P, 2, P])
        wgu = sb("wgu", [P, KC, 2 * DFF])
        wd = sb("wd", [P, FC, D])
        wr = sb("wr", [P, KC, E1])
        wa = sb("wa", [P, KC, 2 * P])
        wb = sb("wb", [P, 2 * DFF])
        wad = sb("wad", [P, FC, P])
        wbd = sb("wbd", [P, D])

        xs = lanes("xs", [P, D])
        y = lanes("y", [P, D])
        xb = lanes("xb", [P, D])
        cx = lanes("cx", [P, D])
        cxT = lanes("cxT", [P, KC, P])
        tokmask = lanes("tokmask", [P, 1])
        xT = lanes("xT", [P, KC, P])
        qe = lanes("qe", [P, KC, P])
        qo = lanes("qo", [P, KC, P])
        kT = lanes("kT", [P, KC, P])
        onat = lanes("onat", [P, D])
        oT = lanes("oT", [P, KC, P])
        va = lanes("va", [P, NH, HA])
        big = lanes("big", [P, 2 * FC * 3 * P])
        rmax = lanes("rmax", [P, NH])
        rsum = lanes("rsum", [P, NH])
        stats = lanes("stats", [P, 6])
        mv = lanes("mv", [P, 2])
        ve = lanes("ve", [P, 1])
        rstd = lanes("rstd", [P, 1])
        ss = lanes("ss", [P, 1])
        ssc = lanes("ssc", [P, 1])
        rn = lanes("rn", [P, 1])
        sm = lanes("sm", [P, 8, 16])
        m8 = lanes("m8", [P, 8])
        i8 = lanes("i8", [P, 8], U32)
        i8f = lanes("i8f", [P, 8])
        one = lanes("one", [P, 4])
        qkv = lanes("qkv", [P, 3 * H0])
        kvb = lanes("kvb", [P, NH // 2, 2 * HA])
        rm = lanes("rm", [P, 4, E1 * R1])
        rmT = lanes("rmT", [P, 4, P])
        xam = lanes("xam", [P, 2, 2, P])

        ps = [[es.enter_context(nc.psum_tensor(f"ps{l}_{i}", [P, BANK], F32)) for i in range(BANKS)]
              for l in range(LANES)]

        w_c, w_a0, w_m, w_mo, w_a1, w_x, w_f = [sem(f"w_{n}") for n in ("const", "attn0", "moe", "moe_o", "attn1", "xattn1", "ffn")]
        pre_dve, pre_pe, pre_act, pre_pool = [sem(f"pre_{n}") for n in ("dve", "pe", "act", "pool")]
        names = ("x_in0 x_in1 ctx_in0 ctx_in1 stored x_ready xT_ps xT_sb q_ps k_ps v_ps q_sb k_sb v_sb cT_ps score_ps shifted prob "
                 "probT_ps probT_sb pv_ps o_sb oT_ps oT_sb proj_ps xb_sb ln_var ln_rstd sq_sum sq_rn "
                 "lg_ps lg_read gate_in gate_exp route_w moe_ps moe_acc qk_sb s_ps s_bias s_exp p_norm pT1_ps pT1_sb "
                 "ao_ps ao_sb mo_ps mo_acc feat_ps feat_act feat_dve v_masked kv_ps kv_sb num_ps r_ps xa_ps r_in r_exp rm_sb rmT_ps rmT_sb "
                 "xam_sb base_ps base_sb lora_ps lora_sb silu_sb h_sb ha_ps zz_sb dve act pool").split()
        S = {n: sem(n) for n in names}
        (x_in0, x_in1, ctx_in0, ctx_in1, stored, x_ready, xT_ps, xT_sb, q_ps, k_ps, v_ps, q_sb, k_sb, v_sb, cT_ps, score_ps, shifted, prob,
         probT_ps, probT_sb, pv_ps, o_sb, oT_ps, oT_sb, proj_ps, xb_sb, ln_var, ln_rstd, sq_sum, sq_rn,
         lg_ps, lg_read, gate_in, gate_exp, route_w, moe_ps, moe_acc, qk_sb, s_ps, s_bias, s_exp, p_norm, pT1_ps, pT1_sb,
         ao_ps, ao_sb, mo_ps, mo_acc, feat_ps, feat_act, feat_dve, v_masked, kv_ps, kv_sb, num_ps, r_ps, xa_ps, r_in, r_exp, rm_sb, rmT_ps,
         rmT_sb, xam_sb, base_ps, base_sb, lora_ps, lora_sb, silu_sb, h_sb, ha_ps, zz_sb, dve_done, act_done,
         pool_done) = [S[n] for n in names]
        x_in, ctx_ld = (x_in0, x_in1), (ctx_in0, ctx_in1)
        cleared = [S[n].num for n in names]
        assert max(cleared) - min(cleared) == len(names) - 1

        LN = range(LANES)

        def nth(k, l):
            return LANES * k + l + 1

        def scores_of(l):
            return big[l][:, 0:NH * P].rearrange("p (b h k) -> p b h k", b=BANKS, h=4)

        def probsT_of(l):
            return big[l][:, NH * P:2 * NH * P].rearrange("p (b n) -> p b n", b=BANKS)

        def feat_q(l):
            return big[l][:, 0:BANKS * 2 * P].rearrange("p (b n) -> p b n", b=BANKS)

        def feat_k(l):
            return big[l][:, BANKS * 2 * P:BANKS * 4 * P].rearrange("p (b n) -> p b n", b=BANKS)

        def slot(j, c, par):
            return 8 * c + 2 * j + par

        def ffc(f):
            return min(P, DFF - f * P)

        def g3(l, f):
            return big[l][0:ffc(f), f * 3 * P:(f + 1) * 3 * P].rearrange("p (v t) -> p v t", v=3)

        def u3(l, f):
            o = (FC + f) * 3 * P
            return big[l][0:ffc(f), o:o + 3 * P].rearrange("p (v t) -> p v t", v=3)

        with nc.Block() as pre:
            @pre.sync
            def _(sp):
                def load(dst, src, s):
                    sp.dma_start(dst, src).then_inc(s, 16)

                load(cst[:, :], const, w_c)
                load(simn[:, :, :], sim.rearrange("(c p) e -> p c e", p=P), w_c)
                load(sig[:, :], gates, w_c)
                load(bqk0[:, :], b_qk0, w_c)
                load(wqkv0[:, :, :], w_qkv0.rearrange("(c p) n -> p c n", p=P), w_a0)
                load(bv0[:, :], b_v0, w_a0)
                load(wo0[:, :, :], w_o0.rearrange("(c p) n -> p c n", p=P), w_a0)
                load(bo0[:, :], b_o0, w_a0)
                moe_v = moe_qkv.rearrange("(c p) e n -> p c e n", p=P)
                for c in range(KC):
                    load(wmoe[:, c, :, :], moe_v[:, c, :, :], w_m)
                load(wmo[:, :, :], moe_o.rearrange("e h c -> h e c"), w_mo)
                load(wqk1[:, :, :], w_qk1.rearrange("(c p) n -> p c n", p=P), w_a1)
                load(wv1[:, :, :], w_v1.rearrange("(c p) n -> p c n", p=P), w_a1)
                load(wo1[:, :, :], w_o1.rearrange("(c p) n -> p c n", p=P), w_a1)
                load(xqk[:, :, :], x_qk.rearrange("(c p) n -> p c n", p=P), w_x)
                load(xv[:, :, :], x_v.rearrange("(c p) n -> p c n", p=P), w_x)
                load(xo[:, :, :], x_o.rearrange("(c p) n -> p c n", p=P), w_x)
                load(xbqk[:, :], x_bqk, w_x)
                load(xbv[:, :], x_bv, w_x)
                load(xbo[:, :], x_bo, w_x)
                load(xf[:, :, :], x_f.rearrange("w p n -> p w n"), w_x)
                load(wgu[:, :, :], f_gu.rearrange("(c p) n -> p c n", p=P), w_f)
                load(wd[:, 0:FC - 1, :], f_d[0:(FC - 1) * P, :].rearrange("(c p) n -> p c n", p=P), w_f)
                load(wd[0:ffc(FC - 1), FC - 1, :], f_d[(FC - 1) * P:DFF, :], w_f)
                load(wr[:, :, :], f_r.rearrange("(c p) n -> p c n", p=P), w_f)
                load(wa[:, :, :], f_a.rearrange("(c p) n -> p c n", p=P), w_f)
                load(wb[:, :], f_b, w_f)
                load(wad[:, 0:FC - 1, :], f_ad[0:(FC - 1) * P, :].rearrange("(c p) n -> p c n", p=P), w_f)
                load(wad[0:ffc(FC - 1), FC - 1, :], f_ad[(FC - 1) * P:DFF, :], w_f)
                load(wbd[:, :], f_bd, w_f)

            @pre.vector
            def _(dve):
                nc.vector.memset(ones[:, :], 1.0).then_inc(pre_dve, 1)
                nc.vector.memset(neg_half[:, :], -0.5)
                nc.vector.memset(neg_half16[:, :], -0.5)
                nc.vector.memset(eps[:, :], LN_EPS)
                for l in LN:
                    nc.vector.memset(va[l][:, :, :], 1.0)
                dve.wait_ge(w_c, 64)
                nc.vector.tensor_copy(ident_b[:, :], ident)
                nc.vector.tensor_copy(mask_b[:, :], cst[:, C_MASK:C_MASK + BANK])
                nc.vector.tensor_scalar(bq0_eo[:, 0, :], bqk0[:, 0:KC], even, None, ALU.mult)
                nc.vector.tensor_scalar(bq0_eo[:, 1, :], bqk0[:, 0:KC], odd, None, ALU.mult)
                nc.vector.tensor_tensor(simsq[:, :, :], simn[:, :, :], simn[:, :, :], ALU.mult).then_inc(pre_dve, 1)
                dve.wait_ge(pre_act, 1)
                nc.vector.tensor_scalar(sig[:, :], sig[:, :], 1.0, None, ALU.add).then_inc(pre_dve, 1)
                dve.wait_ge(pre_dve, 3)
                nc.vector.reciprocal(sig[:, :], sig[:, :])
                dve.wait_ge(pre_pe, 1)
                nc.vector.tensor_scalar(simr[:, :], ps[0][0][:, 0:E0], 1e-24, None, ALU.max).then_inc(pre_dve, 1)
                dve.wait_ge(pre_pool, 1)
                nc.vector.tensor_tensor(simn[:, :, :], simn[:, :, :],
                                        simr[:, :].unsqueeze(1).broadcast_to([P, KC, E0]), ALU.mult).then_inc(pre_dve, 1)

            @pre.scalar
            def _(act):
                act.wait_ge(w_c, 64)
                nc.scalar.activation(sig[:, :], sig[:, :], ACT.Exp, scale=-1.0).then_inc(pre_act, 1)

            @pre.tensor
            def _(pe):
                pe.wait_ge(pre_dve, 2)
                for c in range(KC):
                    mm = nc.tensor.matmul(ps[0][0][:, 0:E0], ones[:, :], simsq[:, c, :], start=(c == 0), stop=(c == KC - 1))
                mm.then_inc(pre_pe, 1)

            @pre.gpsimd
            def _(pool):
                pool.wait_ge(pre_dve, 4)
                nc.gpsimd.tensor_tensor(simr[:, :], simr[:, :], neg_half16[:, :], ALU.pow).then_inc(pre_pool, 1)

        x_v = x.rearrange("(i l) p c -> i l p c", l=LANES)
        c_v = ctx_in.rearrange("(i l) p c -> i l p c", l=LANES)
        m_v = mask_in.rearrange("(i l) p c -> i l p c", l=LANES)
        o_v = out.rearrange("(i l) p c -> i l p c", l=LANES)

        def flat(ap):
            return ap.rearrange("a p c -> (a p) c")

        with nc.Fori(0, 16 // LANES) as it:
            with nc.Block() as block:

                @block.sync
                def _(sp):
                    for l in LN:
                        sp.dma_start(xs[l][:, :], flat(x_v[bass.ds(it, 1), l, :, :])).then_inc(x_in[l], 16)
                        sp.dma_start(cx[l][:, :], flat(c_v[bass.ds(it, 1), l, :, :])).then_inc(ctx_ld[l], 16)
                        sp.dma_start(tokmask[l][:, :], flat(m_v[bass.ds(it, 1), l, :, :])).then_inc(ctx_ld[l], 16)
                    for l in LN:
                        sp.wait_ge(x_ready, nth(5, l))
                        sp.dma_start(flat(o_v[bass.ds(it, 1), l, :, :]), xs[l][:, :]).then_inc(stored, 16)
                    sp.wait_ge(stored, 16 * LANES)

                @block.tensor
                def _(pe):
                    def x_transposed(L):
                        for l in LN:
                            if L == 0:
                                pe.wait_ge(x_in[l], 16)
                            else:
                                pe.wait_ge(x_ready, nth(L - 1, l))
                            for c in range(KC):
                                mm = nc.tensor.transpose(ps[l][0][:, c * P:(c + 1) * P], xs[l][:, c * P:(c + 1) * P], ident)
                            mm.then_inc(xT_ps, 1)

                    def qk_projected(k, L, w, src):
                        for l in LN:
                            pe.wait_ge(xT_sb, nth(L, l))
                            for part, done in ((0, q_ps), (1, k_ps)):
                                a = xT[l] if part == 0 or src is None else src[l]
                                for m in range(KC):
                                    for c in range(KC):
                                        o = part * D + m * P
                                        mm = nc.tensor.matmul(ps[l][1 + part][:, m * P:(m + 1) * P], w[:, c, o:o + P],
                                                              a[:, c, :], start=(c == 0), stop=(c == KC - 1))
                                mm.then_inc(done, 1)

                    def v_projected(w, n, src):
                        for l in LN:
                            for c in range(KC):
                                mm = nc.tensor.matmul(ps[l][3][:, 0:n], src[l][:, c, :], w(c), start=(c == 0), stop=(c == KC - 1))
                            mm.then_inc(v_ps, 1)

                    def heads(k, kt, group):
                        for l in LN:
                            pe.wait_ge(q_sb, nth(k, l))
                            pe.wait_ge(k_sb, nth(k, l))
                            pe.wait_ge(v_sb, nth(k, l))
                            for j in range(BANKS):
                                nc.tensor.matmul(ps[l][j][:, :], ident_b[:, :], mask_b[:, :], start=True, stop=False,
                                                 skip_group_check=True)
                            for c in range(KC):
                                for par, q in enumerate((qe, qo)):
                                    for j in range(BANKS):
                                        r = slice(32 * j, 32 * j + 32)
                                        o = (2 * c + par) * P
                                        mm = nc.tensor.matmul(ps[l][j][:, o:o + P], q[l][r, c, :], kt[l][r, c, :],
                                                              start=False, stop=(c == KC - 1 and par == 1),
                                                              tile_position=(32 * j, 0), skip_group_check=True)
                                        if c == KC - 1 and par == 1:
                                            mm.then_inc(score_ps, 1)
                        for l in LN:
                            for j in range(BANKS):
                                pe.wait_ge(prob, BANKS * (LANES * k + l) + j + 1)
                                for h in range(4):
                                    mm = nc.tensor.transpose(ps[l][j][:, h * P:(h + 1) * P], scores_of(l)[:, j, h, :], ident)
                                mm.then_inc(probT_ps, 1)
                        for l in LN:
                            pe.wait_ge(probT_sb, BANKS * (LANES * k + l) + BANKS)
                            for j in range(BANKS):
                                for c in range(KC):
                                    for par in range(2):
                                        h = slot(j, c, par)
                                        o = (2 * c + par) * P
                                        mm = nc.tensor.matmul(ps[l][0][:, h * HA:(h + 1) * HA], probsT_of(l)[:, j, o:o + P],
                                                              va[l][:, h // group, :], start=True, stop=True)
                            mm.then_inc(pv_ps, 1)

                    def out_transposed(k):
                        for l in LN:
                            pe.wait_ge(o_sb, nth(k, l))
                            for c in range(KC):
                                mm = nc.tensor.transpose(ps[l][1][:, c * P:(c + 1) * P], onat[l][:, c * P:(c + 1) * P], ident)
                            mm.then_inc(oT_ps, 1)

                    def out_projected(k, w):
                        for l in LN:
                            pe.wait_ge(oT_sb, nth(k, l))
                            for c in range(KC):
                                mm = nc.tensor.matmul(ps[l][2][:, 0:D], oT[l][:, c, :], w[:, c, :], start=(c == 0), stop=(c == KC - 1))
                            mm.then_inc(proj_ps, 1)

                    x_transposed(0)
                    pe.wait_ge(w_a0, 64)
                    qk_projected(0, 0, wqkv0, None)
                    v_projected(lambda c: wqkv0[:, c, 2 * D:3 * D], D, xT)
                    heads(0, kT, 1)
                    out_transposed(0)
                    out_projected(0, wo0)

                    for l in LN:
                        pe.wait_ge(ctx_ld[l], 32)
                        for c in range(KC):
                            mm = nc.tensor.transpose(ps[l][3][:, c * P:(c + 1) * P], cx[l][:, c * P:(c + 1) * P], ident)
                        mm.then_inc(cT_ps, 1)
                    x_transposed(1)
                    heads(1, cxT, 1)

                    x_transposed(2)
                    for l in LN:
                        pe.wait_ge(xT_sb, nth(1, l))
                        for c in range(KC):
                            mm = nc.tensor.matmul(ps[l][1][:, 0:E0], xT[l][:, c, :], simn[:, c, :], start=(c == 0), stop=(c == KC - 1))
                        mm.then_inc(lg_ps, 1)
                    pe.wait_ge(w_m, 32)
                    for l in LN:
                        for e in range(E0):
                            n = E0 * l + e
                            if e == 3:
                                pe.wait_ge(lg_read, l + 1)
                            if e >= BANKS:
                                pe.wait_ge(moe_acc, n - BANKS + 1)
                            for c in range(KC):
                                mm = nc.tensor.matmul(ps[l][(e + 2) % BANKS][:, 0:3 * H0], xT[l][:, c, :], wmoe[:, c, e, :],
                                                      start=(c == 0), stop=(c == KC - 1))
                            mm.then_inc(moe_ps, 1)
                    for l in LN:
                        pe.wait_ge(moe_acc, E0 * (l + 1))
                        for i in range(2):
                            mm = nc.tensor.transpose(ps[l][0][:, i * P:(i + 1) * P], qkv[l][:, i * P:(i + 1) * P], ident)
                        mm.then_inc(xT_ps, 1)
                    for l in LN:
                        pe.wait_ge(qk_sb, l + 1)
                        nc.tensor.matmul(ps[l][1][:, 0:P], ident_b[:, :], mask_b[:, 0:P], start=True, stop=False)
                        nc.tensor.matmul(ps[l][1][:, 0:P], qe[l][:, 0, :], qe[l][:, 1, :], start=False, stop=True).then_inc(s_ps, 1)
                    for l in LN:
                        pe.wait_ge(p_norm, l + 1)
                        nc.tensor.transpose(ps[l][2][:, 0:P], qo[l][:, 0, :], ident).then_inc(pT1_ps, 1)
                    for l in LN:
                        pe.wait_ge(pT1_sb, l + 1)
                        nc.tensor.matmul(ps[l][3][:, 0:P], qkv[l][:, 2 * P:3 * P], qo[l][:, 1, :], start=True, stop=True).then_inc(ao_ps, 1)
                    pe.wait_ge(w_mo, 16)
                    for l in LN:
                        pe.wait_ge(ao_sb, l + 1)
                        for i in range(E0 // 2):
                            n = E0 // 2 * l + i
                            if i >= BANKS:
                                pe.wait_ge(mo_acc, 2 * (n - BANKS + 1))
                            nc.tensor.matmul(ps[l][i % BANKS][:, :], kT[l][:, 0, :], wmo[:, 2 * i:2 * i + 2, :], start=True,
                                             stop=True).then_inc(mo_ps, 1)

                    x_transposed(3)
                    pe.wait_ge(w_a1, 48)
                    qk_projected(1, 2, wqk1, None)
                    v_projected(lambda c: wv1[:, c, :], 64, xT)
                    heads(2, kT, 4)
                    out_transposed(2)
                    out_projected(1, wo1)

                    x_transposed(4)
                    pe.wait_ge(w_x, 16 * 7)
                    qk_projected(2, 3, xqk, cxT)
                    v_projected(lambda c: xv[:, c, :], D, cxT)
                    for l in LN:
                        pe.wait_ge(q_sb, nth(3, l))
                        pe.wait_ge(k_sb, nth(3, l))
                        pe.wait_ge(v_sb, nth(3, l))
                        for c in range(KC):
                            for j in range(BANKS):
                                r = slice(32 * j, 32 * j + 32)
                                o = c * P
                                nc.tensor.matmul(ps[l][j][:, o:o + P], xf[r, 0, :], qe[l][r, c, :], start=True, stop=True,
                                                 tile_position=(32 * j, 0))
                                mm = nc.tensor.matmul(ps[l][j][:, 2 * P + o:2 * P + o + P], kT[l][r, c, :], xf[r, 1, :],
                                                      start=True, stop=True, tile_position=(32 * j, 0))
                                if c == KC - 1:
                                    mm.then_inc(feat_ps, 1)
                    for l in LN:
                        pe.wait_ge(feat_act, 2 * (l + 1))
                        pe.wait_ge(feat_dve, 2 * (l + 1))
                        pe.wait_ge(v_masked, l + 1)
                        for m in range(NH // 2):
                            c, j = m // BANKS, m % BANKS
                            mm = nc.tensor.matmul(ps[l][0][:, 2 * HA * m:2 * HA * (m + 1)], feat_k(l)[:, j, c * P:(c + 1) * P],
                                                  va[l][:, 2 * m:2 * m + 2, :], start=True, stop=True)
                        mm.then_inc(kv_ps, 1)
                    for l in LN:
                        pe.wait_ge(kv_sb, l + 1)
                        for m in range(NH // 2):
                            c, j = m // BANKS, m % BANKS
                            mm = nc.tensor.matmul(ps[l][0][:, 2 * HA * m:2 * HA * (m + 1)], feat_q(l)[:, j, c * P:(c + 1) * P],
                                                  kvb[l][:, m, :], start=True, stop=True)
                        mm.then_inc(num_ps, 1)
                    out_transposed(3)
                    out_projected(2, xo)

                    x_transposed(5)
                    pe.wait_ge(w_f, 16 * 9)
                    for l in LN:
                        pe.wait_ge(xT_sb, nth(4, l))
                        for c in range(KC):
                            mm = nc.tensor.matmul(ps[l][1][:, 0:E1], xT[l][:, c, :], wr[:, c, :], start=(c == 0), stop=(c == KC - 1))
                        mm.then_inc(r_ps, 1)
                        for m in range(2):
                            for c in range(KC):
                                mm = nc.tensor.matmul(ps[l][2][:, m * P:(m + 1) * P], wa[:, c, m * P:(m + 1) * P], xT[l][:, c, :],
                                                      start=(c == 0), stop=(c == KC - 1))
                        mm.then_inc(xa_ps, 1)
                    for l in LN:
                        pe.wait_ge(rm_sb, l + 1)
                        for i in range(4):
                            mm = nc.tensor.transpose(ps[l][3][:, i * P:(i + 1) * P], rm[l][:, i, :], ident)
                        mm.then_inc(rmT_ps, 1)
                    for l in LN:
                        pe.wait_ge(xam_sb, l + 1)
                    for f in range(FC):
                        for l in LN:
                            n = LANES * f + l
                            w = ffc(f)
                            if f >= 2:
                                pe.wait_ge(base_sb, n - 2 * LANES + 1)
                            for m in range(2):
                                for c in range(KC):
                                    o = m * DFF + f * P
                                    mm = nc.tensor.matmul(ps[l][2 * (f % 2)][0:w, m * P:(m + 1) * P], wgu[:, c, o:o + w],
                                                          xT[l][:, c, :], start=(c == 0), stop=(c == KC - 1))
                            mm.then_inc(base_ps, 1)
                            if f >= 2:
                                pe.wait_ge(lora_sb, n - 2 * LANES + 1)
                            for m in range(2):
                                o = m * DFF + f * P
                                mm = nc.tensor.matmul(ps[l][2 * (f % 2) + 1][0:w, m * 2 * P:(m + 1) * 2 * P], wb[:, o:o + w],
                                                      xam[l][:, m, :, :], start=True, stop=True)
                            mm.then_inc(lora_ps, 1)
                    for l in LN:
                        pe.wait_ge(lora_sb, LANES * (FC - 1) + l + 1)
                        pe.wait_ge(base_sb, LANES * (FC - 1) + l + 1)
                        pe.wait_ge(h_sb, LANES * (FC - 1) + l + 1)
                        for f in range(FC):
                            w = ffc(f)
                            mm = nc.tensor.matmul(ps[l][1][:, 0:2 * P], wad[0:w, f, :], g3(l, f)[:, 1:3, :], start=(f == 0), stop=(f == FC - 1))
                        mm.then_inc(ha_ps, 1)
                        for f in range(FC):
                            w = ffc(f)
                            nc.tensor.matmul(ps[l][0][:, 0:D], g3(l, f)[:, 0, :], wd[0:w, f, :], start=(f == 0), stop=False)
                    for l in LN:
                        pe.wait_ge(zz_sb, l + 1)
                        for s in range(2):
                            mm = nc.tensor.matmul(ps[l][0][:, 0:D], kT[l][:, s, :], wbd[:, :], start=False, stop=(s == 1))
                        mm.then_inc(proj_ps, 1)

                @block.scalar
                def _(act):
                    def copied(dst, src, need, count, done):
                        for l in LN:
                            act.wait_ge(need, count + l)
                            nc.scalar.activation(dst(l), src(l), ACT.Copy).then_inc(done, 1)

                    def bank(b, n, m=KC):
                        return lambda l: ps[l][b][:, 0:m * n].rearrange("p (m n) -> p m n", m=m)

                    def whole(t):
                        return lambda l: t[l][:, :, :]

                    def heads(k):
                        for l in LN:
                            for j in range(BANKS):
                                act.wait_ge(shifted, BANKS * (LANES * k + l) + j + 1)
                                sc = scores_of(l)[:, j, :, :]
                                nc.scalar.activation(sc, sc, ACT.Exp, scale=HD ** -0.5).then_inc(prob, 1)
                        for l in LN:
                            for j in range(BANKS):
                                act.wait_ge(probT_ps, BANKS * (LANES * k + l) + j + 1)
                                nc.scalar.activation(probsT_of(l)[:, j, :], ps[l][j][:, :], ACT.Copy).then_inc(probT_sb, 1)

                    copied(whole(xT), bank(0, P), xT_ps, nth(0, 0), xT_sb)
                    for l in LN:
                        act.wait_ge(k_ps, l + 1)
                        for c in range(KC):
                            a = nc.scalar.activation(kT[l][:, c, :], ps[l][2][:, c * P:(c + 1) * P], ACT.Identity, bias=bqk0[:, 2 + c:3 + c])
                        a.then_inc(k_sb, 1)
                    heads(0)
                    copied(whole(oT), bank(1, P), oT_ps, nth(0, 0), oT_sb)

                    copied(whole(cxT), bank(3, P), cT_ps, 1, k_sb)
                    heads(1)

                    for l in LN:
                        act.wait_ge(x_ready, nth(1, l))
                        nc.scalar.activation(onat[l][:, :], xs[l][:, :], ACT.Square, accum_out=ss[l][:, :]).then_inc(sq_sum, 1)
                    copied(whole(xT), bank(0, P), xT_ps, nth(2, 0), xT_sb)
                    for l in LN:
                        act.wait_ge(gate_in, l + 1)
                        nc.scalar.activation(sm[l][:, 2, :], sm[l][:, 1, :], ACT.Exp, bias=one[l][:, 0:1]).then_inc(gate_exp, 1)
                    copied(whole(qe), bank(0, P), xT_ps, nth(3, 0), qk_sb)
                    for l in LN:
                        act.wait_ge(s_bias, l + 1)
                        nc.scalar.activation(qo[l][:, 0, :], ps[l][1][:, 0:P], ACT.Exp, bias=one[l][:, 1:2], scale=H0 ** -0.5,
                                             accum_out=one[l][:, 2:3]).then_inc(s_exp, 1)
                    copied(lambda l: qo[l][:, 1, :], lambda l: ps[l][2][:, 0:P], pT1_ps, 1, pT1_sb)
                    copied(lambda l: kT[l][:, 0, :], lambda l: ps[l][3][:, 0:P], ao_ps, 1, ao_sb)

                    copied(whole(xT), bank(0, P), xT_ps, nth(4, 0), xT_sb)
                    copied(whole(kT), bank(2, P), k_ps, nth(1, 0), k_sb)
                    for l in LN:
                        act.wait_ge(v_ps, nth(1, l))
                        nc.scalar.activation(va[l][:, 0:4, 0:HD], ps[l][3][:, 0:64].rearrange("p (h d) -> p h d", h=4), ACT.Copy).then_inc(v_sb, 1)
                    heads(2)
                    copied(whole(oT), bank(1, P), oT_ps, nth(1, 0), oT_sb)

                    copied(whole(xT), bank(0, P), xT_ps, nth(5, 0), xT_sb)
                    for l in LN:
                        act.wait_ge(k_ps, nth(2, l))
                        for c in range(KC):
                            a = nc.scalar.activation(kT[l][:, c, :], ps[l][2][:, c * P:(c + 1) * P], ACT.Identity, bias=xbqk[:, 2 + c:3 + c])
                        a.then_inc(k_sb, 1)
                    for l in LN:
                        for j in (0, 1):
                            act.wait_ge(feat_ps, BANKS * l + j + 1)
                            nc.scalar.activation(feat_q(l)[:, j, :], ps[l][j][:, 0:2 * P], ACT.Relu)
                            nc.scalar.activation(feat_k(l)[:, j, :], ps[l][j][:, 2 * P:4 * P], ACT.Relu).then_inc(feat_act, 1)
                    copied(whole(oT), bank(1, P), oT_ps, nth(2, 0), oT_sb)

                    copied(whole(xT), bank(0, P), xT_ps, nth(6, 0), xT_sb)
                    for l in LN:
                        act.wait_ge(r_in, l + 1)
                        nc.scalar.activation(sm[l][:, 0, 0:E1], sm[l][:, 0, 0:E1], ACT.Exp, bias=one[l][:, 0:1], accum_out=one[l][:, 1:2]).then_inc(r_exp, 1)
                    copied(lambda l: rmT[l][:, :, :], bank(3, P, 4), rmT_ps, 1, rmT_sb)
                    for f in range(FC + 1):
                        if f < FC:
                            for l in LN:
                                act.wait_ge(base_ps, LANES * f + l + 1)
                                w = ffc(f)
                                nc.scalar.activation(g3(l, f)[:, 0, :], ps[l][2 * (f % 2)][0:w, 0:P], ACT.Copy)
                                nc.scalar.activation(u3(l, f)[:, 0, :], ps[l][2 * (f % 2)][0:w, P:2 * P], ACT.Copy).then_inc(base_sb, 1)
                        if f >= 1:
                            for l in LN:
                                act.wait_ge(lora_sb, LANES * (f - 1) + l + 1)
                                nc.scalar.activation(g3(l, f - 1), g3(l, f - 1), ACT.Silu).then_inc(silu_sb, 1)

                @block.gpsimd
                def _(pool):
                    n = [0]

                    def then(ins):
                        n[0] += 1
                        ins.then_inc(pool_done, 1)
                        pool.wait_ge(pool_done, n[0])

                    def inverse_std(L):
                        for l in LN:
                            pool.wait_ge(ln_var, nth(L, l))
                            then(nc.gpsimd.tensor_tensor(ve[l][:, :], mv[l][:, 1:2], eps[:, :], ALU.add))
                            nc.gpsimd.tensor_tensor(rstd[l][:, :], ve[l][:, :], neg_half[:, :], ALU.pow).then_inc(ln_rstd, 1)

                    pool.wait_ge(w_a0, 64)
                    for l in LN:
                        pool.wait_ge(x_in[l], 16)
                        nc.gpsimd.tensor_tensor(xb[l][:, :], xs[l][:, :], bo0[:, :], ALU.add).then_inc(xb_sb, 1)
                    inverse_std(0)
                    for l in LN:
                        pool.wait_ge(ctx_ld[l], 32)
                        pool.wait_ge(pv_ps, nth(0, l))
                        nc.gpsimd.tensor_copy(va[l][:, :, 0:HD], cx[l][:, :].rearrange("p (h d) -> p h d", h=NH)).then_inc(v_sb, 1)
                    inverse_std(1)
                    for l in LN:
                        pool.wait_ge(sq_sum, l + 1)
                        then(nc.gpsimd.tensor_scalar(ssc[l][:, :], ss[l][:, :], 1e-24, None, ALU.max))
                        nc.gpsimd.tensor_tensor(rn[l][:, :], ssc[l][:, :], neg_half[:, :], ALU.pow).then_inc(sq_rn, 1)
                    inverse_std(2)
                    inverse_std(3)
                    pool.wait_ge(w_x, 16 * 7)
                    for l in LN:
                        pool.wait_ge(x_ready, nth(3, l))
                        nc.gpsimd.tensor_tensor(xb[l][:, :], xs[l][:, :], xbo[:, :], ALU.add).then_inc(xb_sb, 1)
                    for l in LN:
                        pool.wait_ge(v_sb, nth(3, l))
                        nc.gpsimd.tensor_scalar(va[l][:, :, :], va[l][:, :, :], tokmask[l][:, 0:1], None, ALU.mult).then_inc(v_masked, 1)
                    inverse_std(4)
                    for f in range(FC):
                        for l in LN:
                            pool.wait_ge(silu_sb, LANES * f + l + 1)
                            nc.gpsimd.tensor_tensor(g3(l, f), g3(l, f), u3(l, f), ALU.mult).then_inc(h_sb, 1)
                    inverse_std(5)

                @block.vector
                def _(dve):
                    n = [0]

                    def then(ins):
                        n[0] += 1
                        ins.then_inc(dve_done, 1)
                        dve.wait_ge(dve_done, n[0])

                    def norm(L):
                        for l in LN:
                            then(nc.vector.bn_stats(stats[l][:, :], y[l][:, :]))
                            nc.vector.bn_aggr(mv[l][:, :], stats[l][:, :]).then_inc(ln_var, 1)
                        for l in LN:
                            dve.wait_ge(ln_rstd, nth(L, l))
                            nc.vector.tensor_scalar(xs[l][:, :], y[l][:, :], mv[l][:, 0:1], rstd[l][:, 0:1], ALU.subtract,
                                                    ALU.mult).then_inc(x_ready, 1)

                    def heads(k):
                        for l in LN:
                            for j in range(BANKS):
                                dve.wait_ge(score_ps, BANKS * (LANES * k + l) + j + 1)
                                sc = ps[l][j][:, :].rearrange("p (h k) -> p h k", h=4)
                                mx = rmax[l][:, 4 * j:4 * j + 4]
                                then(nc.vector.tensor_reduce(mx, sc, AX.X, ALU.max))
                                nc.vector.tensor_tensor(scores_of(l)[:, j, :, :], sc, mx.unsqueeze(2).broadcast_to([P, 4, P]),
                                                        ALU.subtract).then_inc(shifted, 1)
                        for l in LN:
                            dve.wait_ge(pv_ps, nth(k, l))
                            pv = ps[l][0][:, 0:NH * HA].rearrange("p (h d) -> p h d", h=NH)
                            then(nc.vector.reciprocal(rsum[l][:, :].unsqueeze(2), pv[:, :, HD:HA]))
                            nc.vector.tensor_tensor(onat[l][:, :].rearrange("p (h d) -> p h d", h=NH), pv[:, :, 0:HD],
                                                    rsum[l][:, :].unsqueeze(2).broadcast_to([P, NH, HD]), ALU.mult).then_inc(o_sb, 1)

                    def v_biased(k, bias):
                        for l in LN:
                            dve.wait_ge(v_ps, nth(k, l))
                            nc.vector.tensor_tensor(va[l][:, :, 0:HD], ps[l][3][:, 0:D].rearrange("p (h d) -> p h d", h=NH),
                                                    bias[:, :].rearrange("p (h d) -> p h d", h=NH), ALU.add).then_inc(v_sb, 1)

                    dve.wait_ge(w_a0, 64)
                    for l in LN:
                        dve.wait_ge(q_ps, nth(0, l))
                        for i, (q, keep) in enumerate(((qe, even), (qo, odd))):
                            for c in range(KC):
                                v = nc.vector.tensor_scalar(q[l][:, c, :], ps[l][1][:, c * P:(c + 1) * P], keep, bq0_eo[:, i, c:c + 1],
                                                            ALU.mult, ALU.add)
                        v.then_inc(q_sb, 1)
                    v_biased(0, bv0)
                    heads(0)
                    for l in LN:
                        dve.wait_ge(proj_ps, nth(0, l))
                        dve.wait_ge(xb_sb, nth(0, l))
                        then(nc.vector.tensor_tensor(y[l][:, :], ps[l][2][:, 0:D], xb[l][:, :], ALU.add))
                    norm(0)

                    for l in LN:
                        dve.wait_ge(xT_ps, nth(1, l))
                        src = ps[l][0][:, 0:D].rearrange("p (c n) -> p c n", c=KC)
                        nc.vector.tensor_scalar(qe[l][:, :, :], src, even, None, ALU.mult)
                        nc.vector.tensor_scalar(qo[l][:, :, :], src, odd, None, ALU.mult).then_inc(q_sb, 1)
                    heads(1)
                    for l in LN:
                        dve.wait_ge(o_sb, nth(1, l))
                        then(nc.vector.tensor_tensor(y[l][:, :], onat[l][:, :], xs[l][:, :], ALU.add))
                    norm(1)

                    for l in LN:
                        t = sm[l]
                        dve.wait_ge(lg_ps, l + 1)
                        dve.wait_ge(sq_rn, l + 1)
                        nc.vector.scalar_tensor_tensor(t[:, 0, :], ps[l][1][:, 0:E0], rn[l][:, 0:1], sig[:, :], ALU.mult,
                                                       ALU.subtract).then_inc(lg_read, 1)
                        dve.wait_ge(lg_read, l + 1)
                        then(nc.vector.tensor_scalar(t[:, 1, :], t[:, 0, :], 0.0, None, ALU.max))
                        then(nc.vector.max(m8[l][:, :], t[:, 0, :]))
                        nc.vector.tensor_scalar(one[l][:, 0:1], m8[l][:, 0:1], 0.0, -1.0, ALU.max, ALU.mult).then_inc(gate_in, 1)
                        then(nc.vector.max_index(i8[l][:, :], m8[l][:, :], t[:, 0, :]))
                        then(nc.vector.tensor_copy(i8f[l][:, :], i8[l][:, :]))
                        nc.vector.tensor_scalar(t[:, 4, :], t[:, 0, :], 0.0, None, ALU.is_gt)
                        nc.vector.tensor_scalar(one[l][:, 1:2], m8[l][:, 0:1], 0.0, None, ALU.is_le)
                        then(nc.vector.tensor_scalar(t[:, 3, :], iota, i8f[l][:, 0:1], None, ALU.is_equal))
                        then(nc.vector.scalar_tensor_tensor(t[:, 5, :], iota, i8f[l][:, 1:2], t[:, 3, :], ALU.is_equal, ALU.max))
                        then(nc.vector.scalar_tensor_tensor(t[:, 6, :], t[:, 5, :], one[l][:, 1:2], t[:, 4, :], ALU.mult, ALU.max))
                        dve.wait_ge(gate_exp, l + 1)
                        then(nc.vector.scalar_tensor_tensor(t[:, 7, :], t[:, 2, :], 1.0, t[:, 6, :], ALU.mult, ALU.mult,
                                                            accum_out=one[l][:, 2:3]))
                        then(nc.vector.reciprocal(one[l][:, 3:4], one[l][:, 2:3]))
                        then(nc.vector.tensor_scalar(t[:, 3, :], t[:, 7, :], one[l][:, 3:4], None, ALU.mult))
                    for l in LN:
                        for e in range(E0):
                            dve.wait_ge(moe_ps, E0 * l + e + 1)
                            src = ps[l][(e + 2) % BANKS][:, 0:3 * H0]
                            we = sm[l][:, 3, e:e + 1]
                            if e == 0:
                                v = nc.vector.tensor_scalar(qkv[l][:, :], src, we, None, ALU.mult)
                            else:
                                dve.wait_ge(moe_acc, E0 * l + e)
                                v = nc.vector.scalar_tensor_tensor(qkv[l][:, :], src, we, qkv[l][:, :], ALU.mult, ALU.add)
                            v.then_inc(moe_acc, 1)
                    for l in LN:
                        dve.wait_ge(s_ps, l + 1)
                        then(nc.vector.tensor_reduce(one[l][:, 0:1], ps[l][1][:, 0:P], AX.X, ALU.max))
                        nc.vector.tensor_scalar(one[l][:, 1:2], one[l][:, 0:1], -(H0 ** -0.5), None, ALU.mult).then_inc(s_bias, 1)
                    for l in LN:
                        dve.wait_ge(s_exp, l + 1)
                        then(nc.vector.reciprocal(one[l][:, 3:4], one[l][:, 2:3]))
                        nc.vector.tensor_scalar(qo[l][:, 0, :], qo[l][:, 0, :], one[l][:, 3:4], None, ALU.mult).then_inc(p_norm, 1)
                    for l in LN:
                        for i in range(E0 // 2):
                            dve.wait_ge(mo_ps, E0 // 2 * l + i + 1)
                            for s in range(2):
                                e = 2 * i + s
                                if e:
                                    dve.wait_ge(mo_acc, E0 * l + e)
                                nc.vector.scalar_tensor_tensor(y[l][:, :], ps[l][i % BANKS][:, s * D:(s + 1) * D], sm[l][:, 3, e:e + 1],
                                                               (y if e else xs)[l][:, :], ALU.mult, ALU.add).then_inc(mo_acc, 1)
                    dve.wait_ge(mo_acc, E0 * LANES)
                    norm(2)

                    for l in LN:
                        dve.wait_ge(q_ps, nth(1, l))
                        src = ps[l][1][:, 0:D].rearrange("p (c n) -> p c n", c=KC)
                        nc.vector.tensor_scalar(qe[l][:, :, :], src, even, None, ALU.mult)
                        nc.vector.tensor_scalar(qo[l][:, :, :], src, odd, None, ALU.mult).then_inc(q_sb, 1)
                    heads(2)
                    for l in LN:
                        dve.wait_ge(proj_ps, nth(1, l))
                        then(nc.vector.tensor_tensor(y[l][:, :], ps[l][2][:, 0:D], xs[l][:, :], ALU.add))
                    norm(3)

                    dve.wait_ge(w_x, 16 * 7)
                    for l in LN:
                        dve.wait_ge(q_ps, nth(2, l))
                        for c in range(KC):
                            v = nc.vector.tensor_scalar(qe[l][:, c, :], ps[l][1][:, c * P:(c + 1) * P], xbqk[:, c:c + 1], None, ALU.add)
                        v.then_inc(q_sb, 1)
                    v_biased(2, xbv)
                    for l in LN:
                        for j in (2, 3):
                            dve.wait_ge(feat_ps, BANKS * l + j + 1)
                            nc.vector.tensor_scalar(feat_q(l)[:, j, :], ps[l][j][:, 0:2 * P], 0.0, None, ALU.max)
                            nc.vector.tensor_scalar(feat_k(l)[:, j, :], ps[l][j][:, 2 * P:4 * P], 0.0, None, ALU.max).then_inc(feat_dve, 1)
                    for l in LN:
                        dve.wait_ge(kv_ps, l + 1)
                        nc.vector.tensor_tensor(kvb[l][:, :, :], ps[l][0][:, 0:NH * HA].rearrange("p (m n) -> p m n", m=NH // 2),
                                                block_mask.unsqueeze(1).broadcast_to([P, NH // 2, 2 * HA]), ALU.mult).then_inc(kv_sb, 1)
                    for l in LN:
                        dve.wait_ge(num_ps, l + 1)
                        pv = ps[l][0][:, 0:NH * HA].rearrange("p (h d) -> p h d", h=NH)
                        then(nc.vector.tensor_scalar(rmax[l][:, :].unsqueeze(2), pv[:, :, HD:HA], 1e-8, None, ALU.add))
                        then(nc.vector.reciprocal(rsum[l][:, :], rmax[l][:, :]))
                        nc.vector.tensor_tensor(onat[l][:, :].rearrange("p (h d) -> p h d", h=NH), pv[:, :, 0:HD],
                                                rsum[l][:, :].unsqueeze(2).broadcast_to([P, NH, HD]), ALU.mult).then_inc(o_sb, 1)
                    for l in LN:
                        nc.vector.memset(va[l][:, :, HD:HA], 1.0)
                    for l in LN:
                        dve.wait_ge(proj_ps, nth(2, l))
                        dve.wait_ge(xb_sb, nth(1, l))
                        then(nc.vector.tensor_tensor(y[l][:, :], ps[l][2][:, 0:D], xb[l][:, :], ALU.add))
                    norm(4)

                    for l in LN:
                        t = sm[l]
                        dve.wait_ge(r_ps, l + 1)
                        then(nc.vector.tensor_reduce(one[l][:, 0:1], ps[l][1][:, 0:E1], AX.X, ALU.max, negate=True))
                        nc.vector.tensor_copy(t[:, 0, 0:E1], ps[l][1][:, 0:E1]).then_inc(r_in, 1)
                    for l in LN:
                        t = sm[l]
                        dve.wait_ge(r_exp, l + 1)
                        then(nc.vector.reciprocal(one[l][:, 2:3], one[l][:, 1:2]))
                        then(nc.vector.tensor_scalar(t[:, 1, 0:E1], t[:, 0, 0:E1], one[l][:, 2:3], None, ALU.mult))
                        then(nc.vector.max(m8[l][:, :], t[:, 1, 0:E1]))
                        then(nc.vector.max_index(i8[l][:, :], m8[l][:, :], t[:, 1, 0:E1]))
                        then(nc.vector.tensor_copy(i8f[l][:, :], i8[l][:, :]))
                        for s in range(2):
                            nc.vector.tensor_scalar(t[:, 2 + s, 0:E1], iota[:, 0:E1], i8f[l][:, s:s + 1], LORA_SCALE, ALU.is_equal, ALU.mult)
                            v = nc.vector.tensor_scalar(t[:, 4 + s, 0:E1], iota[:, 0:E1], i8f[l][:, s:s + 1], m8[l][:, s:s + 1], ALU.is_equal, ALU.mult)
                        then(v)
                        nc.vector.tensor_copy(rm[l][:, 0:2, :].rearrange("p s (e r) -> p s e r", r=R1),
                                              t[:, 2:4, 0:E1].unsqueeze(3).broadcast_to([P, 2, E1, R1]))
                        nc.vector.tensor_scalar(rm[l][:, 2:4, :].rearrange("p s (e r) -> p s e r", r=R1),
                                                t[:, 4:6, 0:E1].unsqueeze(3).broadcast_to([P, 2, E1, R1]), LORA_SCALE, None,
                                                ALU.mult).then_inc(rm_sb, 1)
                    for l in LN:
                        dve.wait_ge(rmT_sb, l + 1)
                        dve.wait_ge(xa_ps, l + 1)
                        for m in range(2):
                            v = nc.vector.tensor_tensor(xam[l][:, m, :, :], ps[l][2][:, m * P:(m + 1) * P].unsqueeze(1).broadcast_to([P, 2, P]),
                                                        rmT[l][:, 0:2, :], ALU.mult)
                        v.then_inc(xam_sb, 1)
                    for f in range(FC):
                        for l in LN:
                            w = ffc(f)
                            dve.wait_ge(base_sb, LANES * f + l + 1)
                            dve.wait_ge(lora_ps, LANES * f + l + 1)
                            for m, t3 in enumerate((g3(l, f), u3(l, f))):
                                v = nc.vector.tensor_tensor(t3[:, 1:3, :], ps[l][2 * (f % 2) + 1][0:w, m * 2 * P:(m + 1) * 2 * P].rearrange("p (s t) -> p s t", s=2),
                                                            t3[:, 0:1, :].broadcast_to([w, 2, P]), ALU.add)
                            v.then_inc(lora_sb, 1)
                    for l in LN:
                        dve.wait_ge(ha_ps, l + 1)
                        nc.vector.tensor_tensor(kT[l][:, :, :], ps[l][1][:, 0:2 * P].rearrange("p (s t) -> p s t", s=2), rmT[l][:, 2:4, :],
                                                ALU.mult).then_inc(zz_sb, 1)
                    for l in LN:
                        dve.wait_ge(proj_ps, nth(3, l))
                        then(nc.vector.tensor_tensor(y[l][:, :], ps[l][0][:, 0:D], xs[l][:, :], ALU.add))
                    norm(5)

            nc.all_engine_barrier(sems_to_clear=range(min(cleared), max(cleared) + 1))


def _laid_out(i):
    import numpy as np

    def rows(v):
        return np.broadcast_to(v, (P, v.shape[-1]))

    a = {k: np.asarray(v) for k, v in i.items()}
    const = np.zeros((P, NCONST), np.float32)
    const[:, C_ID:C_ID + P] = np.eye(P)
    const[:, C_MASK:C_MASK + BANK] = np.tile(np.where(np.arange(P)[None, :] > np.arange(P)[:, None], -1e30, 0.0), (1, 4))
    const[:, C_IOTA:C_IOTA + 16] = np.arange(16)
    const[0:64, C_BLK:C_BLK + HA] = 1.0
    const[64:P, C_BLK + HA:C_BLK + 2 * HA] = 1.0
    const[:, C_PAR] = (np.arange(P) // HD) % 2 == 0
    const[:, C_PAR + 1] = (np.arange(P) // HD) % 2 == 1
    feat = np.zeros((2, P, P), np.float32)
    for w, name in enumerate(("L1_xattn_Wqf", "L1_xattn_Wkf")):
        for j in range(4):
            for s in range(2):
                feat[w, 32 * j + 16 * s:32 * j + 16 * s + 16, 64 * s:64 * s + 64] = a[name].T
    bqkv = a["L0_attn_b_qkv"]
    return {
        "x": a["x"],
        "ctx": a["ctx_2048"],
        "mask": a["mask_BxS2_ff1"].reshape(16, P, 1),
        "const": const,
        "w_qkv0": a["L0_attn_w_qkv"].T,
        "b_qk0": bqkv[0:2 * D].reshape(4, P).T,
        "b_v0": rows(bqkv[2 * D:]),
        "w_o0": a["L0_attn_w_out"].T,
        "b_o0": rows(a["L0_attn_b_out"]),
        "sim": a["L0_ffn_sim_matrix"],
        "gates": rows(a["L0_ffn_gates"]),
        "moe_qkv": np.concatenate([a[f"L0_ffn_{n}_proj"].transpose(1, 0, 2) for n in "qkv"], axis=2),
        "moe_o": a["L0_ffn_o_proj"],
        "w_qk1": np.concatenate([a["L1_attn_Wq"], np.repeat(a["L1_attn_Wk"].reshape(D, 4, HD), 4, axis=1).reshape(D, D)], axis=1),
        "w_v1": a["L1_attn_Wv"],
        "w_o1": a["L1_attn_Wo"],
        "x_qk": np.concatenate([a["L1_xattn_Wq"].T, a["L1_xattn_Wk"].T], axis=1),
        "x_v": a["L1_xattn_Wv"].T,
        "x_o": a["L1_xattn_Wo"].T,
        "x_bqk": np.concatenate([a["L1_xattn_bq"], a["L1_xattn_bk"]]).reshape(4, P).T,
        "x_bv": rows(a["L1_xattn_bv"]),
        "x_bo": rows(a["L1_xattn_bo"]),
        "x_f": feat,
        "f_gu": np.concatenate([a["L1_ffn_Wg"].T, a["L1_ffn_Wu"].T], axis=1),
        "f_d": a["L1_ffn_Wd"].T,
        "f_r": a["L1_ffn_Wr"].T,
        "f_a": np.concatenate([a["L1_ffn_Ag"].reshape(P, D).T, a["L1_ffn_Au"].reshape(P, D).T], axis=1),
        "f_b": np.concatenate([a[f"L1_ffn_B{n}"].transpose(0, 2, 1).reshape(P, DFF) for n in "gu"], axis=1),
        "f_ad": a["L1_ffn_Ad"].reshape(P, DFF).T,
        "f_bd": a["L1_ffn_Bd"].transpose(0, 2, 1).reshape(P, D),
    }


def kernel(**inputs):
    import numpy as _np
    import concourse.bacc as _bacc
    from concourse import mybir as _mybir
    from concourse.bass_utils import run_bass_kernel_spmd as _run

    nc = _bacc.Bacc("TRN2", target_bir_lowering=False, num_devices=1)
    arrays, args = {}, []
    for name, a in _laid_out(inputs).items():
        a = _np.ascontiguousarray(a)
        arrays[f"in_{name}"] = a
        args.append(nc.dram_tensor(f"in_{name}", a.shape, _mybir.dt.from_np(a.dtype), kind="ExternalInput").ap())
    args.append(nc.dram_tensor("out_0", (16, P, D), _mybir.dt.float32, kind="ExternalOutput").ap())
    decoder(nc, *args)
    r = _run(nc, [arrays], core_ids=[0])
    return r.results[0]["out_0"]
```

```python
from contextlib import ExitStack

import concourse.bass as bass
from concourse import mybir

ALU = mybir.AluOpType
ACT = mybir.ActivationFunctionType
AX = mybir.AxisListType
F32 = mybir.dt.float32
BF16 = mybir.dt.bfloat16
U32 = mybir.dt.uint32

P = 128
D = 256
KC = D // P
SEQS = 16
LOOP = SEQS - 3
NH, HD = 16, 16
HA = HD + 1
HW = 32
E0, H0 = 16, 128
DFF, E1, R1 = 704, 8, 16
FC = -(-DFF // P)
BANKS = 4
BANK = 512
LN_EPS = 1e-5
LORA_SCALE = 2.0
C_ID, C_IOTA, C_BLK, C_PAR = 0, 128, 144, 178
NCONST = 180

ORDER = """
F n4 | F m4 | A xT0 | A qkv0 | F xT | A sc0 | B n2 | F b0 | F r | F rt | A pT0 | F b1 | A pv0 | F b2 | A tr0
F rT | F b3 | B m2 | A oT0 | A vc | F b4 | A pj0 | F b5 | A n0 | F l0 | F l1 | A cT | A m0 | F s0 | F l2 | F s1
F l3 | A xT1 | F s2 | F l4 | F s3 | F s4 | F l5 | F s5 | A sc1 | F d0 | F d1 | A pT1 | A pv1 | F d2 | A tr1
A n1 | F d3 | F d4 | F d5 | F z | A m1 | A xT2 | F zz | F pj | A sq | F n5 | A lg | A rt | A e0 | A e1 | B xT3
A e2 | A e3 | B qkv3 | A e4 | A e5 | B sc3 | A e6 | A e7 | B pT3 | A e8 | B pv3 | A e9 | A e10 | B tr3 | A e11
A e12 | B oT3 | A e13 | A e14 | A e15 | B cT | B pj3 | B n3 | A qkT | B cv | A s | B ck | B m3 | A rs | A pT2
B xb | B vm | B xT4 | A ao | B q4 | A w0 | B ft | A w1 | A w2 | B kv | A w3 | F m5 | A w4 | B nm | A w5 | A w6
B oT4 | A w7 | B pj4
""".replace("\n", "|").split("|")
ORDER = [step.strip() for step in ORDER if step.strip()]


class Stage:
    pass


def decoder(nc, x, ctx_in, mask_in, const, causal, w_qkv0, b_qk0, b_v0, w_o0, b_o0, sim, gates, moe_qkv, moe_o,
            w_qk1, w_v1, w_o1, x_qk, x_v, x_o, x_bqk, x_bv, x_bo, x_f, f_gu, f_d, f_r, f_a, f_b, f_ad, f_bd, out):
    with ExitStack() as es:
        def sb(name, shape, dt=F32):
            return es.enter_context(nc.sbuf_tensor(name, shape, dt))

        def sem(name):
            return es.enter_context(nc.semaphore(name))

        cst = sb("cst", [P, NCONST])
        ident = cst[:, C_ID:C_ID + P]
        iota = cst[:, C_IOTA:C_IOTA + 16]
        block_mask = cst[:, C_BLK:C_BLK + 2 * HA]
        even, odd = cst[:, C_PAR:C_PAR + 1], cst[:, C_PAR + 1:C_PAR + 2]
        ident_b = sb("ident_b", [P, P], BF16)
        mask_b = sb("mask_b", [P, BANK], BF16)
        ones = sb("ones", [P, P])
        neg_half = sb("neg_half", [P, 1])
        eps = sb("eps", [P, 1])
        wqkv0 = sb("wqkv0", [P, KC, 3 * D])
        bqk0 = sb("bqk0", [P, 4])
        bq0_eo = sb("bq0_eo", [P, 2, KC])
        bv0 = sb("bv0", [P, D])
        wo0 = sb("wo0", [P, KC, D])
        bo0 = sb("bo0", [P, D])
        simn = sb("simn", [P, KC, E0])
        simsq = sb("simsq", [P, KC, E0])
        simr = sb("simr", [P, E0])
        neg_half16 = sb("neg_half16", [P, E0])
        sig = sb("sig", [P, E0])
        wmoe = sb("wmoe", [P, KC, E0, 3 * H0])
        wmo = sb("wmo", [P, E0, D])
        wqk1 = sb("wqk1", [P, KC, 2 * D])
        wv1 = sb("wv1", [P, KC, 64])
        wo1 = sb("wo1", [P, KC, D])
        xqk = sb("xqk", [P, KC, 2 * D])
        xv = sb("xv", [P, KC, D])
        xo = sb("xo", [P, KC, D])
        xbqk = sb("xbqk", [P, 4])
        xbv = sb("xbv", [P, D])
        xbo = sb("xbo", [P, D])
        xf = sb("xf", [P, 2, P])
        wgu = sb("wgu", [P, KC, 2 * DFF])
        wd = sb("wd", [P, FC, D])
        wr = sb("wr", [P, KC, E1])
        wa = sb("wa", [P, KC, 2 * P])
        wb = sb("wb", [P, 2 * DFF])
        wad = sb("wad", [P, FC, P])
        wbd = sb("wbd", [P, D])

        w_c, w_x0, w_a0, w_m, w_mo, w_a1, w_x, w_f = [sem(f"w_{n}") for n in ("const", "x0", "attn0", "moe", "moe_o", "attn1", "xattn1", "ffn")]
        pre_dve, pre_pe, pre_act, pre_pool = [sem(f"pre_{n}") for n in ("dve", "pe", "act", "pool")]
        cleared = []

        def counts(stage, names):
            new = [sem(f"{stage}_{n}") for n in names.split()]
            cleared.extend(s.num for s in new)
            return new

        A, B, F = Stage(), Stage(), Stage()
        A.ps, B.ps = [[es.enter_context(nc.psum_tensor(f"ps_{s}{n}", [P, BANK], F32)) for n in range(BANKS)] for s in "ab"]
        F.ps = B.ps

        for S, s in ((A, "a"), (B, "b"), (F, "f")):
            S.stats, S.mv, S.ve, S.rstd = sb(f"{s}_stats", [P, 6]), sb(f"{s}_mv", [P, 2]), sb(f"{s}_ve", [P, 1]), sb(f"{s}_rstd", [P, 1])
            S.x, S.xT = sb(f"{s}_x", [P, D]), sb(f"{s}_xT", [P, KC, P])
            S.ln_var, S.ln_rstd, S.x_ready, S.xT_ps, S.xT_sb = counts(s, "ln_var ln_rstd x_ready xT_ps xT_sb")

        for S, s in ((A, "a"), (F, "f")):
            S.sm, S.one = sb(f"{s}_sm", [P, 8, 16]), sb(f"{s}_one", [P, 4])
            S.m8, S.i8, S.i8f = sb(f"{s}_m8", [P, 8]), sb(f"{s}_i8", [P, 8], U32), sb(f"{s}_i8f", [P, 8])

        for S, s in ((A, "a"), (B, "b")):
            S.xb = sb(f"{s}_xb", [P, D])
            S.cx, S.cxT = sb(f"{s}_cx", [P, D]), sb(f"{s}_cxT", [P, KC, P])
            S.qe = sb(f"{s}_qe", [P, KC, P])
            S.qo = sb(f"{s}_qo", [P, KC, P])
            S.kT = sb(f"{s}_kT", [P, KC, P])
            S.probs = sb(f"{s}_probs", [P, BANKS, BANK])
            S.rmax, S.rsum = sb(f"{s}_rmax", [P, NH]), sb(f"{s}_rsum", [P, NH])
            S.onat, S.oT = sb(f"{s}_onat", [P, D]), sb(f"{s}_oT", [P, KC, P])
            S.ctx_ld, S.xb_sb = counts(s, "ctx_ld xb_sb")
            S.q_ps, S.k_ps, S.v_ps, S.q_sb, S.k_sb, S.v_sb, S.cT_ps = counts(s, "q_ps k_ps v_ps q_sb k_sb v_sb cT_ps")
            S.score_ps, S.shifted, S.prob, S.probT_ps, S.probT_sb = counts(s, "score_ps shifted prob probT_ps probT_sb")
            S.pvT_ps, S.pvT_sb, S.pv_ps, S.o_sb, S.oT_ps, S.oT_sb, S.proj_ps = counts(s, "pvT_ps pvT_sb pv_ps o_sb oT_ps oT_sb proj_ps")

        A.xin, A.y, A.yout = sb("a_xin", [P, D]), sb("a_y", [P, D]), sb("a_yout", [P, D])
        A.va, A.vc = sb("a_va", [P, NH, HW]), sb("a_vc", [P, NH, HW])
        A.ss, A.ssc, A.rn = sb("a_ss", [P, 1]), sb("a_ssc", [P, 1]), sb("a_rn", [P, 1])
        A.qkv = sb("a_qkv", [P, 3 * H0])
        A.x_ld, A.vc_sb, A.sq_sum, A.sq_rn, A.lg_ps, A.lg_read = counts("a", "x_ld vc_sb sq_sum sq_rn lg_ps lg_read")
        A.gate_in, A.gate_exp, A.moe_ps, A.moe_acc, A.qkT_ps, A.qkT_sb = counts("a", "gate_in gate_exp moe_ps moe_acc qkT_ps qkT_sb")
        A.s_ps, A.s_bias, A.s_exp, A.pT1_ps, A.pT1_sb = counts("a", "s_ps s_bias s_exp pT1_ps pT1_sb")
        A.ao_ps, A.ao_sb, A.mo_ps, A.mo_acc = counts("a", "ao_ps ao_sb mo_ps mo_acc")

        B.y3, B.y, B.tokmask = sb("b_y3", [P, D]), sb("b_y", [P, D]), sb("b_tokmask", [P, 1])
        B.va = sb("b_va", [P, 4, HW])
        B.vx, B.vm = sb("b_vx", [P, NH, HA]), sb("b_vm", [P, NH, HA])
        B.kvb = sb("b_kvb", [P, NH // 2, 2 * HA])
        B.cT_sb, B.mask_ld, B.v_masked, B.feat_ps, B.feat_act, B.feat_dve = counts("b", "cT_sb mask_ld v_masked feat_ps feat_act feat_dve")
        B.kv_ps, B.kv_sb, B.num_ps = counts("b", "kv_ps kv_sb num_ps")

        F.y, F.res = sb("f_y", [P, D]), sb("f_res", [P, D])
        F.gu = sb("f_gu", [P, 2 * FC * 3 * P])
        F.rm, F.rmT = sb("f_rm", [P, 4, E1 * R1]), sb("f_rmT", [P, 4, P])
        F.zz = sb("f_zz", [P, 2, P])
        F.r_ps, F.xa_ps, F.r_in, F.r_exp, F.rm_sb, F.rmT_ps, F.rmT_sb = counts("f", "r_ps xa_ps r_in r_exp rm_sb rmT_ps rmT_sb")
        F.xam_sb, F.base_ps, F.base_sb, F.lora_ps, F.lora_sb = counts("f", "xam_sb base_ps base_sb lora_ps lora_sb")
        F.silu_sb, F.h_sb, F.ha_ps, F.zz_sb, F.proj_ps, F.stored = counts("f", "silu_sb h_sb ha_ps zz_sb proj_ps stored")
        dve_done, pool_done = counts("own", "dve pool")
        assert max(cleared) - min(cleared) == len(cleared) - 1

        fq = B.probs[:, 0:2, :].rearrange("p b (j n) -> p (b j) n", j=2)
        fk = B.probs[:, 2:4, :].rearrange("p b (j n) -> p (b j) n", j=2)
        xam = F.rm[:, :, :].rearrange("p (m s) n -> p m s n", m=2)
        mask_f = F.gu[:, 0:BANK]

        def ffc(f):
            return min(P, DFF - f * P)

        def g3(f):
            return F.gu[0:ffc(f), f * 3 * P:(f + 1) * 3 * P].rearrange("p (v t) -> p v t", v=3)

        def u3(f):
            o = (FC + f) * 3 * P
            return F.gu[0:ffc(f), o:o + 3 * P].rearrange("p (v t) -> p v t", v=3)

        def load_late_weights(sp):
            def load(dst, src, s):
                sp.dma_start(dst, src).then_inc(s, 16)

            moe_v = moe_qkv.rearrange("(c p) e n -> p c e n", p=P)
            for c in range(KC):
                load(wmoe[:, c, :, :], moe_v[:, c, :, :], w_m)
            load(wmo[:, :, :], moe_o.rearrange("e h c -> h e c"), w_mo)
            load(wqk1[:, :, :], w_qk1.rearrange("(c p) n -> p c n", p=P), w_a1)
            load(wv1[:, :, :], w_v1.rearrange("(c p) n -> p c n", p=P), w_a1)
            load(wo1[:, :, :], w_o1.rearrange("(c p) n -> p c n", p=P), w_a1)
            load(xqk[:, :, :], x_qk.rearrange("(c p) n -> p c n", p=P), w_x)
            load(xv[:, :, :], x_v.rearrange("(c p) n -> p c n", p=P), w_x)
            load(xo[:, :, :], x_o.rearrange("(c p) n -> p c n", p=P), w_x)
            load(xbqk[:, :], x_bqk, w_x)
            load(xbv[:, :], x_bv, w_x)
            load(xbo[:, :], x_bo, w_x)
            load(xf[:, :, :], x_f.rearrange("w p n -> p w n"), w_x)
            load(wgu[:, :, :], f_gu.rearrange("(c p) n -> p c n", p=P), w_f)
            load(wd[:, 0:FC - 1, :], f_d[0:(FC - 1) * P, :].rearrange("(c p) n -> p c n", p=P), w_f)
            load(wd[0:ffc(FC - 1), FC - 1, :], f_d[(FC - 1) * P:DFF, :], w_f)
            load(wr[:, :, :], f_r.rearrange("(c p) n -> p c n", p=P), w_f)
            load(wa[:, :, :], f_a.rearrange("(c p) n -> p c n", p=P), w_f)
            load(wb[:, :], f_b, w_f)
            load(wad[:, 0:FC - 1, :], f_ad[0:(FC - 1) * P, :].rearrange("(c p) n -> p c n", p=P), w_f)
            load(wad[0:ffc(FC - 1), FC - 1, :], f_ad[(FC - 1) * P:DFF, :], w_f)
            load(wbd[:, :], f_bd, w_f)

        with nc.Block() as pre:
            @pre.sync
            def _(sp):
                def load(dst, src, s):
                    sp.dma_start(dst, src).then_inc(s, 16)

                load(cst[:, :], const, w_c)
                load(mask_f, causal, w_c)
                load(simn[:, :, :], sim.rearrange("(c p) e -> p c e", p=P), w_c)
                load(sig[:, :], gates, w_c)
                load(bqk0[:, :], b_qk0, w_c)
                load(A.xin[:, :], x[0:1, :, :].rearrange("a p c -> (a p) c"), w_x0)
                load(wqkv0[:, :, :], w_qkv0.rearrange("(c p) n -> p c n", p=P), w_a0)
                load(bv0[:, :], b_v0, w_a0)
                load(wo0[:, :, :], w_o0.rearrange("(c p) n -> p c n", p=P), w_a0)
                load(bo0[:, :], b_o0, w_a0)
                sp.wait_ge(w_x0, 16)

            @pre.vector
            def _(dve):
                nc.vector.memset(ones[:, :], 1.0).then_inc(pre_dve, 1)
                nc.vector.memset(neg_half[:, :], -0.5)
                nc.vector.memset(neg_half16[:, :], -0.5)
                nc.vector.memset(eps[:, :], LN_EPS)
                for v in (A.va, A.vc, B.va, B.vx):
                    nc.vector.memset(v[:, :, :], 1.0)
                dve.wait_ge(w_c, 16 * 5)
                nc.vector.tensor_copy(ident_b[:, :], ident)
                nc.vector.tensor_copy(mask_b[:, :], mask_f)
                nc.vector.tensor_scalar(bq0_eo[:, 0, :], bqk0[:, 0:KC], even, None, ALU.mult)
                nc.vector.tensor_scalar(bq0_eo[:, 1, :], bqk0[:, 0:KC], odd, None, ALU.mult)
                nc.vector.tensor_tensor(simsq[:, :, :], simn[:, :, :], simn[:, :, :], ALU.mult).then_inc(pre_dve, 1)
                dve.wait_ge(pre_act, 1)
                nc.vector.tensor_scalar(sig[:, :], sig[:, :], 1.0, None, ALU.add).then_inc(pre_dve, 1)
                dve.wait_ge(pre_dve, 3)
                nc.vector.reciprocal(sig[:, :], sig[:, :])
                dve.wait_ge(pre_pe, 1)
                nc.vector.tensor_scalar(simr[:, :], A.ps[0][:, 0:E0], 1e-24, None, ALU.max).then_inc(pre_dve, 1)
                dve.wait_ge(pre_pool, 1)
                nc.vector.tensor_tensor(simn[:, :, :], simn[:, :, :],
                                        simr[:, :].unsqueeze(1).broadcast_to([P, KC, E0]), ALU.mult).then_inc(pre_dve, 1)

            @pre.scalar
            def _(act):
                act.wait_ge(w_c, 16 * 5)
                nc.scalar.activation(sig[:, :], sig[:, :], ACT.Exp, scale=-1.0).then_inc(pre_act, 1)

            @pre.tensor
            def _(pe):
                pe.wait_ge(pre_dve, 2)
                for c in range(KC):
                    mm = nc.tensor.matmul(A.ps[0][:, 0:E0], ones[:, :], simsq[:, c, :], start=(c == 0), stop=(c == KC - 1))
                mm.then_inc(pre_pe, 1)

            @pre.gpsimd
            def _(pool):
                pool.wait_ge(pre_dve, 4)
                nc.gpsimd.tensor_tensor(simr[:, :], simr[:, :], neg_half16[:, :], ALU.pow).then_inc(pre_pool, 1)

        def seq(t, i, off, it):
            if it is None:
                return t[i + off:i + off + 1, :, :].rearrange("a p c -> (a p) c")
            return t[i + off:i + off + LOOP, :, :][bass.ds(it, 1), :, :].rearrange("a p c -> (a p) c")

        def body(i, it, stages):
            order = [step for step in ORDER if step[0] in stages]
            with nc.Block(no_gpsimd_drain=True) as block:

                @block.sync
                def _(sp):
                    if "A" in stages:
                        sp.dma_start(A.cx[:, :], seq(ctx_in, i, 0, it)).then_inc(A.ctx_ld, 16)
                    if "B" in stages:
                        sp.dma_start(B.cx[:, :], seq(ctx_in, i, -1, it)).then_inc(B.ctx_ld, 16)
                        sp.dma_start(B.tokmask[:, :], seq(mask_in, i, -1, it)).then_inc(B.mask_ld, 16)
                    if i == 0:
                        load_late_weights(sp)
                    if "F" in stages:
                        sp.wait_ge(F.x_ready, 2)
                        sp.dma_start(seq(out, i, -2, it), F.res[:, :]).then_inc(F.stored, 16)
                    if "A" in stages and i < SEQS - 1:
                        sp.wait_ge(A.xT_ps, 1)
                        sp.wait_ge(A.xb_sb, 1)
                        sp.dma_start(A.xin[:, :], seq(x, i, 1, it)).then_inc(A.x_ld, 16)
                        sp.wait_ge(A.x_ld, 16)
                    if "F" in stages:
                        sp.wait_ge(F.stored, 16)

                @block.tensor
                def _(pe):
                    def x_transposed(S, src, n, ready=True):
                        if ready:
                            pe.wait_ge(S.x_ready, n)
                        for c in range(KC):
                            mm = nc.tensor.transpose(S.ps[0][:, c * P:(c + 1) * P], src[:, c * P:(c + 1) * P], ident)
                        mm.then_inc(S.xT_ps, 1)

                    def rows_projected(S, b, w, o, src, done):
                        for m in range(KC):
                            for c in range(KC):
                                mm = nc.tensor.matmul(S.ps[b][:, m * P:(m + 1) * P], w[:, c, o + m * P:o + (m + 1) * P],
                                                      src[:, c, :], start=(c == 0), stop=(c == KC - 1))
                        mm.then_inc(done, 1)

                    def v_projected(S, w, n, src):
                        for c in range(KC):
                            mm = nc.tensor.matmul(S.ps[3][:, 0:n], src[:, c, :], w(c), start=(c == 0), stop=(c == KC - 1))
                        mm.then_inc(S.v_ps, 1)

                    def scores(S, k, kt):
                        pe.wait_ge(S.q_sb, k + 1)
                        pe.wait_ge(S.k_sb, k + 1)
                        pe.wait_ge(S.v_sb, 1)
                        for j in range(BANKS):
                            nc.tensor.matmul(S.ps[j][:, :], ident_b[:, :], mask_b[:, :], start=True, stop=False,
                                             skip_group_check=True)
                            for c in range(KC):
                                for par, q in enumerate((S.qe, S.qo)):
                                    r = slice(32 * j, 32 * j + 32)
                                    o = (2 * c + par) * P
                                    mm = nc.tensor.matmul(S.ps[j][:, o:o + P], q[r, c, :], kt[r, c, :],
                                                          start=False, stop=(c == KC - 1 and par == 1),
                                                          tile_position=(32 * j, 0), skip_group_check=True)
                            mm.then_inc(S.score_ps, 1)

                    def probs_transposed(S, k):
                        for j in range(BANKS):
                            pe.wait_ge(S.prob, BANKS * k + j + 1)
                            for h in range(4):
                                mm = nc.tensor.transpose(S.ps[j][:, h * P:(h + 1) * P], S.probs[:, j, h * P:(h + 1) * P], ident)
                            mm.then_inc(S.probT_ps, 1)

                    def values_summed(S, k, v, group):
                        if k == 1:
                            pe.wait_ge(A.vc_sb, 1)
                        for j in range(BANKS):
                            pe.wait_ge(S.probT_sb, BANKS * k + j + 1)
                            for c in range(KC):
                                for par in range(2):
                                    h = 8 * c + 2 * j + par
                                    o = (2 * c + par) * P
                                    r = 32 * (h % 4)
                                    mm = nc.tensor.matmul(S.ps[0][r:r + 32, h // 4 * P:(h // 4 + 1) * P], v[:, h // group, :],
                                                          S.probs[:, j, o:o + P], start=True, stop=True,
                                                          tile_position=(0, r), skip_group_check=True)
                        mm.then_inc(S.pvT_ps, 1)

                    def sums_transposed(S, k):
                        pe.wait_ge(S.pvT_sb, k + 1)
                        for g in range(4):
                            mm = nc.tensor.transpose(S.ps[1][:, g * P:(g + 1) * P], S.probs[:, 0, g * P:(g + 1) * P], ident)
                        mm.then_inc(S.pv_ps, 1)

                    def ctx_transposed(S, k):
                        pe.wait_ge(S.ctx_ld, 16)
                        pe.wait_ge(S.probT_sb, BANKS * (k + 1))
                        for c in range(KC):
                            mm = nc.tensor.transpose(S.ps[3][:, c * P:(c + 1) * P], S.cx[:, c * P:(c + 1) * P], ident)
                        mm.then_inc(S.cT_ps, 1)

                    def out_transposed(S, k):
                        pe.wait_ge(S.o_sb, k + 1)
                        for c in range(KC):
                            mm = nc.tensor.transpose(S.ps[1][:, c * P:(c + 1) * P], S.onat[:, c * P:(c + 1) * P], ident)
                        mm.then_inc(S.oT_ps, 1)

                    def out_projected(S, k, w):
                        pe.wait_ge(S.oT_sb, k + 1)
                        for c in range(KC):
                            mm = nc.tensor.matmul(S.ps[0][:, 0:D], S.oT[:, c, :], w[:, c, :], start=(c == 0), stop=(c == KC - 1))
                        mm.then_inc(S.proj_ps, 1)

                    def a_qkv():
                        pe.wait_ge(w_a0, 64)
                        pe.wait_ge(A.xT_sb, 1)
                        rows_projected(A, 1, wqkv0, 0, A.xT, A.q_ps)
                        rows_projected(A, 2, wqkv0, D, A.xT, A.k_ps)
                        v_projected(A, lambda c: wqkv0[:, c, 2 * D:3 * D], D, A.xT)

                    def a_logits():
                        pe.wait_ge(A.xT_sb, 2)
                        for c in range(KC):
                            mm = nc.tensor.matmul(A.ps[1][:, 0:E0], A.xT[:, c, :], simn[:, c, :], start=(c == 0), stop=(c == KC - 1))
                        mm.then_inc(A.lg_ps, 1)

                    def a_expert(e):
                        if e == 0:
                            pe.wait_ge(w_m, 32)
                        if e == 3:
                            pe.wait_ge(A.lg_read, 1)
                        if e >= BANKS:
                            pe.wait_ge(A.moe_acc, e - BANKS + 1)
                        for c in range(KC):
                            mm = nc.tensor.matmul(A.ps[(e + 2) % BANKS][:, 0:3 * H0], A.xT[:, c, :], wmoe[:, c, e, :],
                                                  start=(c == 0), stop=(c == KC - 1))
                        mm.then_inc(A.moe_ps, 1)

                    def a_qk_transposed():
                        pe.wait_ge(A.moe_acc, E0)
                        for n in range(2):
                            mm = nc.tensor.transpose(A.ps[0][:, n * P:(n + 1) * P], A.qkv[:, n * P:(n + 1) * P], ident)
                        mm.then_inc(A.qkT_ps, 1)

                    def a_scores():
                        pe.wait_ge(A.qkT_sb, 1)
                        nc.tensor.matmul(A.ps[1][:, 0:P], ident_b[:, :], mask_b[:, 0:P], start=True, stop=False)
                        nc.tensor.matmul(A.ps[1][:, 0:P], A.qe[:, 0, :], A.qe[:, 1, :], start=False, stop=True).then_inc(A.s_ps, 1)

                    def a_prob_transposed():
                        pe.wait_ge(A.s_exp, 1)
                        nc.tensor.transpose(A.ps[2][:, 0:P], A.qo[:, 0, :], ident).then_inc(A.pT1_ps, 1)

                    def a_values():
                        pe.wait_ge(A.pT1_sb, 1)
                        nc.tensor.matmul(A.ps[3][:, 0:P], A.qkv[:, 2 * P:3 * P], A.qo[:, 1, :], start=True, stop=True).then_inc(A.ao_ps, 1)

                    def a_expert_out(n):
                        if n == 0:
                            pe.wait_ge(w_mo, 16)
                            pe.wait_ge(A.ao_sb, 1)
                        if n >= BANKS:
                            pe.wait_ge(A.mo_acc, 2 * (n - BANKS + 1))
                        nc.tensor.matmul(A.ps[n % BANKS][:, :], A.kT[:, 0, :], wmo[:, 2 * n:2 * n + 2, :], start=True,
                                         stop=True).then_inc(A.mo_ps, 1)

                    def b_qkv():
                        pe.wait_ge(w_a1, 48)
                        pe.wait_ge(B.xT_sb, 1)
                        rows_projected(B, 1, wqk1, 0, B.xT, B.q_ps)
                        rows_projected(B, 2, wqk1, D, B.xT, B.k_ps)
                        v_projected(B, lambda c: wv1[:, c, :], 64, B.xT)

                    def b_x_transposed():
                        if "F" in stages:
                            pe.wait_ge(F.ln_var, 2)
                        x_transposed(B, B.x, 1)

                    def b_ctx_k():
                        pe.wait_ge(w_x, 16 * 7)
                        pe.wait_ge(B.cT_sb, 1)
                        pe.wait_ge(B.probT_sb, BANKS)
                        rows_projected(B, 2, xqk, D, B.cxT, B.k_ps)

                    def b_ctx_v():
                        pe.wait_ge(w_x, 16 * 7)
                        pe.wait_ge(B.cT_sb, 1)
                        v_projected(B, lambda c: xv[:, c, :], D, B.cxT)

                    def b_q():
                        pe.wait_ge(B.xT_sb, 2)
                        rows_projected(B, 1, xqk, 0, B.xT, B.q_ps)

                    def b_features():
                        pe.wait_ge(B.q_sb, 2)
                        pe.wait_ge(B.k_sb, 2)
                        pe.wait_ge(B.v_sb, 2)
                        for j in range(BANKS):
                            for c in range(KC):
                                r = slice(32 * j, 32 * j + 32)
                                o = c * P
                                nc.tensor.matmul(B.ps[j][:, o:o + P], xf[r, 0, :], B.qe[r, c, :], start=True, stop=True,
                                                 tile_position=(32 * j, 0))
                                mm = nc.tensor.matmul(B.ps[j][:, 2 * P + o:2 * P + o + P], B.kT[r, c, :], xf[r, 1, :],
                                                      start=True, stop=True, tile_position=(32 * j, 0))
                            mm.then_inc(B.feat_ps, 1)

                    def b_kv():
                        pe.wait_ge(B.feat_act, 2)
                        pe.wait_ge(B.feat_dve, 2)
                        pe.wait_ge(B.v_masked, 1)
                        for m in range(NH // 2):
                            c, j = m // BANKS, m % BANKS
                            mm = nc.tensor.matmul(B.ps[0][:, 2 * HA * m:2 * HA * (m + 1)], fk[:, j, c * P:(c + 1) * P],
                                                  B.vm[:, 2 * m:2 * m + 2, :], start=True, stop=True)
                        mm.then_inc(B.kv_ps, 1)

                    def b_num():
                        pe.wait_ge(B.kv_sb, 1)
                        for m in range(NH // 2):
                            c, j = m // BANKS, m % BANKS
                            mm = nc.tensor.matmul(B.ps[0][:, 2 * HA * m:2 * HA * (m + 1)], fq[:, j, c * P:(c + 1) * P],
                                                  B.kvb[:, m, :], start=True, stop=True)
                        mm.then_inc(B.num_ps, 1)

                    def f_router():
                        pe.wait_ge(w_f, 16 * 9)
                        pe.wait_ge(F.xT_sb, 1)
                        for c in range(KC):
                            mm = nc.tensor.matmul(F.ps[1][:, 0:E1], F.xT[:, c, :], wr[:, c, :], start=(c == 0), stop=(c == KC - 1))
                        mm.then_inc(F.r_ps, 1)
                        for m in range(2):
                            for c in range(KC):
                                mm = nc.tensor.matmul(F.ps[2][:, m * P:(m + 1) * P], wa[:, c, m * P:(m + 1) * P], F.xT[:, c, :],
                                                      start=(c == 0), stop=(c == KC - 1))
                        mm.then_inc(F.xa_ps, 1)

                    def f_ranks_transposed():
                        pe.wait_ge(F.rm_sb, 1)
                        for n in range(4):
                            mm = nc.tensor.transpose(F.ps[3][:, n * P:(n + 1) * P], F.rm[:, n, :], ident)
                        mm.then_inc(F.rmT_ps, 1)

                    def f_base(f):
                        if f == 0:
                            pe.wait_ge(w_f, 16 * 9)
                            pe.wait_ge(F.xT_sb, 1)
                        if f == 1:
                            pe.wait_ge(F.r_in, 1)
                        if f >= 2:
                            pe.wait_ge(F.base_sb, f - 1)
                        w = ffc(f)
                        for m in range(2):
                            for c in range(KC):
                                o = m * DFF + f * P
                                mm = nc.tensor.matmul(F.ps[f % 2][0:w, m * P:(m + 1) * P], wgu[:, c, o:o + w],
                                                      F.xT[:, c, :], start=(c == 0), stop=(c == KC - 1))
                        mm.then_inc(F.base_ps, 1)

                    def f_lora(f):
                        if f == 0:
                            pe.wait_ge(F.xam_sb, 1)
                        if f == 1:
                            pe.wait_ge(F.rmT_sb, 1)
                        if f >= 2:
                            pe.wait_ge(F.lora_sb, f - 1)
                        w = ffc(f)
                        for m in range(2):
                            o = m * DFF + f * P
                            mm = nc.tensor.matmul(F.ps[2 + f % 2][0:w, m * 2 * P:(m + 1) * 2 * P], wb[:, o:o + w],
                                                  xam[:, m, :, :], start=True, stop=True)
                        mm.then_inc(F.lora_ps, 1)

                    def f_down(f):
                        if f == 0:
                            pe.wait_ge(F.base_sb, FC)
                        pe.wait_ge(F.h_sb, f + 1)
                        w = ffc(f)
                        mm = nc.tensor.matmul(F.ps[1][:, 0:2 * P], wad[0:w, f, :], g3(f)[:, 1:3, :], start=(f == 0), stop=(f == FC - 1))
                        if f == FC - 1:
                            mm.then_inc(F.ha_ps, 1)
                        nc.tensor.matmul(F.ps[0][:, 0:D], g3(f)[:, 0, :], wd[0:w, f, :], start=(f == 0), stop=False)

                    def f_down_lora():
                        pe.wait_ge(F.zz_sb, 1)
                        for s in range(2):
                            mm = nc.tensor.matmul(F.ps[0][:, 0:D], F.zz[:, s, :], wbd[:, :], start=False, stop=(s == 1))
                        mm.then_inc(F.proj_ps, 1)

                    steps = {
                        "A xT0": lambda: x_transposed(A, A.xin, 0, ready=False),
                        "A qkv0": a_qkv,
                        "A sc0": lambda: scores(A, 0, A.kT),
                        "A pT0": lambda: probs_transposed(A, 0),
                        "A pv0": lambda: values_summed(A, 0, A.va, 1),
                        "A tr0": lambda: sums_transposed(A, 0),
                        "A cT": lambda: ctx_transposed(A, 0),
                        "A oT0": lambda: out_transposed(A, 0),
                        "A pj0": lambda: out_projected(A, 0, wo0),
                        "A xT1": lambda: x_transposed(A, A.x, 1),
                        "A sc1": lambda: scores(A, 1, A.cxT),
                        "A pT1": lambda: probs_transposed(A, 1),
                        "A pv1": lambda: values_summed(A, 1, A.vc, 1),
                        "A tr1": lambda: sums_transposed(A, 1),
                        "A xT2": lambda: x_transposed(A, A.x, 2),
                        "A lg": a_logits,
                        "A qkT": a_qk_transposed,
                        "A s": a_scores,
                        "A pT2": a_prob_transposed,
                        "A ao": a_values,
                        "B xT3": b_x_transposed,
                        "B qkv3": b_qkv,
                        "B sc3": lambda: scores(B, 0, B.kT),
                        "B pT3": lambda: probs_transposed(B, 0),
                        "B pv3": lambda: values_summed(B, 0, B.va, 4),
                        "B tr3": lambda: sums_transposed(B, 0),
                        "B cT": lambda: ctx_transposed(B, 0),
                        "B cv": b_ctx_v,
                        "B ck": b_ctx_k,
                        "B oT3": lambda: out_transposed(B, 0),
                        "B pj3": lambda: out_projected(B, 0, wo1),
                        "B xT4": lambda: x_transposed(B, B.x, 2),
                        "B q4": b_q,
                        "B ft": b_features,
                        "B kv": b_kv,
                        "B nm": b_num,
                        "B oT4": lambda: out_transposed(B, 1),
                        "B pj4": lambda: out_projected(B, 1, xo),
                        "F xT": lambda: x_transposed(F, F.x, 1),
                        "F r": f_router,
                        "F rT": f_ranks_transposed,
                        "F zz": f_down_lora,
                    }
                    for step in order:
                        if step in steps:
                            steps[step]()
                        elif step[:3] == "A e":
                            a_expert(int(step[3:]))
                        elif step[:3] == "A w":
                            a_expert_out(int(step[3:]))
                        elif step[:3] == "F b":
                            f_base(int(step[3:]))
                        elif step[:3] == "F l":
                            f_lora(int(step[3:]))
                        elif step[:3] == "F d":
                            f_down(int(step[3:]))

                @block.scalar
                def _(act):
                    def copied(dst, src, need, count, done):
                        act.wait_ge(need, count)
                        nc.scalar.activation(dst, src, ACT.Copy).then_inc(done, 1)

                    def two(S, b):
                        return S.ps[b][:, 0:D].rearrange("p (c n) -> p c n", c=KC)

                    def k_copied(S, k, bias):
                        act.wait_ge(S.k_ps, k + 1)
                        for c in range(KC):
                            a = nc.scalar.activation(S.kT[:, c, :], S.ps[2][:, c * P:(c + 1) * P], ACT.Identity, bias=bias[:, 2 + c:3 + c])
                        a.then_inc(S.k_sb, 1)

                    def exps(S, k):
                        for j in range(BANKS):
                            act.wait_ge(S.shifted, BANKS * k + j + 1)
                            nc.scalar.activation(S.probs[:, j, :], S.probs[:, j, :], ACT.Exp, scale=HD ** -0.5).then_inc(S.prob, 1)

                    def probsT(S, k):
                        for j in range(BANKS):
                            copied(S.probs[:, j, :], S.ps[j][:, :], S.probT_ps, BANKS * k + j + 1, S.probT_sb)

                    def b_qkv():
                        copied(B.kT[:, :, :], two(B, 2), B.k_ps, 1, B.k_sb)
                        copied(B.va[:, :, 0:HD], B.ps[3][:, 0:64].rearrange("p (h d) -> p h d", h=4), B.v_ps, 1, B.v_sb)

                    def b_features():
                        for j in (0, 1):
                            act.wait_ge(B.feat_ps, j + 1)
                            nc.scalar.activation(fq[:, j, :], B.ps[j][:, 0:2 * P], ACT.Relu)
                            nc.scalar.activation(fk[:, j, :], B.ps[j][:, 2 * P:4 * P], ACT.Relu).then_inc(B.feat_act, 1)

                    def a_squares():
                        act.wait_ge(A.x_ready, 2)
                        nc.scalar.activation(A.onat[:, :], A.x[:, :], ACT.Square, accum_out=A.ss[:, :]).then_inc(A.sq_sum, 1)

                    def a_gate_exp():
                        act.wait_ge(A.gate_in, 1)
                        nc.scalar.activation(A.sm[:, 2, :], A.sm[:, 1, :], ACT.Exp, bias=A.one[:, 0:1]).then_inc(A.gate_exp, 1)

                    def a_exp():
                        act.wait_ge(A.s_bias, 1)
                        nc.scalar.activation(A.qo[:, 0, :], A.ps[1][:, 0:P], ACT.Exp, bias=A.one[:, 1:2], scale=H0 ** -0.5,
                                             accum_out=A.one[:, 2:3]).then_inc(A.s_exp, 1)

                    def f_router_exp():
                        act.wait_ge(F.r_in, 1)
                        nc.scalar.activation(F.sm[:, 0, 0:E1], F.sm[:, 0, 0:E1], ACT.Exp, bias=F.one[:, 0:1],
                                             accum_out=F.one[:, 1:2]).then_inc(F.r_exp, 1)

                    def f_base(f):
                        act.wait_ge(F.base_ps, f + 1)
                        w = ffc(f)
                        nc.scalar.activation(g3(f)[:, 0, :], F.ps[f % 2][0:w, 0:P], ACT.Copy)
                        nc.scalar.activation(u3(f)[:, 0, :], F.ps[f % 2][0:w, P:2 * P], ACT.Copy).then_inc(F.base_sb, 1)

                    def f_silu(f):
                        act.wait_ge(F.lora_sb, f + 1)
                        nc.scalar.activation(g3(f), g3(f), ACT.Silu).then_inc(F.silu_sb, 1)

                    steps = {
                        "A xT0": lambda: copied(A.xT[:, :, :], two(A, 0), A.xT_ps, 1, A.xT_sb),
                        "A qkv0": lambda: k_copied(A, 0, bqk0),
                        "A sc0": lambda: exps(A, 0),
                        "A pT0": lambda: probsT(A, 0),
                        "A pv0": lambda: copied(A.probs[:, 0, :], A.ps[0][:, :], A.pvT_ps, 1, A.pvT_sb),
                        "A cT": lambda: copied(A.cxT[:, :, :], two(A, 3), A.cT_ps, 1, A.k_sb),
                        "A oT0": lambda: copied(A.oT[:, :, :], two(A, 1), A.oT_ps, 1, A.oT_sb),
                        "A sc1": lambda: exps(A, 1),
                        "A pT1": lambda: probsT(A, 1),
                        "A pv1": lambda: copied(A.probs[:, 0, :], A.ps[0][:, :], A.pvT_ps, 2, A.pvT_sb),
                        "A sq": a_squares,
                        "A xT2": lambda: copied(A.xT[:, :, :], two(A, 0), A.xT_ps, 3, A.xT_sb),
                        "A rt": a_gate_exp,
                        "A qkT": lambda: copied(A.qe[:, :, :], two(A, 0), A.qkT_ps, 1, A.qkT_sb),
                        "A s": a_exp,
                        "A pT2": lambda: copied(A.qo[:, 1, :], A.ps[2][:, 0:P], A.pT1_ps, 1, A.pT1_sb),
                        "A ao": lambda: copied(A.kT[:, 0, :], A.ps[3][:, 0:P], A.ao_ps, 1, A.ao_sb),
                        "B xT3": lambda: copied(B.xT[:, :, :], two(B, 0), B.xT_ps, 1, B.xT_sb),
                        "B qkv3": b_qkv,
                        "B sc3": lambda: exps(B, 0),
                        "B pT3": lambda: probsT(B, 0),
                        "B pv3": lambda: copied(B.probs[:, 0, :], B.ps[0][:, :], B.pvT_ps, 1, B.pvT_sb),
                        "B cT": lambda: copied(B.cxT[:, :, :], two(B, 3), B.cT_ps, 1, B.cT_sb),
                        "B ck": lambda: k_copied(B, 1, xbqk),
                        "B oT3": lambda: copied(B.oT[:, :, :], two(B, 1), B.oT_ps, 1, B.oT_sb),
                        "B xT4": lambda: copied(B.xT[:, :, :], two(B, 0), B.xT_ps, 2, B.xT_sb),
                        "B ft": b_features,
                        "B oT4": lambda: copied(B.oT[:, :, :], two(B, 1), B.oT_ps, 2, B.oT_sb),
                        "F xT": lambda: copied(F.xT[:, :, :], two(F, 0), F.xT_ps, 1, F.xT_sb),
                        "F rt": f_router_exp,
                        "F rT": lambda: copied(F.rmT[:, :, :], F.ps[3][:, :].rearrange("p (m n) -> p m n", m=4), F.rmT_ps, 1, F.rmT_sb),
                    }
                    for step in order:
                        if step in steps:
                            steps[step]()
                        elif step[:3] == "F b":
                            f_base(int(step[3:]))
                        elif step[:3] == "F s":
                            f_silu(int(step[3:]))

                @block.gpsimd
                def _(pool):
                    n = [0]

                    def then(ins):
                        n[0] += 1
                        ins.then_inc(pool_done, 1)
                        pool.wait_ge(pool_done, n[0])

                    def inverse_std(S, count):
                        pool.wait_ge(S.ln_var, count)
                        then(nc.gpsimd.tensor_tensor(S.ve[:, :], S.mv[:, 1:2], eps[:, :], ALU.add))
                        nc.gpsimd.tensor_tensor(S.rstd[:, :], S.ve[:, :], neg_half[:, :], ALU.pow).then_inc(S.ln_rstd, 1)

                    def a_x_biased():
                        pool.wait_ge(w_a0, 64)
                        nc.gpsimd.tensor_tensor(A.xb[:, :], A.xin[:, :], bo0[:, :], ALU.add).then_inc(A.xb_sb, 1)

                    def a_values():
                        pool.wait_ge(A.ctx_ld, 16)
                        nc.gpsimd.tensor_copy(A.vc[:, :, 0:HD], A.cx[:, :].rearrange("p (h d) -> p h d", h=NH)).then_inc(A.vc_sb, 1)

                    def a_inverse_norm():
                        pool.wait_ge(A.sq_sum, 1)
                        then(nc.gpsimd.tensor_scalar(A.ssc[:, :], A.ss[:, :], 1e-24, None, ALU.max))
                        nc.gpsimd.tensor_tensor(A.rn[:, :], A.ssc[:, :], neg_half[:, :], ALU.pow).then_inc(A.sq_rn, 1)

                    def b_x_biased():
                        pool.wait_ge(w_x, 16 * 7)
                        pool.wait_ge(B.x_ready, 2)
                        nc.gpsimd.tensor_tensor(B.xb[:, :], B.x[:, :], xbo[:, :], ALU.add).then_inc(B.xb_sb, 1)

                    def b_values_masked():
                        pool.wait_ge(B.mask_ld, 16)
                        pool.wait_ge(B.v_sb, 2)
                        nc.gpsimd.tensor_scalar(B.vm[:, :, :], B.vx[:, :, :], B.tokmask[:, 0:1], None, ALU.mult).then_inc(B.v_masked, 1)

                    def f_gated(f):
                        pool.wait_ge(F.silu_sb, f + 1)
                        nc.gpsimd.tensor_tensor(g3(f), g3(f), u3(f), ALU.mult).then_inc(F.h_sb, 1)

                    steps = {
                        "A xT0": a_x_biased,
                        "A vc": a_values,
                        "A n0": lambda: inverse_std(A, 1),
                        "A n1": lambda: inverse_std(A, 2),
                        "A sq": a_inverse_norm,
                        "B n2": lambda: inverse_std(B, 1),
                        "B n3": lambda: inverse_std(B, 2),
                        "B xb": b_x_biased,
                        "B vm": b_values_masked,
                        "F n4": lambda: inverse_std(F, 1),
                        "F n5": lambda: inverse_std(F, 2),
                    }
                    for step in order:
                        if step in steps:
                            steps[step]()
                        elif step[:3] == "F s":
                            f_gated(int(step[3:]))

                @block.vector
                def _(dve):
                    n = [0]

                    def then(ins):
                        n[0] += 1
                        ins.then_inc(dve_done, 1)
                        dve.wait_ge(dve_done, n[0])

                    def statistics(S, y):
                        then(nc.vector.bn_stats(S.stats[:, :], y[:, :]))
                        nc.vector.bn_aggr(S.mv[:, :], S.stats[:, :]).then_inc(S.ln_var, 1)

                    def normed(S, x_out, y, count):
                        dve.wait_ge(S.ln_rstd, count)
                        nc.vector.tensor_scalar(x_out[:, :], y[:, :], S.mv[:, 0:1], S.rstd[:, 0:1], ALU.subtract,
                                                ALU.mult).then_inc(S.x_ready, 1)

                    def q_split(S, src, need, count):
                        dve.wait_ge(need, count)
                        src = src[:, 0:D].rearrange("p (c n) -> p c n", c=KC)
                        nc.vector.tensor_scalar(S.qe[:, :, :], src, even, None, ALU.mult)
                        nc.vector.tensor_scalar(S.qo[:, :, :], src, odd, None, ALU.mult).then_inc(S.q_sb, 1)

                    def v_biased(S, k, dst, bias):
                        dve.wait_ge(S.v_ps, k + 1)
                        nc.vector.tensor_tensor(dst[:, :, 0:HD], S.ps[3][:, 0:D].rearrange("p (h d) -> p h d", h=NH),
                                                bias[:, :].rearrange("p (h d) -> p h d", h=NH), ALU.add).then_inc(S.v_sb, 1)

                    def shifted(S, k):
                        for j in range(BANKS):
                            dve.wait_ge(S.score_ps, BANKS * k + j + 1)
                            sc = S.ps[j][:, :].rearrange("p (h k) -> p h k", h=4)
                            mx = S.rmax[:, 4 * j:4 * j + 4]
                            then(nc.vector.tensor_reduce(mx, sc, AX.X, ALU.max))
                            nc.vector.tensor_tensor(S.probs[:, j, :].rearrange("p (h k) -> p h k", h=4), sc,
                                                    mx.unsqueeze(2).broadcast_to([P, 4, P]), ALU.subtract).then_inc(S.shifted, 1)

                    def averaged(S, k):
                        dve.wait_ge(S.pv_ps, k + 1)
                        pv = S.ps[1][:, :].rearrange("p (h d) -> p h d", h=NH)
                        then(nc.vector.reciprocal(S.rsum[:, :].unsqueeze(2), pv[:, :, HD:HA]))
                        nc.vector.tensor_tensor(S.onat[:, :].rearrange("p (h d) -> p h d", h=NH), pv[:, :, 0:HD],
                                                S.rsum[:, :].unsqueeze(2).broadcast_to([P, NH, HD]), ALU.mult).then_inc(S.o_sb, 1)

                    def a_qkv():
                        dve.wait_ge(w_a0, 64)
                        dve.wait_ge(A.q_ps, 1)
                        for m, (q, keep) in enumerate(((A.qe, even), (A.qo, odd))):
                            for c in range(KC):
                                v = nc.vector.tensor_scalar(q[:, c, :], A.ps[1][:, c * P:(c + 1) * P], keep, bq0_eo[:, m, c:c + 1],
                                                            ALU.mult, ALU.add)
                        v.then_inc(A.q_sb, 1)
                        v_biased(A, 0, A.va, bv0)

                    def a_summed(y_in, need):
                        dve.wait_ge(need, 1)
                        dve.wait_ge(A.xb_sb, 1)
                        then(nc.vector.tensor_tensor(A.y[:, :], y_in, A.xb[:, :], ALU.add))

                    def a_values_averaged():
                        averaged(A, 1)
                        dve.wait_ge(A.o_sb, 2)
                        then(nc.vector.tensor_tensor(A.y[:, :], A.onat[:, :], A.x[:, :], ALU.add))

                    def a_route():
                        t, one = A.sm, A.one
                        dve.wait_ge(A.lg_ps, 1)
                        dve.wait_ge(A.sq_rn, 1)
                        nc.vector.scalar_tensor_tensor(t[:, 0, :], A.ps[1][:, 0:E0], A.rn[:, 0:1], sig[:, :], ALU.mult,
                                                       ALU.subtract).then_inc(A.lg_read, 1)
                        dve.wait_ge(A.lg_read, 1)
                        nc.vector.tensor_scalar(t[:, 1, :], t[:, 0, :], 0.0, None, ALU.max)
                        then(nc.vector.max(A.m8[:, :], t[:, 0, :]))
                        nc.vector.tensor_scalar(one[:, 0:1], A.m8[:, 0:1], 0.0, -1.0, ALU.max, ALU.mult).then_inc(A.gate_in, 1)
                        then(nc.vector.max_index(A.i8[:, :], A.m8[:, :], t[:, 0, :]))
                        nc.vector.tensor_copy(A.i8f[:, :], A.i8[:, :])
                        nc.vector.tensor_scalar(t[:, 4, :], t[:, 0, :], 0.0, None, ALU.is_gt)
                        then(nc.vector.tensor_scalar(one[:, 1:2], A.m8[:, 0:1], 0.0, None, ALU.is_le))
                        then(nc.vector.tensor_scalar(t[:, 3, :], iota, A.i8f[:, 0:1], None, ALU.is_equal))
                        then(nc.vector.scalar_tensor_tensor(t[:, 5, :], iota, A.i8f[:, 1:2], t[:, 3, :], ALU.is_equal, ALU.max))
                        then(nc.vector.scalar_tensor_tensor(t[:, 6, :], t[:, 5, :], one[:, 1:2], t[:, 4, :], ALU.mult, ALU.max))
                        dve.wait_ge(A.gate_exp, 1)
                        then(nc.vector.scalar_tensor_tensor(t[:, 7, :], t[:, 2, :], 1.0, t[:, 6, :], ALU.mult, ALU.mult,
                                                            accum_out=one[:, 2:3]))
                        then(nc.vector.reciprocal(one[:, 3:4], one[:, 2:3]))
                        then(nc.vector.tensor_scalar(t[:, 3, :], t[:, 7, :], one[:, 3:4], None, ALU.mult))

                    def a_expert(e):
                        dve.wait_ge(A.moe_ps, e + 1)
                        src = A.ps[(e + 2) % BANKS][:, 0:3 * H0]
                        we = A.sm[:, 3, e:e + 1]
                        if e == 0:
                            v = nc.vector.tensor_scalar(A.qkv[:, :], src, we, None, ALU.mult)
                        else:
                            dve.wait_ge(A.moe_acc, e)
                            v = nc.vector.scalar_tensor_tensor(A.qkv[:, :], src, we, A.qkv[:, :], ALU.mult, ALU.add)
                        v.then_inc(A.moe_acc, 1)

                    def a_scores():
                        dve.wait_ge(A.s_ps, 1)
                        then(nc.vector.tensor_reduce(A.one[:, 0:1], A.ps[1][:, 0:P], AX.X, ALU.max))
                        nc.vector.tensor_scalar(A.one[:, 1:2], A.one[:, 0:1], -(H0 ** -0.5), None, ALU.mult).then_inc(A.s_bias, 1)

                    def a_weights_normed():
                        dve.wait_ge(A.s_exp, 1)
                        then(nc.vector.reciprocal(A.one[:, 3:4], A.one[:, 2:3]))
                        then(nc.vector.tensor_scalar(A.sm[:, 5, :], A.sm[:, 3, :], A.one[:, 3:4], None, ALU.mult))

                    def a_expert_out(i):
                        dve.wait_ge(A.mo_ps, i + 1)
                        for s in range(2):
                            e = 2 * i + s
                            if e:
                                dve.wait_ge(A.mo_acc, e)
                            nc.vector.scalar_tensor_tensor(A.yout[:, :], A.ps[i % BANKS][:, s * D:(s + 1) * D], A.sm[:, 5, e:e + 1],
                                                           (A.yout if e else A.x)[:, :], ALU.mult, ALU.add).then_inc(A.mo_acc, 1)
                        if i == E0 // 2 - 1:
                            dve.wait_ge(A.mo_acc, E0)

                    def b_summed(k, x_in):
                        dve.wait_ge(B.proj_ps, k + 1)
                        if k == 1:
                            dve.wait_ge(B.xb_sb, 1)
                        then(nc.vector.tensor_tensor((B.y if k else B.y3)[:, :], B.ps[0][:, 0:D], x_in[:, :], ALU.add))

                    def b_q():
                        dve.wait_ge(w_x, 16 * 7)
                        dve.wait_ge(B.q_ps, 2)
                        for c in range(KC):
                            v = nc.vector.tensor_scalar(B.qe[:, c, :], B.ps[1][:, c * P:(c + 1) * P], xbqk[:, c:c + 1], None, ALU.add)
                        v.then_inc(B.q_sb, 1)

                    def b_features():
                        for j in (2, 3):
                            dve.wait_ge(B.feat_ps, j + 1)
                            nc.vector.tensor_scalar(fq[:, j, :], B.ps[j][:, 0:2 * P], 0.0, None, ALU.max)
                            nc.vector.tensor_scalar(fk[:, j, :], B.ps[j][:, 2 * P:4 * P], 0.0, None, ALU.max).then_inc(B.feat_dve, 1)

                    def b_kv():
                        dve.wait_ge(B.kv_ps, 1)
                        nc.vector.tensor_tensor(B.kvb[:, :, :], B.ps[0][:, 0:NH * HA].rearrange("p (m n) -> p m n", m=NH // 2),
                                                block_mask.unsqueeze(1).broadcast_to([P, NH // 2, 2 * HA]), ALU.mult).then_inc(B.kv_sb, 1)

                    def b_num():
                        dve.wait_ge(B.num_ps, 1)
                        pv = B.ps[0][:, 0:NH * HA].rearrange("p (h d) -> p h d", h=NH)
                        then(nc.vector.tensor_scalar(B.rmax[:, :].unsqueeze(2), pv[:, :, HD:HA], 1e-8, None, ALU.add))
                        then(nc.vector.reciprocal(B.rsum[:, :], B.rmax[:, :]))
                        nc.vector.tensor_tensor(B.onat[:, :].rearrange("p (h d) -> p h d", h=NH), pv[:, :, 0:HD],
                                                B.rsum[:, :].unsqueeze(2).broadcast_to([P, NH, HD]), ALU.mult).then_inc(B.o_sb, 1)

                    def f_logits():
                        dve.wait_ge(F.r_ps, 1)
                        then(nc.vector.tensor_reduce(F.one[:, 0:1], F.ps[1][:, 0:E1], AX.X, ALU.max, negate=True))
                        nc.vector.tensor_copy(F.sm[:, 0, 0:E1], F.ps[1][:, 0:E1]).then_inc(F.r_in, 1)

                    def f_route():
                        t = F.sm
                        dve.wait_ge(F.r_exp, 1)
                        then(nc.vector.reciprocal(F.one[:, 2:3], F.one[:, 1:2]))
                        then(nc.vector.tensor_scalar(t[:, 1, 0:E1], t[:, 0, 0:E1], F.one[:, 2:3], None, ALU.mult))
                        then(nc.vector.max(F.m8[:, :], t[:, 1, 0:E1]))
                        then(nc.vector.max_index(F.i8[:, :], F.m8[:, :], t[:, 1, 0:E1]))
                        then(nc.vector.tensor_copy(F.i8f[:, :], F.i8[:, :]))
                        for s in range(2):
                            nc.vector.tensor_scalar(t[:, 2 + s, 0:E1], iota[:, 0:E1], F.i8f[:, s:s + 1], LORA_SCALE, ALU.is_equal, ALU.mult)
                            v = nc.vector.tensor_scalar(t[:, 4 + s, 0:E1], iota[:, 0:E1], F.i8f[:, s:s + 1], F.m8[:, s:s + 1], ALU.is_equal, ALU.mult)
                        then(v)
                        nc.vector.tensor_copy(F.rm[:, 0:2, :].rearrange("p s (e r) -> p s e r", r=R1),
                                              t[:, 2:4, 0:E1].unsqueeze(3).broadcast_to([P, 2, E1, R1]))
                        nc.vector.tensor_scalar(F.rm[:, 2:4, :].rearrange("p s (e r) -> p s e r", r=R1),
                                                t[:, 4:6, 0:E1].unsqueeze(3).broadcast_to([P, 2, E1, R1]), LORA_SCALE, None,
                                                ALU.mult).then_inc(F.rm_sb, 1)

                    def f_ranks_masked():
                        dve.wait_ge(F.rmT_sb, 1)
                        dve.wait_ge(F.xa_ps, 1)
                        for m in range(2):
                            v = nc.vector.tensor_tensor(xam[:, m, :, :], F.ps[2][:, m * P:(m + 1) * P].unsqueeze(1).broadcast_to([P, 2, P]),
                                                        F.rmT[:, 0:2, :], ALU.mult)
                        v.then_inc(F.xam_sb, 1)

                    def f_lora(f):
                        w = ffc(f)
                        dve.wait_ge(F.base_sb, f + 1)
                        dve.wait_ge(F.lora_ps, f + 1)
                        for m, t3 in enumerate((g3(f), u3(f))):
                            v = nc.vector.tensor_tensor(t3[:, 1:3, :], F.ps[2 + f % 2][0:w, m * 2 * P:(m + 1) * 2 * P].rearrange("p (s t) -> p s t", s=2),
                                                        t3[:, 0:1, :].broadcast_to([w, 2, P]), ALU.add)
                        v.then_inc(F.lora_sb, 1)

                    def f_down_ranks():
                        dve.wait_ge(F.ha_ps, 1)
                        nc.vector.tensor_tensor(F.zz[:, :, :], F.ps[1][:, 0:2 * P].rearrange("p (s t) -> p s t", s=2), F.rmT[:, 2:4, :],
                                                ALU.mult).then_inc(F.zz_sb, 1)

                    def f_summed():
                        dve.wait_ge(F.proj_ps, 1)
                        then(nc.vector.tensor_tensor(F.y[:, :], F.ps[0][:, 0:D], F.x[:, :], ALU.add))

                    steps = {
                        "A qkv0": a_qkv,
                        "A sc0": lambda: shifted(A, 0),
                        "A tr0": lambda: averaged(A, 0),
                        "A pj0": lambda: a_summed(A.ps[0][:, 0:D], A.proj_ps),
                        "A n0": lambda: statistics(A, A.y),
                        "A m0": lambda: normed(A, A.x, A.y, 1),
                        "A xT1": lambda: q_split(A, A.ps[0], A.xT_ps, 2),
                        "A sc1": lambda: shifted(A, 1),
                        "A tr1": a_values_averaged,
                        "A n1": lambda: statistics(A, A.y),
                        "A m1": lambda: normed(A, A.x, A.y, 2),
                        "A rt": a_route,
                        "A s": a_scores,
                        "A rs": a_weights_normed,
                        "B n2": lambda: statistics(B, A.yout),
                        "B m2": lambda: normed(B, B.x, A.yout, 1),
                        "B qkv3": lambda: q_split(B, B.ps[1], B.q_ps, 1),
                        "B sc3": lambda: shifted(B, 0),
                        "B tr3": lambda: averaged(B, 0),
                        "B cv": lambda: v_biased(B, 1, B.vx, xbv),
                        "B pj3": lambda: b_summed(0, B.x),
                        "B n3": lambda: statistics(B, B.y3),
                        "B m3": lambda: normed(B, B.x, B.y3, 2),
                        "B q4": b_q,
                        "B ft": b_features,
                        "B kv": b_kv,
                        "B nm": b_num,
                        "B pj4": lambda: b_summed(1, B.xb),
                        "F n4": lambda: statistics(F, B.y),
                        "F m4": lambda: normed(F, F.x, B.y, 1),
                        "F r": f_logits,
                        "F rt": f_route,
                        "F rT": f_ranks_masked,
                        "F z": f_down_ranks,
                        "F pj": f_summed,
                        "F n5": lambda: statistics(F, F.y),
                        "F m5": lambda: normed(F, F.res, F.y, 2),
                    }
                    for step in order:
                        if step in steps:
                            steps[step]()
                        elif step[:3] == "A e":
                            a_expert(int(step[3:]))
                        elif step[:3] == "A w":
                            a_expert_out(int(step[3:]))
                        elif step[:3] == "F l":
                            f_lora(int(step[3:]))

            nc.all_engine_barrier(sems_to_clear=range(min(cleared), max(cleared) + 1))

        body(0, None, "A")
        body(1, None, "AB")
        with nc.Fori(0, LOOP) as it:
            body(2, it, "ABF")
        body(SEQS - 1, None, "ABF")
        body(SEQS, None, "BF")
        body(SEQS + 1, None, "F")


def _laid_out(i):
    import numpy as np

    def rows(v):
        return np.broadcast_to(v, (P, v.shape[-1]))

    a = {k: np.asarray(v) for k, v in i.items()}
    const = np.zeros((P, NCONST), np.float32)
    const[:, C_ID:C_ID + P] = np.eye(P)
    causal = np.tile(np.where(np.arange(P)[None, :] > np.arange(P)[:, None], -1e30, 0.0), (1, 4)).astype(np.float32)
    const[:, C_IOTA:C_IOTA + 16] = np.arange(16)
    const[0:64, C_BLK:C_BLK + HA] = 1.0
    const[64:P, C_BLK + HA:C_BLK + 2 * HA] = 1.0
    const[:, C_PAR] = (np.arange(P) // HD) % 2 == 0
    const[:, C_PAR + 1] = (np.arange(P) // HD) % 2 == 1
    feat = np.zeros((2, P, P), np.float32)
    for w, name in enumerate(("L1_xattn_Wqf", "L1_xattn_Wkf")):
        for j in range(4):
            for s in range(2):
                feat[w, 32 * j + 16 * s:32 * j + 16 * s + 16, 64 * s:64 * s + 64] = a[name].T
    bqkv = a["L0_attn_b_qkv"]
    return {
        "x": a["x"],
        "ctx": a["ctx_2048"],
        "mask": a["mask_BxS2_ff1"].reshape(16, P, 1),
        "const": const,
        "causal": causal,
        "w_qkv0": a["L0_attn_w_qkv"].T,
        "b_qk0": bqkv[0:2 * D].reshape(4, P).T,
        "b_v0": rows(bqkv[2 * D:]),
        "w_o0": a["L0_attn_w_out"].T,
        "b_o0": rows(a["L0_attn_b_out"]),
        "sim": a["L0_ffn_sim_matrix"],
        "gates": rows(a["L0_ffn_gates"]),
        "moe_qkv": np.concatenate([a[f"L0_ffn_{n}_proj"].transpose(1, 0, 2) for n in "qkv"], axis=2),
        "moe_o": a["L0_ffn_o_proj"],
        "w_qk1": np.concatenate([a["L1_attn_Wq"], np.repeat(a["L1_attn_Wk"].reshape(D, 4, HD), 4, axis=1).reshape(D, D)], axis=1),
        "w_v1": a["L1_attn_Wv"],
        "w_o1": a["L1_attn_Wo"],
        "x_qk": np.concatenate([a["L1_xattn_Wq"].T, a["L1_xattn_Wk"].T], axis=1),
        "x_v": a["L1_xattn_Wv"].T,
        "x_o": a["L1_xattn_Wo"].T,
        "x_bqk": np.concatenate([a["L1_xattn_bq"], a["L1_xattn_bk"]]).reshape(4, P).T,
        "x_bv": rows(a["L1_xattn_bv"]),
        "x_bo": rows(a["L1_xattn_bo"]),
        "x_f": feat,
        "f_gu": np.concatenate([a["L1_ffn_Wg"].T, a["L1_ffn_Wu"].T], axis=1),
        "f_d": a["L1_ffn_Wd"].T,
        "f_r": a["L1_ffn_Wr"].T,
        "f_a": np.concatenate([a["L1_ffn_Ag"].reshape(P, D).T, a["L1_ffn_Au"].reshape(P, D).T], axis=1),
        "f_b": np.concatenate([a[f"L1_ffn_B{n}"].transpose(0, 2, 1).reshape(P, DFF) for n in "gu"], axis=1),
        "f_ad": a["L1_ffn_Ad"].reshape(P, DFF).T,
        "f_bd": a["L1_ffn_Bd"].transpose(0, 2, 1).reshape(P, D),
    }


def kernel(**inputs):
    import numpy as _np
    import concourse.bacc as _bacc
    from concourse import mybir as _mybir
    from concourse.bass_utils import run_bass_kernel_spmd as _run

    nc = _bacc.Bacc("TRN2", target_bir_lowering=False, num_devices=1)
    arrays, args = {}, []
    for name, a in _laid_out(inputs).items():
        a = _np.ascontiguousarray(a)
        arrays[f"in_{name}"] = a
        args.append(nc.dram_tensor(f"in_{name}", a.shape, _mybir.dt.from_np(a.dtype), kind="ExternalInput").ap())
    args.append(nc.dram_tensor("out_0", (16, P, D), _mybir.dt.float32, kind="ExternalOutput").ap())
    decoder(nc, *args)
    r = _run(nc, [arrays], core_ids=[0])
    return r.results[0]["out_0"]
```

```python
from contextlib import ExitStack

import concourse.bass as bass
from concourse import mybir

ALU = mybir.AluOpType
ACT = mybir.ActivationFunctionType
AX = mybir.AxisListType
F32 = mybir.dt.float32
BF16 = mybir.dt.bfloat16
U32 = mybir.dt.uint32

P = 128
D = 256
KC = D // P
SEQS = 16
LOOP = SEQS // 2 - 2
NH, HD = 16, 16
HA = HD + 1
HW = 32
E0, H0 = 16, 128
DFF, E1, R1 = 704, 8, 16
FC = -(-DFF // P)
BANKS = 4
BANK = 512
LN_EPS = 1e-5
LORA_SCALE = 2.0
C_ID, C_IOTA, C_BLK, C_PAR = 0, 128, 144, 178
NCONST = 180

ORDER = """
B n2 | F n4 | F m4 | A xT0 | A qkv0 | F xT | A sc0.0 | A sc0.1 | F b.0 | A sc0.2 | A sc0.3 | A pT0.0 | A pT0.1
F r | F rt | A pT0.2 | A pT0.3 | F b.1 | A pv0 | F b.2 | A tr0 | A oT0 | A pj0 | A n0 | F rT | F b.3 | F b.4
A m0 | A vc | A xT1 | A cT | F l.0 | A sc1.0 | A sc1.1 | F b.5 | A sc1.2 | A pT1.0 | A sc1.3 | F l.1 | F l.2
F s.0 | A pT1.1 | F l.3 | F s.1 | F s.2 | A pT1.2 | F l.4 | A pT1.3 | F l.5 | F d.0 | F s.3 | F s.4 | A pv1
F s.5 | F d.1 | A tr1 | F d.2 | A n1 | F d.3 | A m1 | F d.4 | F d.5 | F z | A xT2 | A sq | F zz | F pj | A lg
A rt | F n5 | A e.0 | A e.1 | A e.2 | A e.3 | A e.4 | A e.5 | A e.6 | A e.7 | B m2 | A e.8 | B xT3 | A e.9
B qkv3 | A e.10 | F m5 | B sc3.0 | B sc3.1 | A e.11 | B sc3.2 | B pT3.0 | B sc3.3 | A e.12 | A e.13 | A e.14
B pT3.1 | A e.15 | B pT3.2 | B pT3.3 | A qkT | B pv3 | B cT | A s | B tr3 | B cv | A pT2 | B vm | B oT3 | A ao
A rs | B pj3 | B ck | B n3 | A w.0 | B m3 | A w.1 | A w.2 | B xb | B xT4 | A w.3 | B q4 | A w.4 | A w.5 | B ft.0
B ft.1 | B ft.2 | B ft.3 | A w.6 | A w.7 | B kv | A xT0+ | A qkv0+ | B nm | A sc0.0+ | B oT4 | A sc0.1+
A sc0.2+ | A sc0.3+ | B pj4 | A pT0.0+ | A pT0.1+ | F n4+ | A vc+ | A pT0.2+ | F m4+ | A pT0.3+ | F xT+ | A pv0+
F r+ | A tr0+ | F rt+ | F b.0+ | A cT+ | A oT0+ | F b.1+ | A pj0+ | A n0+ | F rT+ | F b.2+ | A m0+ | F b.3+
A xT1+ | F l.0+ | A sc1.0+ | A sc1.1+ | F b.4+ | A sc1.2+ | A sc1.3+ | F s.0+ | F l.1+ | F l.2+ | A pT1.0+
F s.1+ | A pT1.1+ | F b.5+ | F l.3+ | F s.2+ | F l.4+ | A pT1.2+ | A pT1.3+ | F l.5+ | F d.0+ | F s.3+ | A pv1+
F s.4+ | F d.1+ | F s.5+ | A tr1+ | A n1+ | B n2+ | F d.2+ | F d.3+ | F d.4+ | F d.5+ | A m1+ | A sq+ | A xT2+
F z+ | B m2+ | F zz+ | F pj+ | F n5+ | A lg+ | A rt+ | A e.0+ | B xT3+ | A e.1+ | A e.2+ | A e.3+ | F m5+
A e.4+ | A e.5+ | B qkv3+ | A e.6+ | B sc3.0+ | B sc3.1+ | B sc3.2+ | A e.7+ | A e.8+ | B sc3.3+ | B pT3.0+
A e.9+ | B pT3.1+ | A e.10+ | B pT3.2+ | B pT3.3+ | A e.11+ | B pv3+ | A e.12+ | B tr3+ | A e.13+ | A e.14+
B oT3+ | A e.15+ | B cT+ | B pj3+ | A qkT+ | B n3+ | B ck+ | A s+ | B m3+ | B xb+ | B cv+ | A pT2+ | A rs+
B xT4+ | A ao+ | B vm+ | B q4+ | A w.0+ | B ft.0+ | B ft.1+ | B ft.2+ | A w.1+ | B ft.3+ | A w.2+ | A w.3+
B kv+ | A w.4+ | B nm+ | A w.5+ | A w.6+ | B oT4+ | A w.7+ | B pj4+
""".replace("\n", "|").split("|")
ORDER_FIRST = """
A xT0 | A qkv0 | A sc0.0 | A sc0.1 | A sc0.2 | A sc0.3 | A pT0.0 | A pT0.1 | A pT0.2 | A pT0.3 | A pv0 | A cT
A tr0 | A oT0 | A pj0 | A n0 | A m0 | A xT1 | A sc1.0 | A sc1.1 | A sc1.2 | A pT1.0 | A sc1.3 | A vc | A pT1.1
A pT1.2 | A pT1.3 | A pv1 | A vc+ | A tr1 | A n1 | A m1 | A xT2 | A sq | A lg | A rt | A e.0 | A e.1 | A e.2
A e.3 | A e.4 | A e.5 | A e.6 | A e.7 | A e.8 | A e.9 | A e.10 | A e.11 | A e.12 | A e.13 | A e.14 | A e.15
A qkT | A s | A pT2 | A ao | A rs | A w.0 | A w.1 | A w.2 | A w.3 | A w.4 | A w.5 | A w.6 | A w.7 | A xT0+
A qkv0+ | A sc0.0+ | A sc0.1+ | A sc0.2+ | A sc0.3+ | A pT0.0+ | A pT0.1+ | A pT0.2+ | A pT0.3+ | A pv0+
A tr0+ | A cT+ | B n2+ | A oT0+ | A pj0+ | A n0+ | A m0+ | A xT1+ | B m2+ | A sc1.0+ | A sc1.1+ | A sc1.2+
A sc1.3+ | A pT1.0+ | A pT1.1+ | A pT1.2+ | A pT1.3+ | A pv1+ | B xT3+ | A tr1+ | A n1+ | B qkv3+ | A m1+
A sq+ | A xT2+ | B sc3.0+ | A lg+ | B sc3.1+ | A rt+ | A e.0+ | B sc3.2+ | B pT3.0+ | A e.1+ | B sc3.3+ | A e.2+
A e.3+ | A e.4+ | B pT3.1+ | A e.5+ | A e.6+ | B pT3.2+ | B pT3.3+ | A e.7+ | A e.8+ | B pv3+ | A e.9+ | B tr3+
A e.10+ | B oT3+ | A e.11+ | A e.12+ | A e.13+ | B pj3+ | B cT+ | B n3+ | B m3+ | A e.14+ | A e.15+ | B xT4+
B ck+ | A qkT+ | B q4+ | B cv+ | B vm+ | A s+ | B ft.0+ | A rs+ | A pT2+ | B ft.1+ | B ft.2+ | A ao+ | B ft.3+
A w.0+ | A w.1+ | A w.2+ | B xb+ | A w.3+ | B kv+ | A w.4+ | B nm+ | A w.5+ | A w.6+ | B oT4+ | A w.7+ | B pj4+
""".replace("\n", "|").split("|")
ORDER_LAST = """
F n4 | F m4 | F xT | F r | F rt | F b.0 | F rT | F b.1 | F b.2 | F l.0 | F l.1 | F s.0 | F b.3 | F b.4 | F l.2
F s.1 | F b.5 | F l.3 | F l.4 | F d.0 | F s.2 | F s.3 | F l.5 | F d.1 | F s.4 | F d.2 | F d.3 | F d.4 | B n2
F s.5 | F d.5 | F z | F zz | B m2 | F pj | F n5 | B xT3 | B qkv3 | B sc3.0 | B sc3.1 | B sc3.2 | B sc3.3
B pT3.0 | B pT3.1 | B pT3.2 | B pT3.3 | B pv3 | B tr3 | B oT3 | B pj3 | B n3 | B cT | B m3 | B ck | B xT4 | B cv
B q4 | F m5 | B ft.0 | B xb | B ft.1 | B ft.2 | B ft.3 | B vm | B kv | B nm | B oT4 | B pj4 | F n4+ | F m4+
F xT+ | F r+ | F rt+ | F b.0+ | F b.1+ | F rT+ | F b.2+ | F b.3+ | F l.0+ | F l.1+ | F s.0+ | F b.4+ | F l.2+
F b.5+ | F s.1+ | F l.3+ | F s.2+ | F l.4+ | F d.0+ | F l.5+ | F s.3+ | F s.4+ | F s.5+ | F d.1+ | F d.2+
F d.3+ | F d.4+ | F d.5+ | F z+ | F zz+ | F pj+ | F n5+ | F m5+
""".replace("\n", "|").split("|")


class Stage:

    def __init__(self, name):
        self.name = name
        self.turn = 0


def decoder(nc, x, ctx_in, mask_in, const, causal, w_qkv0, b_qk0, b_v0, w_o0, b_o0, sim, gates, moe_qkv, moe_o,
            w_qk1, w_v1, w_o1, x_qk, x_v, x_o, x_bqk, x_bv, x_bo, x_f, f_gu, f_d, f_r, f_a, f_b, f_ad, f_bd, out):
    with ExitStack() as es:
        def sb(name, shape, dt=F32):
            return es.enter_context(nc.sbuf_tensor(name, shape, dt))

        def sem(name):
            return es.enter_context(nc.semaphore(name))

        cst = sb("cst", [P, NCONST])
        ident = cst[:, C_ID:C_ID + P]
        iota = cst[:, C_IOTA:C_IOTA + 16]
        block_mask = cst[:, C_BLK:C_BLK + 2 * HA]
        even, odd = cst[:, C_PAR:C_PAR + 1], cst[:, C_PAR + 1:C_PAR + 2]
        ident_b = sb("ident_b", [P, P], BF16)
        mask = sb("mask", [P, P])
        mask_b = sb("mask_b", [P, P], BF16)
        ones = sb("ones", [P, P])
        neg_half = sb("neg_half", [P, 1])
        eps = sb("eps", [P, 1])
        wqkv0 = sb("wqkv0", [P, KC, 3 * D])
        bqk0 = sb("bqk0", [P, 4])
        bq0_eo = sb("bq0_eo", [P, 2, KC])
        bv0 = sb("bv0", [P, D])
        wo0 = sb("wo0", [P, KC, D])
        bo0 = sb("bo0", [P, D])
        simn = sb("simn", [P, KC, E0])
        simsq = sb("simsq", [P, KC, E0])
        simr = sb("simr", [P, E0])
        neg_half16 = sb("neg_half16", [P, E0])
        sig = sb("sig", [P, E0])
        wmoe = sb("wmoe", [P, KC, E0, 3 * H0])
        wmo = sb("wmo", [P, E0, D])
        wqk1 = sb("wqk1", [P, KC, 2 * D])
        wv1 = sb("wv1", [P, KC, 64])
        wo1 = sb("wo1", [P, KC, D])
        xqk = sb("xqk", [P, KC, 2 * D])
        xv = sb("xv", [P, KC, D])
        xo = sb("xo", [P, KC, D])
        xbqk = sb("xbqk", [P, 4])
        xbv = sb("xbv", [P, D])
        xbo = sb("xbo", [P, D])
        xf = sb("xf", [P, 2, P])
        wgu = sb("wgu", [P, KC, 2 * DFF])
        wd = sb("wd", [P, FC, D])
        wr = sb("wr", [P, KC, E1])
        wa = sb("wa", [P, KC, 2 * P])
        wb = sb("wb", [P, 2 * DFF])
        wad = sb("wad", [P, FC, P])
        wbd = sb("wbd", [P, D])

        w_c, w_x0, w_a0, w_m, w_mo, w_a1, w_x, w_f = [sem(f"w_{n}") for n in ("const", "x0", "attn0", "moe", "moe_o", "attn1", "xattn1", "ffn")]
        pre_dve, pre_pe, pre_act, pre_pool = [sem(f"pre_{n}") for n in ("dve", "pe", "act", "pool")]
        cleared = []
        events = {}

        def counts(stage, **per_turn):
            new = []
            for n, times in per_turn.items():
                s = sem(f"{stage.name}_{n}")
                cleared.append(s.num)
                events[s.num] = (stage, times if isinstance(times, int) else times["abf".index(stage.name)])
                new.append(s)
            return new

        A, B, F = Stage("a"), Stage("b"), Stage("f")
        A.ps, B.ps = [[es.enter_context(nc.psum_tensor(f"ps_{s}{n}", [P, BANK], F32)) for n in range(BANKS)] for s in "ab"]
        F.ps = B.ps

        for S, s in ((A, "a"), (B, "b"), (F, "f")):
            S.stats, S.mv, S.ve, S.rstd = sb(f"{s}_stats", [P, 6]), sb(f"{s}_mv", [P, 2]), sb(f"{s}_ve", [P, 1]), sb(f"{s}_rstd", [P, 1])
            S.x, S.xT = sb(f"{s}_x", [P, D]), sb(f"{s}_xT", [P, KC, P])
            S.ln_var, S.ln_rstd, S.x_ready, S.xT_ps, S.xT_sb = counts(S, ln_var=2, ln_rstd=2, x_ready=2, xT_ps=(3, 2,
                                                                      1), xT_sb=(2, 2, 1))

        for S, s in ((A, "a"), (F, "f")):
            S.sm, S.one = sb(f"{s}_sm", [P, 8, 16]), sb(f"{s}_one", [P, 4])
            S.m8, S.i8, S.i8f = sb(f"{s}_m8", [P, 8]), sb(f"{s}_i8", [P, 8], U32), sb(f"{s}_i8f", [P, 8])

        for S, s in ((A, "a"), (B, "b")):
            S.xb = sb(f"{s}_xb", [P, D])
            S.cx, S.cxT = sb(f"{s}_cx", [P, D]), sb(f"{s}_cxT", [P, KC, P])
            S.qe = sb(f"{s}_qe", [P, KC, P])
            S.qo = sb(f"{s}_qo", [P, KC, P])
            S.kT = sb(f"{s}_kT", [P, KC, P])
            S.probs = sb(f"{s}_probs", [P, BANKS, BANK])
            S.nmax, S.rsum = sb(f"{s}_nmax", [P, NH]), sb(f"{s}_rsum", [P, NH])
            S.onat, S.oT = sb(f"{s}_onat", [P, D]), sb(f"{s}_oT", [P, KC, P])
            S.ctx_ld, S.xb_sb = counts(S, ctx_ld=16, xb_sb=1)
            S.q_ps, S.k_ps, S.v_ps, S.q_sb, S.k_sb, S.v_sb, S.cT_ps = counts(S, q_ps=(1, 2), k_ps=(1, 2), v_ps=(1, 2),
                                                                             q_sb=2, k_sb=2, v_sb=(1, 2), cT_ps=1)
            S.score_ps, S.masked, S.prob, S.probT_ps, S.probT_sb = counts(S, score_ps=(8, 4), masked=(8, 4), prob=(8,
                                                                           4), probT_ps=(8, 4), probT_sb=(8, 4))
            S.pvT_ps, S.pvT_sb, S.pv_ps, S.o_sb, S.oT_ps, S.oT_sb, S.proj_ps = counts(S, pvT_ps=(2, 1), pvT_sb=(2, 1),
                                                                                      pv_ps=(2, 1), o_sb=2, oT_ps=(1,
                                                                                      2), oT_sb=(1, 2), proj_ps=(1, 2))

        A.xin, A.y, A.yout = sb("a_xin", [P, D]), sb("a_y", [P, D]), sb("a_yout", [P, D])
        A.va, A.vc = sb("a_va", [P, NH, HW]), sb("a_vc", [P, NH, HW])
        A.ss, A.ssc, A.rn = sb("a_ss", [P, 1]), sb("a_ssc", [P, 1]), sb("a_rn", [P, 1])
        A.qkv = sb("a_qkv", [P, 3 * H0])
        A.x_ld, A.vc_sb, A.sq_sum, A.sq_rn, A.lg_ps, A.lg_read = counts(A, x_ld=16, vc_sb=1, sq_sum=1, sq_rn=1,
                                                                        lg_ps=1, lg_read=1)
        A.gate_in, A.gate_exp, A.moe_ps, A.moe_acc, A.qkT_ps, A.qkT_sb = counts(A, gate_in=1, gate_exp=1, moe_ps=16,
                                                                                moe_acc=16, qkT_ps=1, qkT_sb=1)
        A.s_ps, A.s_bias, A.s_exp, A.pT1_ps, A.pT1_sb = counts(A, s_ps=1, s_bias=1, s_exp=1, pT1_ps=1, pT1_sb=1)
        A.ao_ps, A.ao_sb, A.mo_ps, A.mo_acc = counts(A, ao_ps=1, ao_sb=1, mo_ps=8, mo_acc=16)

        B.y3, B.y, B.tokmask = sb("b_y3", [P, D]), sb("b_y", [P, D]), sb("b_tokmask", [P, 1])
        B.va, B.den = sb("b_va", [P, 4, HW]), sb("b_den", [P, NH])
        B.vx, B.vm = sb("b_vx", [P, NH, HA]), sb("b_vm", [P, NH, HA])
        B.kvb = sb("b_kvb", [P, NH // 2, 2 * HA])
        B.cT_sb, B.mask_ld, B.v_masked, B.feat_ps, B.feat_act, B.feat_dve = counts(B, cT_sb=1, mask_ld=16, v_masked=1,
                                                                                   feat_ps=4, feat_act=2, feat_dve=2)
        B.kv_ps, B.kv_sb, B.num_ps = counts(B, kv_ps=1, kv_sb=1, num_ps=1)

        F.y, F.res = sb("f_y", [P, D]), sb("f_res", [P, D])
        F.gu = sb("f_gu", [P, 2 * FC * 3 * P])
        F.rm, F.rmT = sb("f_rm", [P, 4, E1 * R1]), sb("f_rmT", [P, 4, P])
        F.zz = sb("f_zz", [P, 2, P])
        F.r_ps, F.xa_ps, F.r_in, F.r_exp, F.rm_sb, F.rmT_ps, F.rmT_sb = counts(F, r_ps=1, xa_ps=1, r_in=1, r_exp=1,
                                                                               rm_sb=1, rmT_ps=1, rmT_sb=1)
        F.xam_sb, F.base_ps, F.base_sb, F.lora_ps, F.lora_sb = counts(F, xam_sb=1, base_ps=6, base_sb=6, lora_ps=6,
                                                                      lora_sb=6)
        F.silu_sb, F.h_sb, F.ha_ps, F.zz_sb, F.proj_ps, F.stored = counts(F, silu_sb=6, h_sb=6, ha_ps=1, zz_sb=1,
                                                                          proj_ps=1, stored=16)
        dve_done, pool_done = sem("own_dve"), sem("own_pool")
        cleared += [dve_done.num, pool_done.num]
        assert max(cleared) - min(cleared) == len(cleared) - 1

        fq = B.probs[:, 0:2, :].rearrange("p b (j n) -> p (b j) n", j=2)
        fk = B.probs[:, 2:4, :].rearrange("p b (j n) -> p (b j) n", j=2)
        xam = F.rm[:, :, :].rearrange("p (m s) n -> p m s n", m=2)

        def ffc(f):
            return min(P, DFF - f * P)

        def g3(f):
            return F.gu[0:ffc(f), f * 3 * P:(f + 1) * 3 * P].rearrange("p (v t) -> p v t", v=3)

        def u3(f):
            o = (FC + f) * 3 * P
            return F.gu[0:ffc(f), o:o + 3 * P].rearrange("p (v t) -> p v t", v=3)

        def load_late_weights(sp):
            def load(dst, src, s):
                sp.dma_start(dst, src).then_inc(s, 16)

            moe_v = moe_qkv.rearrange("(c p) e n -> p c e n", p=P)
            for c in range(KC):
                load(wmoe[:, c, :, :], moe_v[:, c, :, :], w_m)
            load(wmo[:, :, :], moe_o.rearrange("e h c -> h e c"), w_mo)
            load(wqk1[:, :, :], w_qk1.rearrange("(c p) n -> p c n", p=P), w_a1)
            load(wv1[:, :, :], w_v1.rearrange("(c p) n -> p c n", p=P), w_a1)
            load(wo1[:, :, :], w_o1.rearrange("(c p) n -> p c n", p=P), w_a1)
            load(xqk[:, :, :], x_qk.rearrange("(c p) n -> p c n", p=P), w_x)
            load(xv[:, :, :], x_v.rearrange("(c p) n -> p c n", p=P), w_x)
            load(xo[:, :, :], x_o.rearrange("(c p) n -> p c n", p=P), w_x)
            load(xbqk[:, :], x_bqk, w_x)
            load(xbv[:, :], x_bv, w_x)
            load(xbo[:, :], x_bo, w_x)
            load(xf[:, :, :], x_f.rearrange("w p n -> p w n"), w_x)
            load(wgu[:, :, :], f_gu.rearrange("(c p) n -> p c n", p=P), w_f)
            load(wd[:, 0:FC - 1, :], f_d[0:(FC - 1) * P, :].rearrange("(c p) n -> p c n", p=P), w_f)
            load(wd[0:ffc(FC - 1), FC - 1, :], f_d[(FC - 1) * P:DFF, :], w_f)
            load(wr[:, :, :], f_r.rearrange("(c p) n -> p c n", p=P), w_f)
            load(wa[:, :, :], f_a.rearrange("(c p) n -> p c n", p=P), w_f)
            load(wb[:, :], f_b, w_f)
            load(wad[:, 0:FC - 1, :], f_ad[0:(FC - 1) * P, :].rearrange("(c p) n -> p c n", p=P), w_f)
            load(wad[0:ffc(FC - 1), FC - 1, :], f_ad[(FC - 1) * P:DFF, :], w_f)
            load(wbd[:, :], f_bd, w_f)

        with nc.Block() as pre:
            @pre.sync
            def _(sp):
                def load(dst, src, s):
                    sp.dma_start(dst, src).then_inc(s, 16)

                load(cst[:, :], const, w_c)
                load(mask[:, :], causal, w_c)
                load(simn[:, :, :], sim.rearrange("(c p) e -> p c e", p=P), w_c)
                load(sig[:, :], gates, w_c)
                load(bqk0[:, :], b_qk0, w_c)
                load(A.xin[:, :], x[0:1, :, :].rearrange("a p c -> (a p) c"), w_x0)
                load(wqkv0[:, :, :], w_qkv0.rearrange("(c p) n -> p c n", p=P), w_a0)
                load(bv0[:, :], b_v0, w_a0)
                load(wo0[:, :, :], w_o0.rearrange("(c p) n -> p c n", p=P), w_a0)
                load(bo0[:, :], b_o0, w_a0)
                sp.wait_ge(w_x0, 16)

            @pre.vector
            def _(dve):
                nc.vector.memset(ones[:, :], 1.0).then_inc(pre_dve, 1)
                nc.vector.memset(neg_half[:, :], -0.5)
                nc.vector.memset(neg_half16[:, :], -0.5)
                nc.vector.memset(eps[:, :], LN_EPS)
                for v in (A.va, A.vc, B.va, B.vx):
                    nc.vector.memset(v[:, :, :], 1.0)
                dve.wait_ge(w_c, 16 * 5)
                nc.vector.tensor_copy(ident_b[:, :], ident)
                nc.vector.tensor_copy(mask_b[:, :], mask[:, :])
                nc.vector.tensor_scalar(bq0_eo[:, 0, :], bqk0[:, 0:KC], even, None, ALU.mult)
                nc.vector.tensor_scalar(bq0_eo[:, 1, :], bqk0[:, 0:KC], odd, None, ALU.mult)
                nc.vector.tensor_tensor(simsq[:, :, :], simn[:, :, :], simn[:, :, :], ALU.mult).then_inc(pre_dve, 1)
                dve.wait_ge(pre_act, 1)
                nc.vector.tensor_scalar(sig[:, :], sig[:, :], 1.0, None, ALU.add).then_inc(pre_dve, 1)
                dve.wait_ge(pre_dve, 3)
                nc.vector.reciprocal(sig[:, :], sig[:, :])
                dve.wait_ge(pre_pe, 1)
                nc.vector.tensor_scalar(simr[:, :], A.ps[0][:, 0:E0], 1e-24, None, ALU.max).then_inc(pre_dve, 1)
                dve.wait_ge(pre_pool, 1)
                nc.vector.tensor_tensor(simn[:, :, :], simn[:, :, :],
                                        simr[:, :].unsqueeze(1).broadcast_to([P, KC, E0]), ALU.mult).then_inc(pre_dve, 1)

            @pre.scalar
            def _(act):
                act.wait_ge(w_c, 16 * 5)
                nc.scalar.activation(sig[:, :], sig[:, :], ACT.Exp, scale=-1.0).then_inc(pre_act, 1)

            @pre.tensor
            def _(pe):
                pe.wait_ge(pre_dve, 2)
                for c in range(KC):
                    mm = nc.tensor.matmul(A.ps[0][:, 0:E0], ones[:, :], simsq[:, c, :], start=(c == 0), stop=(c == KC - 1))
                mm.then_inc(pre_pe, 1)

            @pre.gpsimd
            def _(pool):
                pool.wait_ge(pre_dve, 4)
                nc.gpsimd.tensor_tensor(simr[:, :], simr[:, :], neg_half16[:, :], ALU.pow).then_inc(pre_pool, 1)

        def nth(s, n):
            stage, per_turn = events[s.num]
            return stage.turn * per_turn + n

        def seq(t, i, off, it):
            if it is None:
                return t[i + off:i + off + 1, :, :].rearrange("a p c -> (a p) c")
            pairs = t[i + off:i + off + 2 * LOOP, :, :].rearrange("(a two) p c -> a two p c", two=2)
            return pairs[bass.ds(it, 1), 0, :, :].rearrange("a p c -> (a p) c")

        def body(i, it, units, order):
            order = [step.strip() for step in order if step.strip()]
            assert all(step[0] in units[step[-1] == "+"] for step in order)

            def turn_to(unit):
                for stage, name in ((A, "A"), (B, "B"), (F, "F")):
                    stage.turn = 1 if unit and name in units[0] else 0

            with nc.Block(no_gpsimd_drain=True) as block:

                @block.sync
                def _(sp):
                    x_loads = 0
                    for u in (0, 1):
                        turn_to(u)
                        if u == 0 and "A" in units[0]:
                            sp.dma_start(A.cx[:, :], seq(ctx_in, i, 0, it)).then_inc(A.ctx_ld, 16)
                        if "B" in units[u]:
                            if B.turn:
                                sp.wait_ge(B.cT_ps, nth(B.cT_ps, 0))
                                sp.wait_ge(B.v_masked, nth(B.v_masked, 0))
                            sp.dma_start(B.cx[:, :], seq(ctx_in, i, u - 1, it)).then_inc(B.ctx_ld, 16)
                            sp.dma_start(B.tokmask[:, :], seq(mask_in, i, u - 1, it)).then_inc(B.mask_ld, 16)
                        if i == 0 and u == 0:
                            load_late_weights(sp)
                        if "A" in units[u] and i + u < SEQS - 1:
                            sp.wait_ge(A.xT_ps, nth(A.xT_ps, 1))
                            sp.wait_ge(A.xb_sb, nth(A.xb_sb, 1))
                            sp.dma_start(A.xin[:, :], seq(x, i, u + 1, it)).then_inc(A.x_ld, 16)
                            x_loads += 1
                        if u == 0 and "A" in units[1]:
                            sp.wait_ge(A.cT_ps, 1)
                            sp.wait_ge(A.vc_sb, 1)
                            sp.dma_start(A.cx[:, :], seq(ctx_in, i, 1, it)).then_inc(A.ctx_ld, 16)
                        if "F" in units[u]:
                            sp.wait_ge(F.x_ready, nth(F.x_ready, 2))
                            sp.dma_start(seq(out, i, u - 2, it), F.res[:, :]).then_inc(F.stored, 16)
                    if x_loads:
                        sp.wait_ge(A.x_ld, 16 * x_loads)
                    if "F" in units[0] or "F" in units[1]:
                        sp.wait_ge(F.stored, 16 * (("F" in units[0]) + ("F" in units[1])))

                @block.tensor
                def _(pe):
                    def x_transposed(S, src, n, ready=True):
                        if ready:
                            pe.wait_ge(S.x_ready, nth(S.x_ready, n))
                        for c in range(KC):
                            mm = nc.tensor.transpose(S.ps[0][:, c * P:(c + 1) * P], src[:, c * P:(c + 1) * P], ident)
                        mm.then_inc(S.xT_ps, 1)

                    def rows_projected(S, b, w, o, src, done):
                        for m in range(KC):
                            for c in range(KC):
                                mm = nc.tensor.matmul(S.ps[b][:, m * P:(m + 1) * P], w[:, c, o + m * P:o + (m + 1) * P],
                                                      src[:, c, :], start=(c == 0), stop=(c == KC - 1))
                        mm.then_inc(done, 1)

                    def v_projected(S, w, n, src):
                        for c in range(KC):
                            mm = nc.tensor.matmul(S.ps[3][:, 0:n], src[:, c, :], w(c), start=(c == 0), stop=(c == KC - 1))
                        mm.then_inc(S.v_ps, 1)

                    def scores(S, k, kt, j):
                        if j == 0:
                            pe.wait_ge(S.q_sb, nth(S.q_sb, k + 1))
                            pe.wait_ge(S.k_sb, nth(S.k_sb, k + 1))
                            pe.wait_ge(S.v_sb, nth(S.v_sb, 1))
                        for c in range(KC):
                            for par, q in enumerate((S.qe, S.qo)):
                                r = slice(32 * j, 32 * j + 32)
                                o = (2 * c + par) * P
                                mm = nc.tensor.matmul(S.ps[j][:, o:o + P], q[r, c, :], kt[r, c, :],
                                                      start=True, stop=True, tile_position=(32 * j, 0))
                        mm.then_inc(S.score_ps, 1)

                    def probs_transposed(S, k, j):
                        pe.wait_ge(S.prob, nth(S.prob, BANKS * k + j + 1))
                        for h in range(4):
                            mm = nc.tensor.transpose(S.ps[j][:, h * P:(h + 1) * P], S.probs[:, j, h * P:(h + 1) * P], ident)
                        mm.then_inc(S.probT_ps, 1)

                    def values_summed(S, k, v, group):
                        if k == 1:
                            pe.wait_ge(A.vc_sb, nth(A.vc_sb, 1))
                        for j in range(BANKS):
                            pe.wait_ge(S.probT_sb, nth(S.probT_sb, BANKS * k + j + 1))
                            for c in range(KC):
                                for par in range(2):
                                    h = 8 * c + 2 * j + par
                                    o = (2 * c + par) * P
                                    r = 32 * (h % 4)
                                    mm = nc.tensor.matmul(S.ps[0][r:r + 32, h // 4 * P:(h // 4 + 1) * P], v[:, h // group, :],
                                                          S.probs[:, j, o:o + P], start=True, stop=True,
                                                          tile_position=(0, r), skip_group_check=True)
                        mm.then_inc(S.pvT_ps, 1)

                    def sums_transposed(S, k):
                        pe.wait_ge(S.pvT_sb, nth(S.pvT_sb, k + 1))
                        for g in range(4):
                            mm = nc.tensor.transpose(S.ps[1][:, g * P:(g + 1) * P], S.probs[:, 0, g * P:(g + 1) * P], ident)
                        mm.then_inc(S.pv_ps, 1)

                    def ctx_transposed(S, k):
                        pe.wait_ge(S.ctx_ld, nth(S.ctx_ld, 16))
                        pe.wait_ge(S.probT_sb, nth(S.probT_sb, BANKS * (k + 1)))
                        for c in range(KC):
                            mm = nc.tensor.transpose(S.ps[3][:, c * P:(c + 1) * P], S.cx[:, c * P:(c + 1) * P], ident)
                        mm.then_inc(S.cT_ps, 1)

                    def out_transposed(S, k):
                        pe.wait_ge(S.o_sb, nth(S.o_sb, k + 1))
                        for c in range(KC):
                            mm = nc.tensor.transpose(S.ps[1][:, c * P:(c + 1) * P], S.onat[:, c * P:(c + 1) * P], ident)
                        mm.then_inc(S.oT_ps, 1)

                    def out_projected(S, k, w):
                        pe.wait_ge(S.oT_sb, nth(S.oT_sb, k + 1))
                        for c in range(KC):
                            mm = nc.tensor.matmul(S.ps[0][:, 0:D], S.oT[:, c, :], w[:, c, :], start=(c == 0), stop=(c == KC - 1))
                        mm.then_inc(S.proj_ps, 1)

                    def a_x_transposed():
                        if A.turn:
                            pe.wait_ge(A.x_ld, nth(A.x_ld, 0))
                            pe.wait_ge(A.mo_acc, nth(A.mo_acc, 0))
                        x_transposed(A, A.xin, 0, ready=False)

                    def a_qkv():
                        pe.wait_ge(w_a0, 64)
                        pe.wait_ge(A.xT_sb, nth(A.xT_sb, 1))
                        rows_projected(A, 1, wqkv0, 0, A.xT, A.q_ps)
                        rows_projected(A, 2, wqkv0, D, A.xT, A.k_ps)
                        v_projected(A, lambda c: wqkv0[:, c, 2 * D:3 * D], D, A.xT)

                    def a_logits():
                        pe.wait_ge(A.xT_sb, nth(A.xT_sb, 2))
                        for c in range(KC):
                            mm = nc.tensor.matmul(A.ps[1][:, 0:E0], A.xT[:, c, :], simn[:, c, :], start=(c == 0), stop=(c == KC - 1))
                        mm.then_inc(A.lg_ps, 1)

                    def a_expert(e):
                        if e == 0:
                            pe.wait_ge(w_m, 32)
                        if e == 3:
                            pe.wait_ge(A.lg_read, nth(A.lg_read, 1))
                        if e >= BANKS:
                            pe.wait_ge(A.moe_acc, nth(A.moe_acc, e - BANKS + 1))
                        for c in range(KC):
                            mm = nc.tensor.matmul(A.ps[(e + 2) % BANKS][:, 0:3 * H0], A.xT[:, c, :], wmoe[:, c, e, :],
                                                  start=(c == 0), stop=(c == KC - 1))
                        mm.then_inc(A.moe_ps, 1)

                    def a_qk_transposed():
                        pe.wait_ge(A.moe_acc, nth(A.moe_acc, E0))
                        for n in range(2):
                            mm = nc.tensor.transpose(A.ps[0][:, n * P:(n + 1) * P], A.qkv[:, n * P:(n + 1) * P], ident)
                        mm.then_inc(A.qkT_ps, 1)

                    def a_scores():
                        pe.wait_ge(A.qkT_sb, nth(A.qkT_sb, 1))
                        nc.tensor.matmul(A.ps[1][:, 0:P], ident_b[:, :], mask_b[:, 0:P], start=True, stop=False)
                        nc.tensor.matmul(A.ps[1][:, 0:P], A.qe[:, 0, :], A.qe[:, 1, :], start=False, stop=True).then_inc(A.s_ps, 1)

                    def a_prob_transposed():
                        pe.wait_ge(A.s_exp, nth(A.s_exp, 1))
                        nc.tensor.transpose(A.ps[2][:, 0:P], A.qo[:, 0, :], ident).then_inc(A.pT1_ps, 1)

                    def a_values():
                        pe.wait_ge(A.pT1_sb, nth(A.pT1_sb, 1))
                        nc.tensor.matmul(A.ps[3][:, 0:P], A.qkv[:, 2 * P:3 * P], A.qo[:, 1, :], start=True, stop=True).then_inc(A.ao_ps, 1)

                    def a_expert_out(n):
                        if n == 0:
                            pe.wait_ge(w_mo, 16)
                            pe.wait_ge(A.ao_sb, nth(A.ao_sb, 1))
                        if n >= BANKS:
                            pe.wait_ge(A.mo_acc, nth(A.mo_acc, 2 * (n - BANKS + 1)))
                        nc.tensor.matmul(A.ps[n % BANKS][:, :], A.kT[:, 0, :], wmo[:, 2 * n:2 * n + 2, :], start=True,
                                         stop=True).then_inc(A.mo_ps, 1)

                    def b_qkv():
                        pe.wait_ge(w_a1, 48)
                        pe.wait_ge(B.xT_sb, nth(B.xT_sb, 1))
                        rows_projected(B, 1, wqk1, 0, B.xT, B.q_ps)
                        rows_projected(B, 2, wqk1, D, B.xT, B.k_ps)
                        v_projected(B, lambda c: wv1[:, c, :], 64, B.xT)

                    def b_x_transposed():
                        if "F" in units[0]:
                            pe.wait_ge(F.ln_var, nth(F.ln_var, 2))
                        x_transposed(B, B.x, 1)

                    def b_ctx_k():
                        pe.wait_ge(w_x, 16 * 7)
                        pe.wait_ge(B.cT_sb, nth(B.cT_sb, 1))
                        pe.wait_ge(B.probT_sb, nth(B.probT_sb, BANKS))
                        rows_projected(B, 2, xqk, D, B.cxT, B.k_ps)

                    def b_ctx_v():
                        pe.wait_ge(w_x, 16 * 7)
                        pe.wait_ge(B.cT_sb, nth(B.cT_sb, 1))
                        v_projected(B, lambda c: xv[:, c, :], D, B.cxT)

                    def b_q():
                        pe.wait_ge(B.xT_sb, nth(B.xT_sb, 2))
                        rows_projected(B, 1, xqk, 0, B.xT, B.q_ps)

                    def b_features(j):
                        if j == 0:
                            pe.wait_ge(B.q_sb, nth(B.q_sb, 2))
                            pe.wait_ge(B.k_sb, nth(B.k_sb, 2))
                            pe.wait_ge(B.v_sb, nth(B.v_sb, 2))
                        for c in range(KC):
                            r = slice(32 * j, 32 * j + 32)
                            o = c * P
                            nc.tensor.matmul(B.ps[j][:, o:o + P], xf[r, 0, :], B.qe[r, c, :], start=True, stop=True,
                                             tile_position=(32 * j, 0))
                            mm = nc.tensor.matmul(B.ps[j][:, 2 * P + o:2 * P + o + P], B.kT[r, c, :], xf[r, 1, :],
                                                  start=True, stop=True, tile_position=(32 * j, 0))
                        mm.then_inc(B.feat_ps, 1)

                    def b_kv():
                        pe.wait_ge(B.feat_act, nth(B.feat_act, 2))
                        pe.wait_ge(B.feat_dve, nth(B.feat_dve, 2))
                        pe.wait_ge(B.v_masked, nth(B.v_masked, 1))
                        for m in range(NH // 2):
                            c, j = m // BANKS, m % BANKS
                            mm = nc.tensor.matmul(B.ps[0][:, 2 * HA * m:2 * HA * (m + 1)], fk[:, j, c * P:(c + 1) * P],
                                                  B.vm[:, 2 * m:2 * m + 2, :], start=True, stop=True)
                        mm.then_inc(B.kv_ps, 1)

                    def b_num():
                        pe.wait_ge(B.kv_sb, nth(B.kv_sb, 1))
                        for m in range(NH // 2):
                            c, j = m // BANKS, m % BANKS
                            mm = nc.tensor.matmul(B.ps[0][:, 2 * HA * m:2 * HA * (m + 1)], fq[:, j, c * P:(c + 1) * P],
                                                  B.kvb[:, m, :], start=True, stop=True)
                        mm.then_inc(B.num_ps, 1)

                    def f_router():
                        pe.wait_ge(w_f, 16 * 9)
                        pe.wait_ge(F.xT_sb, nth(F.xT_sb, 1))
                        for c in range(KC):
                            mm = nc.tensor.matmul(F.ps[1][:, 0:E1], F.xT[:, c, :], wr[:, c, :], start=(c == 0), stop=(c == KC - 1))
                        mm.then_inc(F.r_ps, 1)
                        for m in range(2):
                            for c in range(KC):
                                mm = nc.tensor.matmul(F.ps[2][:, m * P:(m + 1) * P], wa[:, c, m * P:(m + 1) * P], F.xT[:, c, :],
                                                      start=(c == 0), stop=(c == KC - 1))
                        mm.then_inc(F.xa_ps, 1)

                    def f_ranks_transposed():
                        pe.wait_ge(F.rm_sb, nth(F.rm_sb, 1))
                        for n in range(4):
                            mm = nc.tensor.transpose(F.ps[3][:, n * P:(n + 1) * P], F.rm[:, n, :], ident)
                        mm.then_inc(F.rmT_ps, 1)

                    def f_base(f):
                        if f == 0:
                            pe.wait_ge(w_f, 16 * 9)
                            pe.wait_ge(F.xT_sb, nth(F.xT_sb, 1))
                        if f == 1:
                            pe.wait_ge(F.r_in, nth(F.r_in, 1))
                        if f >= 2:
                            pe.wait_ge(F.base_sb, nth(F.base_sb, f - 1))
                        w = ffc(f)
                        for m in range(2):
                            for c in range(KC):
                                o = m * DFF + f * P
                                mm = nc.tensor.matmul(F.ps[f % 2][0:w, m * P:(m + 1) * P], wgu[:, c, o:o + w],
                                                      F.xT[:, c, :], start=(c == 0), stop=(c == KC - 1))
                        mm.then_inc(F.base_ps, 1)

                    def f_lora(f):
                        if f == 0:
                            pe.wait_ge(F.xam_sb, nth(F.xam_sb, 1))
                        if f == 1:
                            pe.wait_ge(F.rmT_sb, nth(F.rmT_sb, 1))
                        if f >= 2:
                            pe.wait_ge(F.lora_sb, nth(F.lora_sb, f - 1))
                        w = ffc(f)
                        for m in range(2):
                            o = m * DFF + f * P
                            mm = nc.tensor.matmul(F.ps[2 + f % 2][0:w, m * 2 * P:(m + 1) * 2 * P], wb[:, o:o + w],
                                                  xam[:, m, :, :], start=True, stop=True)
                        mm.then_inc(F.lora_ps, 1)

                    def f_down(f):
                        if f == 0:
                            pe.wait_ge(F.base_sb, nth(F.base_sb, FC))
                        pe.wait_ge(F.h_sb, nth(F.h_sb, f + 1))
                        w = ffc(f)
                        mm = nc.tensor.matmul(F.ps[1][:, 0:2 * P], wad[0:w, f, :], g3(f)[:, 1:3, :], start=(f == 0), stop=(f == FC - 1))
                        if f == FC - 1:
                            mm.then_inc(F.ha_ps, 1)
                        nc.tensor.matmul(F.ps[0][:, 0:D], g3(f)[:, 0, :], wd[0:w, f, :], start=(f == 0), stop=False)

                    def f_down_lora():
                        pe.wait_ge(F.zz_sb, nth(F.zz_sb, 1))
                        for s in range(2):
                            mm = nc.tensor.matmul(F.ps[0][:, 0:D], F.zz[:, s, :], wbd[:, :], start=False, stop=(s == 1))
                        mm.then_inc(F.proj_ps, 1)

                    steps = {
                        "A xT0": a_x_transposed,
                        "A qkv0": a_qkv,
                        "A sc0": lambda j: scores(A, 0, A.kT, j),
                        "A pT0": lambda j: probs_transposed(A, 0, j),
                        "A pv0": lambda: values_summed(A, 0, A.va, 1),
                        "A tr0": lambda: sums_transposed(A, 0),
                        "A cT": lambda: ctx_transposed(A, 0),
                        "A oT0": lambda: out_transposed(A, 0),
                        "A pj0": lambda: out_projected(A, 0, wo0),
                        "A xT1": lambda: x_transposed(A, A.x, 1),
                        "A sc1": lambda j: scores(A, 1, A.cxT, j),
                        "A pT1": lambda j: probs_transposed(A, 1, j),
                        "A pv1": lambda: values_summed(A, 1, A.vc, 1),
                        "A tr1": lambda: sums_transposed(A, 1),
                        "A xT2": lambda: x_transposed(A, A.x, 2),
                        "A lg": a_logits,
                        "A qkT": a_qk_transposed,
                        "A s": a_scores,
                        "A pT2": a_prob_transposed,
                        "A ao": a_values,
                        "B xT3": b_x_transposed,
                        "B qkv3": b_qkv,
                        "B sc3": lambda j: scores(B, 0, B.kT, j),
                        "B pT3": lambda j: probs_transposed(B, 0, j),
                        "B pv3": lambda: values_summed(B, 0, B.va, 4),
                        "B tr3": lambda: sums_transposed(B, 0),
                        "B cT": lambda: ctx_transposed(B, 0),
                        "B cv": b_ctx_v,
                        "B ck": b_ctx_k,
                        "B oT3": lambda: out_transposed(B, 0),
                        "B pj3": lambda: out_projected(B, 0, wo1),
                        "B xT4": lambda: x_transposed(B, B.x, 2),
                        "B q4": b_q,
                        "B ft": b_features,
                        "B kv": b_kv,
                        "B nm": b_num,
                        "B oT4": lambda: out_transposed(B, 1),
                        "B pj4": lambda: out_projected(B, 1, xo),
                        "F xT": lambda: x_transposed(F, F.x, 1),
                        "F r": f_router,
                        "F rT": f_ranks_transposed,
                        "F zz": f_down_lora,
                        "A e": a_expert,
                        "A w": a_expert_out,
                        "F b": f_base,
                        "F l": f_lora,
                        "F d": f_down,
                    }
                    for step in order:
                        turn_to(step[-1] == "+")
                        name, _, part = step.rstrip("+").partition(".")
                        if name in steps:
                            steps[name](*([int(part)] if part else []))

                @block.scalar
                def _(act):
                    def copied(dst, src, need, count, done):
                        act.wait_ge(need, nth(need, count))
                        nc.scalar.activation(dst, src, ACT.Copy).then_inc(done, 1)

                    def two(S, b):
                        return S.ps[b][:, 0:D].rearrange("p (c n) -> p c n", c=KC)

                    def k_copied(S, k, bias):
                        act.wait_ge(S.k_ps, nth(S.k_ps, k + 1))
                        for c in range(KC):
                            a = nc.scalar.activation(S.kT[:, c, :], S.ps[2][:, c * P:(c + 1) * P], ACT.Identity, bias=bias[:, 2 + c:3 + c])
                        a.then_inc(S.k_sb, 1)

                    def exps(S, k, j):
                        act.wait_ge(S.masked, nth(S.masked, BANKS * k + j + 1))
                        for h in range(4):
                            p = S.probs[:, j, h * P:(h + 1) * P]
                            a = nc.scalar.activation(p, p, ACT.Exp, bias=S.nmax[:, 4 * j + h:4 * j + h + 1])
                        a.then_inc(S.prob, 1)

                    def probsT(S, k, j):
                        copied(S.probs[:, j, :], S.ps[j][:, :], S.probT_ps, BANKS * k + j + 1, S.probT_sb)

                    def b_qkv():
                        copied(B.kT[:, :, :], two(B, 2), B.k_ps, 1, B.k_sb)
                        copied(B.va[:, :, 0:HD], B.ps[3][:, 0:64].rearrange("p (h d) -> p h d", h=4), B.v_ps, 1, B.v_sb)

                    def b_features(j):
                        if j < 2:
                            act.wait_ge(B.feat_ps, nth(B.feat_ps, j + 1))
                            nc.scalar.activation(fq[:, j, :], B.ps[j][:, 0:2 * P], ACT.Relu)
                            nc.scalar.activation(fk[:, j, :], B.ps[j][:, 2 * P:4 * P], ACT.Relu).then_inc(B.feat_act, 1)

                    def a_squares():
                        act.wait_ge(A.x_ready, nth(A.x_ready, 2))
                        nc.scalar.activation(A.onat[:, :], A.x[:, :], ACT.Square, accum_out=A.ss[:, :]).then_inc(A.sq_sum, 1)

                    def a_gate_exp():
                        act.wait_ge(A.gate_in, nth(A.gate_in, 1))
                        nc.scalar.activation(A.sm[:, 2, :], A.sm[:, 1, :], ACT.Exp, bias=A.one[:, 0:1]).then_inc(A.gate_exp, 1)

                    def a_exp():
                        act.wait_ge(A.s_bias, nth(A.s_bias, 1))
                        nc.scalar.activation(A.qo[:, 0, :], A.ps[1][:, 0:P], ACT.Exp, bias=A.one[:, 1:2], scale=H0 ** -0.5,
                                             accum_out=A.one[:, 2:3]).then_inc(A.s_exp, 1)

                    def f_router_exp():
                        act.wait_ge(F.r_in, nth(F.r_in, 1))
                        nc.scalar.activation(F.sm[:, 0, 0:E1], F.sm[:, 0, 0:E1], ACT.Exp, bias=F.one[:, 0:1],
                                             accum_out=F.one[:, 1:2]).then_inc(F.r_exp, 1)

                    def f_base(f):
                        act.wait_ge(F.base_ps, nth(F.base_ps, f + 1))
                        w = ffc(f)
                        nc.scalar.activation(g3(f)[:, 0, :], F.ps[f % 2][0:w, 0:P], ACT.Copy)
                        nc.scalar.activation(u3(f)[:, 0, :], F.ps[f % 2][0:w, P:2 * P], ACT.Copy).then_inc(F.base_sb, 1)

                    def f_silu(f):
                        act.wait_ge(F.lora_sb, nth(F.lora_sb, f + 1))
                        nc.scalar.activation(g3(f), g3(f), ACT.Silu).then_inc(F.silu_sb, 1)

                    steps = {
                        "A xT0": lambda: copied(A.xT[:, :, :], two(A, 0), A.xT_ps, 1, A.xT_sb),
                        "A qkv0": lambda: k_copied(A, 0, bqk0),
                        "A sc0": lambda j: exps(A, 0, j),
                        "A pT0": lambda j: probsT(A, 0, j),
                        "A pv0": lambda: copied(A.probs[:, 0, :], A.ps[0][:, :], A.pvT_ps, 1, A.pvT_sb),
                        "A cT": lambda: copied(A.cxT[:, :, :], two(A, 3), A.cT_ps, 1, A.k_sb),
                        "A oT0": lambda: copied(A.oT[:, :, :], two(A, 1), A.oT_ps, 1, A.oT_sb),
                        "A sc1": lambda j: exps(A, 1, j),
                        "A pT1": lambda j: probsT(A, 1, j),
                        "A pv1": lambda: copied(A.probs[:, 0, :], A.ps[0][:, :], A.pvT_ps, 2, A.pvT_sb),
                        "A sq": a_squares,
                        "A xT2": lambda: copied(A.xT[:, :, :], two(A, 0), A.xT_ps, 3, A.xT_sb),
                        "A rt": a_gate_exp,
                        "A qkT": lambda: copied(A.qe[:, :, :], two(A, 0), A.qkT_ps, 1, A.qkT_sb),
                        "A s": a_exp,
                        "A pT2": lambda: copied(A.qo[:, 1, :], A.ps[2][:, 0:P], A.pT1_ps, 1, A.pT1_sb),
                        "A ao": lambda: copied(A.kT[:, 0, :], A.ps[3][:, 0:P], A.ao_ps, 1, A.ao_sb),
                        "B xT3": lambda: copied(B.xT[:, :, :], two(B, 0), B.xT_ps, 1, B.xT_sb),
                        "B qkv3": b_qkv,
                        "B sc3": lambda j: exps(B, 0, j),
                        "B pT3": lambda j: probsT(B, 0, j),
                        "B pv3": lambda: copied(B.probs[:, 0, :], B.ps[0][:, :], B.pvT_ps, 1, B.pvT_sb),
                        "B cT": lambda: copied(B.cxT[:, :, :], two(B, 3), B.cT_ps, 1, B.cT_sb),
                        "B ck": lambda: k_copied(B, 1, xbqk),
                        "B oT3": lambda: copied(B.oT[:, :, :], two(B, 1), B.oT_ps, 1, B.oT_sb),
                        "B xT4": lambda: copied(B.xT[:, :, :], two(B, 0), B.xT_ps, 2, B.xT_sb),
                        "B ft": b_features,
                        "B oT4": lambda: copied(B.oT[:, :, :], two(B, 1), B.oT_ps, 2, B.oT_sb),
                        "F xT": lambda: copied(F.xT[:, :, :], two(F, 0), F.xT_ps, 1, F.xT_sb),
                        "F rt": f_router_exp,
                        "F rT": lambda: copied(F.rmT[:, :, :], F.ps[3][:, :].rearrange("p (m n) -> p m n", m=4), F.rmT_ps, 1, F.rmT_sb),
                        "F b": f_base,
                        "F s": f_silu,
                    }
                    for step in order:
                        turn_to(step[-1] == "+")
                        name, _, part = step.rstrip("+").partition(".")
                        if name in steps:
                            steps[name](*([int(part)] if part else []))

                @block.gpsimd
                def _(pool):
                    n = [0]

                    def then(ins):
                        n[0] += 1
                        ins.then_inc(pool_done, 1)
                        pool.wait_ge(pool_done, n[0])

                    def inverse_std(S, count):
                        pool.wait_ge(S.ln_var, nth(S.ln_var, count))
                        then(nc.gpsimd.tensor_tensor(S.ve[:, :], S.mv[:, 1:2], eps[:, :], ALU.add))
                        nc.gpsimd.tensor_tensor(S.rstd[:, :], S.ve[:, :], neg_half[:, :], ALU.pow).then_inc(S.ln_rstd, 1)

                    def a_x_biased():
                        if A.turn:
                            pool.wait_ge(A.x_ld, nth(A.x_ld, 0))
                            pool.wait_ge(A.ln_var, nth(A.ln_var, 0))
                        pool.wait_ge(w_a0, 64)
                        nc.gpsimd.tensor_tensor(A.xb[:, :], A.xin[:, :], bo0[:, :], ALU.add).then_inc(A.xb_sb, 1)

                    def a_values():
                        if A.turn:
                            pool.wait_ge(A.pvT_ps, nth(A.pvT_ps, 0))
                        pool.wait_ge(A.ctx_ld, nth(A.ctx_ld, 16))
                        nc.gpsimd.tensor_copy(A.vc[:, :, 0:HD], A.cx[:, :].rearrange("p (h d) -> p h d", h=NH)).then_inc(A.vc_sb, 1)

                    def a_inverse_norm():
                        pool.wait_ge(A.sq_sum, nth(A.sq_sum, 1))
                        then(nc.gpsimd.tensor_scalar(A.ssc[:, :], A.ss[:, :], 1e-24, None, ALU.max))
                        nc.gpsimd.tensor_tensor(A.rn[:, :], A.ssc[:, :], neg_half[:, :], ALU.pow).then_inc(A.sq_rn, 1)

                    def b_x_biased():
                        pool.wait_ge(w_x, 16 * 7)
                        pool.wait_ge(B.x_ready, nth(B.x_ready, 2))
                        nc.gpsimd.tensor_tensor(B.xb[:, :], B.x[:, :], xbo[:, :], ALU.add).then_inc(B.xb_sb, 1)

                    def b_values_masked():
                        pool.wait_ge(B.mask_ld, nth(B.mask_ld, 16))
                        pool.wait_ge(B.v_sb, nth(B.v_sb, 2))
                        nc.gpsimd.tensor_scalar(B.vm[:, :, :], B.vx[:, :, :], B.tokmask[:, 0:1], None, ALU.mult).then_inc(B.v_masked, 1)

                    def f_gated(f):
                        pool.wait_ge(F.silu_sb, nth(F.silu_sb, f + 1))
                        nc.gpsimd.tensor_tensor(g3(f), g3(f), u3(f), ALU.mult).then_inc(F.h_sb, 1)

                    steps = {
                        "A xT0": a_x_biased,
                        "A vc": a_values,
                        "A n0": lambda: inverse_std(A, 1),
                        "A n1": lambda: inverse_std(A, 2),
                        "A sq": a_inverse_norm,
                        "B n2": lambda: inverse_std(B, 1),
                        "B n3": lambda: inverse_std(B, 2),
                        "B xb": b_x_biased,
                        "B vm": b_values_masked,
                        "F n4": lambda: inverse_std(F, 1),
                        "F n5": lambda: inverse_std(F, 2),
                        "F s": f_gated,
                    }
                    for step in order:
                        turn_to(step[-1] == "+")
                        name, _, part = step.rstrip("+").partition(".")
                        if name in steps:
                            steps[name](*([int(part)] if part else []))

                @block.vector
                def _(dve):
                    n = [0]

                    def then(ins):
                        n[0] += 1
                        ins.then_inc(dve_done, 1)
                        dve.wait_ge(dve_done, n[0])

                    def statistics(S, y):
                        then(nc.vector.bn_stats(S.stats[:, :], y[:, :]))
                        nc.vector.bn_aggr(S.mv[:, :], S.stats[:, :]).then_inc(S.ln_var, 1)

                    def normed(S, x_out, y, count):
                        dve.wait_ge(S.ln_rstd, nth(S.ln_rstd, count))
                        nc.vector.tensor_scalar(x_out[:, :], y[:, :], S.mv[:, 0:1], S.rstd[:, 0:1], ALU.subtract,
                                                ALU.mult).then_inc(S.x_ready, 1)

                    def q_split(S, src, need, count):
                        dve.wait_ge(need, nth(need, count))
                        src = src[:, 0:D].rearrange("p (c n) -> p c n", c=KC)
                        nc.vector.tensor_scalar(S.qe[:, :, :], src, even, None, ALU.mult)
                        nc.vector.tensor_scalar(S.qo[:, :, :], src, odd, None, ALU.mult).then_inc(S.q_sb, 1)

                    def v_biased(S, k, dst, bias):
                        if S is B and B.turn:
                            dve.wait_ge(B.v_masked, nth(B.v_masked, 0))
                        dve.wait_ge(S.v_ps, nth(S.v_ps, k + 1))
                        nc.vector.tensor_tensor(dst[:, :, 0:HD], S.ps[3][:, 0:D].rearrange("p (h d) -> p h d", h=NH),
                                                bias[:, :].rearrange("p (h d) -> p h d", h=NH), ALU.add).then_inc(S.v_sb, 1)

                    def masked(S, k, j):
                        dve.wait_ge(S.score_ps, nth(S.score_ps, BANKS * k + j + 1))
                        sc = S.ps[j][:, :].rearrange("p (h k) -> p h k", h=4)
                        p = S.probs[:, j, :].rearrange("p (h k) -> p h k", h=4)
                        then(nc.vector.tensor_tensor(p, sc, mask[:, :].unsqueeze(1).broadcast_to([P, 4, P]), ALU.add))
                        nc.vector.tensor_reduce(S.nmax[:, 4 * j:4 * j + 4], p, AX.X, ALU.max, negate=True).then_inc(S.masked, 1)

                    def averaged(S, k):
                        dve.wait_ge(S.pv_ps, nth(S.pv_ps, k + 1))
                        pv = S.ps[1][:, :].rearrange("p (h d) -> p h d", h=NH)
                        then(nc.vector.reciprocal(S.rsum[:, :].unsqueeze(2), pv[:, :, HD:HA]))
                        nc.vector.tensor_tensor(S.onat[:, :].rearrange("p (h d) -> p h d", h=NH), pv[:, :, 0:HD],
                                                S.rsum[:, :].unsqueeze(2).broadcast_to([P, NH, HD]), ALU.mult).then_inc(S.o_sb, 1)

                    def a_qkv():
                        dve.wait_ge(w_a0, 64)
                        dve.wait_ge(A.q_ps, nth(A.q_ps, 1))
                        for m, (q, keep) in enumerate(((A.qe, even), (A.qo, odd))):
                            for c in range(KC):
                                v = nc.vector.tensor_scalar(q[:, c, :], A.ps[1][:, c * P:(c + 1) * P], keep, bq0_eo[:, m, c:c + 1],
                                                            ALU.mult, ALU.add)
                        v.then_inc(A.q_sb, 1)
                        v_biased(A, 0, A.va, bv0)

                    def a_summed(y_in, need):
                        dve.wait_ge(need, nth(need, 1))
                        dve.wait_ge(A.xb_sb, nth(A.xb_sb, 1))
                        then(nc.vector.tensor_tensor(A.y[:, :], y_in, A.xb[:, :], ALU.add))

                    def a_values_averaged():
                        averaged(A, 1)
                        dve.wait_ge(A.o_sb, nth(A.o_sb, 2))
                        then(nc.vector.tensor_tensor(A.y[:, :], A.onat[:, :], A.x[:, :], ALU.add))

                    def a_route():
                        t, one = A.sm, A.one
                        dve.wait_ge(A.lg_ps, nth(A.lg_ps, 1))
                        dve.wait_ge(A.sq_rn, nth(A.sq_rn, 1))
                        nc.vector.scalar_tensor_tensor(t[:, 0, :], A.ps[1][:, 0:E0], A.rn[:, 0:1], sig[:, :], ALU.mult,
                                                       ALU.subtract).then_inc(A.lg_read, 1)
                        dve.wait_ge(A.lg_read, nth(A.lg_read, 1))
                        nc.vector.tensor_scalar(t[:, 1, :], t[:, 0, :], 0.0, None, ALU.max)
                        then(nc.vector.max(A.m8[:, :], t[:, 0, :]))
                        nc.vector.tensor_scalar(one[:, 0:1], A.m8[:, 0:1], 0.0, -1.0, ALU.max, ALU.mult).then_inc(A.gate_in, 1)
                        then(nc.vector.max_index(A.i8[:, :], A.m8[:, :], t[:, 0, :]))
                        nc.vector.tensor_copy(A.i8f[:, :], A.i8[:, :])
                        nc.vector.tensor_scalar(t[:, 4, :], t[:, 0, :], 0.0, None, ALU.is_gt)
                        then(nc.vector.tensor_scalar(one[:, 1:2], A.m8[:, 0:1], 0.0, None, ALU.is_le))
                        then(nc.vector.tensor_scalar(t[:, 3, :], iota, A.i8f[:, 0:1], None, ALU.is_equal))
                        then(nc.vector.scalar_tensor_tensor(t[:, 5, :], iota, A.i8f[:, 1:2], t[:, 3, :], ALU.is_equal, ALU.max))
                        then(nc.vector.scalar_tensor_tensor(t[:, 6, :], t[:, 5, :], one[:, 1:2], t[:, 4, :], ALU.mult, ALU.max))
                        dve.wait_ge(A.gate_exp, nth(A.gate_exp, 1))
                        then(nc.vector.scalar_tensor_tensor(t[:, 7, :], t[:, 2, :], 1.0, t[:, 6, :], ALU.mult, ALU.mult,
                                                            accum_out=one[:, 2:3]))
                        then(nc.vector.reciprocal(one[:, 3:4], one[:, 2:3]))
                        then(nc.vector.tensor_scalar(t[:, 3, :], t[:, 7, :], one[:, 3:4], None, ALU.mult))

                    def a_expert(e):
                        dve.wait_ge(A.moe_ps, nth(A.moe_ps, e + 1))
                        src = A.ps[(e + 2) % BANKS][:, 0:3 * H0]
                        we = A.sm[:, 3, e:e + 1]
                        if e == 0:
                            v = nc.vector.tensor_scalar(A.qkv[:, :], src, we, None, ALU.mult)
                        else:
                            dve.wait_ge(A.moe_acc, nth(A.moe_acc, e))
                            v = nc.vector.scalar_tensor_tensor(A.qkv[:, :], src, we, A.qkv[:, :], ALU.mult, ALU.add)
                        v.then_inc(A.moe_acc, 1)

                    def a_scores():
                        dve.wait_ge(A.s_ps, nth(A.s_ps, 1))
                        then(nc.vector.tensor_reduce(A.one[:, 0:1], A.ps[1][:, 0:P], AX.X, ALU.max))
                        nc.vector.tensor_scalar(A.one[:, 1:2], A.one[:, 0:1], -(H0 ** -0.5), None, ALU.mult).then_inc(A.s_bias, 1)

                    def a_weights_normed():
                        dve.wait_ge(A.s_exp, nth(A.s_exp, 1))
                        then(nc.vector.reciprocal(A.one[:, 3:4], A.one[:, 2:3]))
                        then(nc.vector.tensor_scalar(A.sm[:, 5, :], A.sm[:, 3, :], A.one[:, 3:4], None, ALU.mult))

                    def a_expert_out(i):
                        dve.wait_ge(A.mo_ps, nth(A.mo_ps, i + 1))
                        for s in range(2):
                            e = 2 * i + s
                            if e:
                                dve.wait_ge(A.mo_acc, nth(A.mo_acc, e))
                            nc.vector.scalar_tensor_tensor(A.yout[:, :], A.ps[i % BANKS][:, s * D:(s + 1) * D], A.sm[:, 5, e:e + 1],
                                                           (A.yout if e else A.x)[:, :], ALU.mult, ALU.add).then_inc(A.mo_acc, 1)
                        if i == E0 // 2 - 1:
                            dve.wait_ge(A.mo_acc, nth(A.mo_acc, E0))

                    def b_first_norm():
                        if B.turn:
                            dve.wait_ge(B.xT_ps, nth(B.xT_ps, 0))
                            dve.wait_ge(B.xb_sb, nth(B.xb_sb, 0))
                        normed(B, B.x, A.yout, 1)

                    def b_summed(k, x_in):
                        dve.wait_ge(B.proj_ps, nth(B.proj_ps, k + 1))
                        if k == 1:
                            dve.wait_ge(B.xb_sb, nth(B.xb_sb, 1))
                        then(nc.vector.tensor_tensor((B.y if k else B.y3)[:, :], B.ps[0][:, 0:D], x_in[:, :], ALU.add))

                    def b_q():
                        dve.wait_ge(w_x, 16 * 7)
                        dve.wait_ge(B.q_ps, nth(B.q_ps, 2))
                        for c in range(KC):
                            v = nc.vector.tensor_scalar(B.qe[:, c, :], B.ps[1][:, c * P:(c + 1) * P], xbqk[:, c:c + 1], None, ALU.add)
                        v.then_inc(B.q_sb, 1)

                    def b_features(j):
                        if j >= 2:
                            dve.wait_ge(B.feat_ps, nth(B.feat_ps, j + 1))
                            nc.vector.tensor_scalar(fq[:, j, :], B.ps[j][:, 0:2 * P], 0.0, None, ALU.max)
                            nc.vector.tensor_scalar(fk[:, j, :], B.ps[j][:, 2 * P:4 * P], 0.0, None, ALU.max).then_inc(B.feat_dve, 1)

                    def b_kv():
                        dve.wait_ge(B.kv_ps, nth(B.kv_ps, 1))
                        nc.vector.tensor_tensor(B.kvb[:, :, :], B.ps[0][:, 0:NH * HA].rearrange("p (m n) -> p m n", m=NH // 2),
                                                block_mask[:, :].unsqueeze(1).broadcast_to([P, NH // 2, 2 * HA]), ALU.mult).then_inc(B.kv_sb, 1)

                    def b_num():
                        dve.wait_ge(B.num_ps, nth(B.num_ps, 1))
                        pv = B.ps[0][:, 0:NH * HA].rearrange("p (h d) -> p h d", h=NH)
                        then(nc.vector.tensor_scalar(B.den[:, :].unsqueeze(2), pv[:, :, HD:HA], 1e-8, None, ALU.add))
                        then(nc.vector.reciprocal(B.rsum[:, :], B.den[:, :]))
                        nc.vector.tensor_tensor(B.onat[:, :].rearrange("p (h d) -> p h d", h=NH), pv[:, :, 0:HD],
                                                B.rsum[:, :].unsqueeze(2).broadcast_to([P, NH, HD]), ALU.mult).then_inc(B.o_sb, 1)

                    def f_logits():
                        dve.wait_ge(F.r_ps, nth(F.r_ps, 1))
                        then(nc.vector.tensor_reduce(F.one[:, 0:1], F.ps[1][:, 0:E1], AX.X, ALU.max, negate=True))
                        nc.vector.tensor_copy(F.sm[:, 0, 0:E1], F.ps[1][:, 0:E1]).then_inc(F.r_in, 1)

                    def f_route():
                        t = F.sm
                        dve.wait_ge(F.r_exp, nth(F.r_exp, 1))
                        then(nc.vector.reciprocal(F.one[:, 2:3], F.one[:, 1:2]))
                        then(nc.vector.tensor_scalar(t[:, 1, 0:E1], t[:, 0, 0:E1], F.one[:, 2:3], None, ALU.mult))
                        then(nc.vector.max(F.m8[:, :], t[:, 1, 0:E1]))
                        then(nc.vector.max_index(F.i8[:, :], F.m8[:, :], t[:, 1, 0:E1]))
                        then(nc.vector.tensor_copy(F.i8f[:, :], F.i8[:, :]))
                        for s in range(2):
                            nc.vector.tensor_scalar(t[:, 2 + s, 0:E1], iota[:, 0:E1], F.i8f[:, s:s + 1], LORA_SCALE, ALU.is_equal, ALU.mult)
                            v = nc.vector.tensor_scalar(t[:, 4 + s, 0:E1], iota[:, 0:E1], F.i8f[:, s:s + 1], F.m8[:, s:s + 1], ALU.is_equal, ALU.mult)
                        then(v)
                        nc.vector.tensor_copy(F.rm[:, 0:2, :].rearrange("p s (e r) -> p s e r", r=R1),
                                              t[:, 2:4, 0:E1].unsqueeze(3).broadcast_to([P, 2, E1, R1]))
                        nc.vector.tensor_scalar(F.rm[:, 2:4, :].rearrange("p s (e r) -> p s e r", r=R1),
                                                t[:, 4:6, 0:E1].unsqueeze(3).broadcast_to([P, 2, E1, R1]), LORA_SCALE, None,
                                                ALU.mult).then_inc(F.rm_sb, 1)

                    def f_ranks_masked():
                        dve.wait_ge(F.rmT_sb, nth(F.rmT_sb, 1))
                        dve.wait_ge(F.xa_ps, nth(F.xa_ps, 1))
                        for m in range(2):
                            v = nc.vector.tensor_tensor(xam[:, m, :, :], F.ps[2][:, m * P:(m + 1) * P].unsqueeze(1).broadcast_to([P, 2, P]),
                                                        F.rmT[:, 0:2, :], ALU.mult)
                        v.then_inc(F.xam_sb, 1)

                    def f_lora(f):
                        w = ffc(f)
                        dve.wait_ge(F.base_sb, nth(F.base_sb, f + 1))
                        dve.wait_ge(F.lora_ps, nth(F.lora_ps, f + 1))
                        for m, t3 in enumerate((g3(f), u3(f))):
                            v = nc.vector.tensor_tensor(t3[:, 1:3, :], F.ps[2 + f % 2][0:w, m * 2 * P:(m + 1) * 2 * P].rearrange("p (s t) -> p s t", s=2),
                                                        t3[:, 0:1, :].broadcast_to([w, 2, P]), ALU.add)
                        v.then_inc(F.lora_sb, 1)

                    def f_down_ranks():
                        dve.wait_ge(F.ha_ps, nth(F.ha_ps, 1))
                        nc.vector.tensor_tensor(F.zz[:, :, :], F.ps[1][:, 0:2 * P].rearrange("p (s t) -> p s t", s=2), F.rmT[:, 2:4, :],
                                                ALU.mult).then_inc(F.zz_sb, 1)

                    def f_last_norm():
                        if F.turn:
                            dve.wait_ge(F.stored, nth(F.stored, 0))
                        normed(F, F.res, F.y, 2)

                    def f_summed():
                        dve.wait_ge(F.proj_ps, nth(F.proj_ps, 1))
                        then(nc.vector.tensor_tensor(F.y[:, :], F.ps[0][:, 0:D], F.x[:, :], ALU.add))

                    steps = {
                        "A qkv0": a_qkv,
                        "A sc0": lambda j: masked(A, 0, j),
                        "A tr0": lambda: averaged(A, 0),
                        "A pj0": lambda: a_summed(A.ps[0][:, 0:D], A.proj_ps),
                        "A n0": lambda: statistics(A, A.y),
                        "A m0": lambda: normed(A, A.x, A.y, 1),
                        "A xT1": lambda: q_split(A, A.ps[0], A.xT_ps, 2),
                        "A sc1": lambda j: masked(A, 1, j),
                        "A tr1": a_values_averaged,
                        "A n1": lambda: statistics(A, A.y),
                        "A m1": lambda: normed(A, A.x, A.y, 2),
                        "A rt": a_route,
                        "A s": a_scores,
                        "A rs": a_weights_normed,
                        "B n2": lambda: statistics(B, A.yout),
                        "B m2": b_first_norm,
                        "B qkv3": lambda: q_split(B, B.ps[1], B.q_ps, 1),
                        "B sc3": lambda j: masked(B, 0, j),
                        "B tr3": lambda: averaged(B, 0),
                        "B cv": lambda: v_biased(B, 1, B.vx, xbv),
                        "B pj3": lambda: b_summed(0, B.x),
                        "B n3": lambda: statistics(B, B.y3),
                        "B m3": lambda: normed(B, B.x, B.y3, 2),
                        "B q4": b_q,
                        "B ft": b_features,
                        "B kv": b_kv,
                        "B nm": b_num,
                        "B pj4": lambda: b_summed(1, B.xb),
                        "F n4": lambda: statistics(F, B.y),
                        "F m4": lambda: normed(F, F.x, B.y, 1),
                        "F r": f_logits,
                        "F rt": f_route,
                        "F rT": f_ranks_masked,
                        "F z": f_down_ranks,
                        "F pj": f_summed,
                        "F n5": lambda: statistics(F, F.y),
                        "F m5": f_last_norm,
                        "A e": a_expert,
                        "A w": a_expert_out,
                        "F l": f_lora,
                    }
                    for step in order:
                        turn_to(step[-1] == "+")
                        name, _, part = step.rstrip("+").partition(".")
                        if name in steps:
                            steps[name](*([int(part)] if part else []))

            nc.all_engine_barrier(sems_to_clear=range(min(cleared), max(cleared) + 1))

        body(0, None, ("A", "AB"), ORDER_FIRST)
        with nc.Fori(0, LOOP) as it:
            body(2, it, ("ABF", "ABF"), ORDER)
        body(SEQS - 2, None, ("ABF", "ABF"), ORDER)
        body(SEQS, None, ("BF", "F"), ORDER_LAST)


def _laid_out(i):
    import numpy as np

    def rows(v):
        return np.broadcast_to(v, (P, v.shape[-1]))

    a = {k: np.asarray(v) for k, v in i.items()}
    const = np.zeros((P, NCONST), np.float32)
    const[:, C_ID:C_ID + P] = np.eye(P)
    causal = np.where(np.arange(P)[None, :] > np.arange(P)[:, None], -1e30, 0.0).astype(np.float32)
    const[:, C_IOTA:C_IOTA + 16] = np.arange(16)
    const[0:64, C_BLK:C_BLK + HA] = 1.0
    const[64:P, C_BLK + HA:C_BLK + 2 * HA] = 1.0
    const[:, C_PAR] = ((np.arange(P) // HD) % 2 == 0) * HD ** -0.5
    const[:, C_PAR + 1] = ((np.arange(P) // HD) % 2 == 1) * HD ** -0.5
    feat = np.zeros((2, P, P), np.float32)
    for w, name in enumerate(("L1_xattn_Wqf", "L1_xattn_Wkf")):
        for j in range(4):
            for s in range(2):
                feat[w, 32 * j + 16 * s:32 * j + 16 * s + 16, 64 * s:64 * s + 64] = a[name].T
    bqkv = a["L0_attn_b_qkv"]
    return {
        "x": a["x"],
        "ctx": a["ctx_2048"],
        "mask": a["mask_BxS2_ff1"].reshape(16, P, 1),
        "const": const,
        "causal": causal,
        "w_qkv0": a["L0_attn_w_qkv"].T,
        "b_qk0": bqkv[0:2 * D].reshape(4, P).T,
        "b_v0": rows(bqkv[2 * D:]),
        "w_o0": a["L0_attn_w_out"].T,
        "b_o0": rows(a["L0_attn_b_out"]),
        "sim": a["L0_ffn_sim_matrix"],
        "gates": rows(a["L0_ffn_gates"]),
        "moe_qkv": np.concatenate([a[f"L0_ffn_{n}_proj"].transpose(1, 0, 2) for n in "qkv"], axis=2),
        "moe_o": a["L0_ffn_o_proj"],
        "w_qk1": np.concatenate([a["L1_attn_Wq"], np.repeat(a["L1_attn_Wk"].reshape(D, 4, HD), 4, axis=1).reshape(D, D)], axis=1),
        "w_v1": a["L1_attn_Wv"],
        "w_o1": a["L1_attn_Wo"],
        "x_qk": np.concatenate([a["L1_xattn_Wq"].T, a["L1_xattn_Wk"].T], axis=1),
        "x_v": a["L1_xattn_Wv"].T,
        "x_o": a["L1_xattn_Wo"].T,
        "x_bqk": np.concatenate([a["L1_xattn_bq"], a["L1_xattn_bk"]]).reshape(4, P).T,
        "x_bv": rows(a["L1_xattn_bv"]),
        "x_bo": rows(a["L1_xattn_bo"]),
        "x_f": feat,
        "f_gu": np.concatenate([a["L1_ffn_Wg"].T, a["L1_ffn_Wu"].T], axis=1),
        "f_d": a["L1_ffn_Wd"].T,
        "f_r": a["L1_ffn_Wr"].T,
        "f_a": np.concatenate([a["L1_ffn_Ag"].reshape(P, D).T, a["L1_ffn_Au"].reshape(P, D).T], axis=1),
        "f_b": np.concatenate([a[f"L1_ffn_B{n}"].transpose(0, 2, 1).reshape(P, DFF) for n in "gu"], axis=1),
        "f_ad": a["L1_ffn_Ad"].reshape(P, DFF).T,
        "f_bd": a["L1_ffn_Bd"].transpose(0, 2, 1).reshape(P, D),
    }


def kernel(**inputs):
    import numpy as _np
    import concourse.bacc as _bacc
    from concourse import mybir as _mybir
    from concourse.bass_utils import run_bass_kernel_spmd as _run

    nc = _bacc.Bacc("TRN2", target_bir_lowering=False, num_devices=1)
    arrays, args = {}, []
    for name, a in _laid_out(inputs).items():
        a = _np.ascontiguousarray(a)
        arrays[f"in_{name}"] = a
        args.append(nc.dram_tensor(f"in_{name}", a.shape, _mybir.dt.from_np(a.dtype), kind="ExternalInput").ap())
    args.append(nc.dram_tensor("out_0", (16, P, D), _mybir.dt.float32, kind="ExternalOutput").ap())
    decoder(nc, *args)
    r = _run(nc, [arrays], core_ids=[0])
    return r.results[0]["out_0"]
```
